# Optimizing a Trainium2 kernel written in Bass

```python
import numpy as np
import jax
import jax.numpy as jnp

def _softmax(x, axis=-1):
    return jax.nn.softmax(x, axis=axis)

def _gelu(x):
    return jax.nn.gelu(x, approximate=True)

def _silu(x):
    return jax.nn.silu(x)

def _sigmoid(x):
    return jax.nn.sigmoid(x)

def _layernorm(x, axis=-1, eps=1e-05):
    m = jnp.mean(x, axis=axis, keepdims=True)
    v = jnp.var(x, axis=axis, keepdims=True)
    return (x - m) / jnp.sqrt(v + eps)

def _scatter_add(tgt, idx, src, axis=0):
    return tgt.at[idx].add(src)

def _segment_sum(src, seg, n):
    return jax.ops.segment_sum(src, seg, n)
kernel_name = 'mk_cond_seq_d4_seqx_r2_59be19'

def setup_inputs(seed: int=0):
    np.random.seed(seed)
    _w = jnp.asarray

    def _rec_inputs():
        import jax
        import jax.numpy as jnp
        _rk = jax.random.key(seed)
        x = -0.000125 + 0.9999 * jax.random.normal(jax.random.fold_in(_rk, 1), (2, 2048, 512), jnp.float32)
        _lenS = 2048 - jax.random.randint(jax.random.fold_in(_rk, 7), (2,), 0, max(1, 2048 // 4) + 1, jnp.int32)
        _lenS2 = 2048 - jax.random.randint(jax.random.fold_in(_rk, 8), (2,), 0, max(1, 2048 // 4) + 1, jnp.int32)
        condB_safetyscore = -0.927215 + 0.920279 * jax.random.normal(jax.random.fold_in(_rk, 11), (2,), jnp.float32)
        condB_theta = jax.random.uniform(jax.random.fold_in(_rk, 12), (2,), jnp.float32, 0.0, 0.983423)
        condB_phi = jax.random.uniform(jax.random.fold_in(_rk, 13), (2,), jnp.float32, 0.0, 0.961312)
        itok_B_34_63 = jax.random.randint(jax.random.fold_in(_rk, 15), (2,), 34, 64, jnp.int32)
        fside_Bx16xSxS_0 = -1.47943e-05 + 1.00017 * jax.random.normal(jax.random.fold_in(_rk, 16), (2, 16, 2048, 2048), jnp.float32)
        itok_B_0_7 = jax.random.randint(jax.random.fold_in(_rk, 17), (2,), 0, 8, jnp.int32)
        _validS = jnp.arange(2048)[None, :] < _lenS[:, None]
        _validS2 = jnp.arange(2048)[None, :] < _lenS2[:, None]
        _causal = jnp.tril(jnp.ones((2048, 2048), dtype=bool))
        mask_Bx1xSxS_bk0 = jnp.logical_not(jnp.broadcast_to(_validS[:, None, None, :], (2, 1, 2048, 2048)))
        return (x, condB_safetyscore, condB_theta, condB_phi, itok_B_34_63, fside_Bx16xSxS_0, itok_B_0_7, mask_Bx1xSxS_bk0)
    x, condB_safetyscore, condB_theta, condB_phi, itok_B_34_63, fside_Bx16xSxS_0, itok_B_0_7, mask_Bx1xSxS_bk0 = _rec_inputs()

    def _L0_cond_setup():
        import jax, jax.numpy as jnp
        import numpy as np
        TEMPERATURE = 1.0
        ACT_THRESHOLD = 0.1
        MAX_ACT = 1.0
        SAFETY_KNOB = 1.0
        EPS = 1e-08

        def gram_schmidt(X):
            r = X.shape[1]
            Q = X
            for i in range(r):
                q = Q[:, i]
                q = q / (jnp.linalg.norm(q) + EPS)
                Q = Q.at[:, i].set(q)
                coeffs = q @ Q[:, i + 1:]
                Q = Q.at[:, i + 1:].add(-jnp.outer(q, coeffs))
            return Q
        key = jax.random.key(seed)
        ks = jax.random.split(key, 8)
        B, S, D, R = (8, 2048, 512, 32)
        init_std = 0.02
        return {'hidden_states': jax.random.normal(ks[0], (B, S, D), jnp.float32), 'safety_score': jax.random.normal(ks[1], (B,), jnp.float32), 'U': jax.random.normal(ks[2], (D, R), jnp.float32) * init_std, 'V': jax.random.normal(ks[3], (D, R), jnp.float32) * init_std, 'safety_bias': jnp.zeros((D,), jnp.float32), 'gate_w1': jax.random.normal(ks[4], (D // 4, D), jnp.float32) * (1.0 / np.sqrt(D)), 'gate_b1': jnp.zeros((D // 4,), jnp.float32), 'gate_w2': jax.random.normal(ks[5], (1, D // 4), jnp.float32) * (1.0 / np.sqrt(D // 4)), 'gate_b2': jnp.zeros((1,), jnp.float32), 'resp_w': jax.random.normal(ks[6], (D, R), jnp.float32) * (1.0 / np.sqrt(R)), 'resp_b': jnp.zeros((D,), jnp.float32)}
    _L0_cond_all = _L0_cond_setup()
    _L0_cond_in = {k: v for k, v in _L0_cond_all.items() if k in ('U', 'V', 'safety_bias', 'gate_w1', 'gate_b1', 'gate_w2', 'gate_b2', 'resp_w', 'resp_b')}
    del _L0_cond_all

    def _L1_cond_setup():
        import jax, jax.numpy as jnp
        import numpy as np
        key = jax.random.key(seed)
        k1, k2, k3 = jax.random.split(key, 3)
        B, N, D = (16, 2048, 512)
        embeddings = jax.random.normal(k1, (B, N, D), dtype=jnp.float32)
        theta = jax.random.uniform(k2, (B,), dtype=jnp.float32)
        phi = jax.random.uniform(k3, (B,), dtype=jnp.float32)
        return {'embeddings': embeddings, 'theta': theta, 'phi': phi}
    _L1_cond_all = _L1_cond_setup()
    _L1_cond_in = {k: v for k, v in _L1_cond_all.items() if k in ()}
    del _L1_cond_all

    def _L2_cond_setup():
        import jax, jax.numpy as jnp
        import numpy as np
        import math
        D_MODEL = 512
        N_HEAD = 16
        HEAD_DIM = D_MODEL // N_HEAD
        D_FF = 2048
        NUM_STEPS = 100.0
        RESCALE = 4000.0
        EPS = 1e-05

        def _sin_emb(t):
            half = D_MODEL // 2
            x = t.astype(jnp.float32) / NUM_STEPS * RESCALE
            freqs = jnp.exp(jnp.arange(half, dtype=jnp.float32) * (-math.log(10000.0) / (half - 1)))
            e = x[:, None] * freqs[None, :]
            return jnp.concatenate([jnp.sin(e), jnp.cos(e)], axis=-1)

        def _ln(x):
            m = jnp.mean(x, axis=-1, keepdims=True)
            v = jnp.var(x, axis=-1, keepdims=True)
            return (x - m) / jnp.sqrt(v + EPS)

        def _gelu2(x):
            return x * jax.nn.sigmoid(1.702 * x)
        key = jax.random.key(seed)
        ks = jax.random.split(key, 24)
        B, S, D, F = (4, 256, D_MODEL, D_FF)
        std = 0.02
        inp = {'src': jax.random.normal(ks[0], (B, S, D), dtype=jnp.float32), 'src_mask': jax.random.randint(ks[1], (B, 1, S, S), 0, 2).astype(bool), 'timestep': jax.random.randint(ks[2], (B,), 0, 100, dtype=jnp.int32), 'attention_bias': jax.random.normal(ks[3], (B, N_HEAD, S, S), dtype=jnp.float32), 'W_ada': jax.random.normal(ks[4], (D, 2 * D), dtype=jnp.float32) * std, 'b_ada': jnp.zeros((2 * D,), dtype=jnp.float32), 'Wq': jax.random.normal(ks[5], (D, D), dtype=jnp.float32) * std, 'bq': jnp.zeros((D,), dtype=jnp.float32), 'Wk': jax.random.normal(ks[6], (D, D), dtype=jnp.float32) * std, 'bk': jnp.zeros((D,), dtype=jnp.float32), 'Wv': jax.random.normal(ks[7], (D, D), dtype=jnp.float32) * std, 'bv': jnp.zeros((D,), dtype=jnp.float32), 'Wo': jax.random.normal(ks[8], (D, D), dtype=jnp.float32) * std, 'bo': jnp.zeros((D,), dtype=jnp.float32), 'W1': jax.random.normal(ks[9], (D, F), dtype=jnp.float32) * std, 'b1': jnp.zeros((F,), dtype=jnp.float32), 'W2': jax.random.normal(ks[10], (F, D), dtype=jnp.float32) * std, 'b2': jnp.zeros((D,), dtype=jnp.float32), 'g2': jnp.ones((D,), dtype=jnp.float32), 'beta2': jnp.zeros((D,), dtype=jnp.float32)}
        return inp
    _L2_cond_all = _L2_cond_setup()
    _L2_cond_in = {k: v for k, v in _L2_cond_all.items() if k in ('W_ada', 'b_ada', 'Wq', 'bq', 'Wk', 'bk', 'Wv', 'bv', 'Wo', 'bo', 'W1', 'b1', 'W2', 'b2', 'g2', 'beta2')}
    del _L2_cond_all

    def _L3_cond_setup():
        import jax, jax.numpy as jnp
        import numpy as np
        E, H, I = (8, 512, 2048)
        B, S = (4, 512)
        LN_EPS = 1e-12
        key = jax.random.key(seed)
        ks = jax.random.split(key, 8)
        x = jax.random.normal(ks[0], (B, S, H), dtype=jnp.float32)
        expert_idx = jax.random.randint(ks[1], (B,), 0, E, dtype=jnp.int64)
        Wi = jax.random.normal(ks[2], (E, H, I), dtype=jnp.float32) * 0.02
        bi = jnp.zeros((E, I), dtype=jnp.float32)
        Wo = jax.random.normal(ks[3], (E, I, H), dtype=jnp.float32) * 0.02
        bo = jnp.zeros((E, H), dtype=jnp.float32)
        gamma = jnp.ones((E, H), dtype=jnp.float32)
        beta = jnp.zeros((E, H), dtype=jnp.float32)
        return {'input_tensor': x, 'expert_idx': expert_idx, 'Wi': Wi, 'bi': bi, 'Wo': Wo, 'bo': bo, 'gamma': gamma, 'beta': beta}
    _L3_cond_all = _L3_cond_setup()
    _L3_cond_in = {k: v for k, v in _L3_cond_all.items() if k in ('Wi', 'bi', 'Wo', 'bo', 'gamma', 'beta')}
    del _L3_cond_all
    return {'x': x, 'condB_safetyscore': condB_safetyscore, 'condB_theta': condB_theta, 'condB_phi': condB_phi, 'itok_B_34_63': itok_B_34_63, 'fside_Bx16xSxS_0': fside_Bx16xSxS_0, 'itok_B_0_7': itok_B_0_7, 'mask_Bx1xSxS_bk0': mask_Bx1xSxS_bk0, 'L0_cond_U': _L0_cond_in['U'], 'L0_cond_V': _L0_cond_in['V'], 'L0_cond_safety_bias': _L0_cond_in['safety_bias'], 'L0_cond_gate_w1': _L0_cond_in['gate_w1'], 'L0_cond_gate_b1': _L0_cond_in['gate_b1'], 'L0_cond_gate_w2': _L0_cond_in['gate_w2'], 'L0_cond_gate_b2': _L0_cond_in['gate_b2'], 'L0_cond_resp_w': _L0_cond_in['resp_w'], 'L0_cond_resp_b': _L0_cond_in['resp_b'], 'L2_cond_W_ada': _L2_cond_in['W_ada'], 'L2_cond_b_ada': _L2_cond_in['b_ada'], 'L2_cond_Wq': _L2_cond_in['Wq'], 'L2_cond_bq': _L2_cond_in['bq'], 'L2_cond_Wk': _L2_cond_in['Wk'], 'L2_cond_bk': _L2_cond_in['bk'], 'L2_cond_Wv': _L2_cond_in['Wv'], 'L2_cond_bv': _L2_cond_in['bv'], 'L2_cond_Wo': _L2_cond_in['Wo'], 'L2_cond_bo': _L2_cond_in['bo'], 'L2_cond_W1': _L2_cond_in['W1'], 'L2_cond_b1': _L2_cond_in['b1'], 'L2_cond_W2': _L2_cond_in['W2'], 'L2_cond_b2': _L2_cond_in['b2'], 'L2_cond_g2': _L2_cond_in['g2'], 'L2_cond_beta2': _L2_cond_in['beta2'], 'L3_cond_Wi': _L3_cond_in['Wi'], 'L3_cond_bi': _L3_cond_in['bi'], 'L3_cond_Wo': _L3_cond_in['Wo'], 'L3_cond_bo': _L3_cond_in['bo'], 'L3_cond_gamma': _L3_cond_in['gamma'], 'L3_cond_beta': _L3_cond_in['beta']}

def reference(x, condB_safetyscore, condB_theta, condB_phi, itok_B_34_63, fside_Bx16xSxS_0, itok_B_0_7, mask_Bx1xSxS_bk0, L0_cond_U, L0_cond_V, L0_cond_safety_bias, L0_cond_gate_w1, L0_cond_gate_b1, L0_cond_gate_w2, L0_cond_gate_b2, L0_cond_resp_w, L0_cond_resp_b, L2_cond_W_ada, L2_cond_b_ada, L2_cond_Wq, L2_cond_bq, L2_cond_Wk, L2_cond_bk, L2_cond_Wv, L2_cond_bv, L2_cond_Wo, L2_cond_bo, L2_cond_W1, L2_cond_b1, L2_cond_W2, L2_cond_b2, L2_cond_g2, L2_cond_beta2, L3_cond_Wi, L3_cond_bi, L3_cond_Wo, L3_cond_bo, L3_cond_gamma, L3_cond_beta):
    import jax
    import jax.numpy as jnp

    def _L0_cond_ref(hidden_states, safety_score, U, V, safety_bias, gate_w1, gate_b1, gate_w2, gate_b2, resp_w, resp_b):
        import jax, jax.numpy as jnp
        import numpy as np
        TEMPERATURE = 1.0
        ACT_THRESHOLD = 0.1
        MAX_ACT = 1.0
        SAFETY_KNOB = 1.0
        EPS = 1e-08

        def gram_schmidt(X):
            r = X.shape[1]
            Q = X
            for i in range(r):
                q = Q[:, i]
                q = q / (jnp.linalg.norm(q) + EPS)
                Q = Q.at[:, i].set(q)
                coeffs = q @ Q[:, i + 1:]
                Q = Q.at[:, i + 1:].add(-jnp.outer(q, coeffs))
            return Q
        R = resp_w.shape[1]
        U_o = gram_schmidt(U)
        V_o = gram_schmidt(V)
        basis = U_o @ V_o.T
        pooled = hidden_states.mean(axis=1)
        h1 = jax.nn.relu(pooled @ gate_w1.T + gate_b1)
        base_act = jax.nn.sigmoid(h1 @ gate_w2.T + gate_b2)
        mod = jax.nn.sigmoid(safety_score[:, None] / TEMPERATURE)
        knob = jnp.clip(jnp.asarray(SAFETY_KNOB, hidden_states.dtype), ACT_THRESHOLD, MAX_ACT)
        strength = (base_act * mod * knob)[:, None, :]
        proj = hidden_states @ basis
        feats = proj @ basis.T[:, :R]
        response = feats @ resp_w.T + resp_b + safety_bias
        return hidden_states + strength * response

    def _L1_cond_ref(embeddings, theta, phi):
        import jax, jax.numpy as jnp
        import numpy as np
        B, N, D = embeddings.shape
        e = embeddings.reshape(B, N, D // 4, 4)
        ct = jnp.cos(theta)[:, None, None]
        st = jnp.sin(theta)[:, None, None]
        cp = jnp.cos(phi)[:, None, None]
        sp = jnp.sin(phi)[:, None, None]
        x0, x1, x2, x3 = (e[..., 0], e[..., 1], e[..., 2], e[..., 3])
        out = jnp.stack([x0 * ct + x1 * st, -x0 * st + x1 * ct, x2 * cp + x3 * sp, -x2 * sp + x3 * cp], axis=-1)
        return out.reshape(B, N, D)

    def _L2_cond_ref(src, src_mask, timestep, attention_bias, W_ada, b_ada, Wq, bq, Wk, bk, Wv, bv, Wo, bo, W1, b1, W2, b2, g2, beta2):
        import jax, jax.numpy as jnp
        import numpy as np
        import math
        D_MODEL = 512
        N_HEAD = 16
        HEAD_DIM = D_MODEL // N_HEAD
        D_FF = 2048
        NUM_STEPS = 100.0
        RESCALE = 4000.0
        EPS = 1e-05

        def _sin_emb(t):
            half = D_MODEL // 2
            x = t.astype(jnp.float32) / NUM_STEPS * RESCALE
            freqs = jnp.exp(jnp.arange(half, dtype=jnp.float32) * (-math.log(10000.0) / (half - 1)))
            e = x[:, None] * freqs[None, :]
            return jnp.concatenate([jnp.sin(e), jnp.cos(e)], axis=-1)

        def _ln(x):
            m = jnp.mean(x, axis=-1, keepdims=True)
            v = jnp.var(x, axis=-1, keepdims=True)
            return (x - m) / jnp.sqrt(v + EPS)

        def _gelu2(x):
            return x * jax.nn.sigmoid(1.702 * x)
        B, S, D = src.shape
        emb = jax.nn.silu(_sin_emb(timestep)) @ W_ada + b_ada
        scale, shift = jnp.split(emb[:, None, :], 2, axis=-1)
        x = _ln(src) * (1.0 + scale) + shift
        q = (x @ Wq + bq).reshape(B, S, N_HEAD, HEAD_DIM).transpose(0, 2, 1, 3)
        k = (x @ Wk + bk).reshape(B, S, N_HEAD, HEAD_DIM).transpose(0, 2, 1, 3)
        v = (x @ Wv + bv).reshape(B, S, N_HEAD, HEAD_DIM).transpose(0, 2, 1, 3)
        scores = jnp.einsum('bhqd,bhkd->bhqk', q / math.sqrt(HEAD_DIM), k)
        scores = scores + attention_bias
        scores = jnp.where(src_mask, -jnp.inf, scores.astype(jnp.float32))
        probs = jax.nn.softmax(scores, axis=-1).astype(v.dtype)
        ctx = jnp.einsum('bhqk,bhkd->bhqd', probs, v)
        ctx = ctx.transpose(0, 2, 1, 3).reshape(B, S, D)
        x = x + (ctx @ Wo + bo)
        h = _ln(x) * g2 + beta2
        ff = _gelu2(h @ W1 + b1) @ W2 + b2
        return x + ff

    def _L3_cond_ref(input_tensor, expert_idx, Wi, bi, Wo, bo, gamma, beta):
        import jax, jax.numpy as jnp
        import numpy as np
        E, H, I = (8, 512, 2048)
        B, S = (4, 512)
        LN_EPS = 1e-12
        Wi_b = Wi[expert_idx]
        bi_b = bi[expert_idx]
        Wo_b = Wo[expert_idx]
        bo_b = bo[expert_idx]
        g_b = gamma[expert_idx]
        be_b = beta[expert_idx]
        h = jax.nn.gelu(jnp.einsum('bsh,bhi->bsi', input_tensor, Wi_b) + bi_b[:, None, :], approximate=False)
        o = jnp.einsum('bsi,bih->bsh', h, Wo_b) + bo_b[:, None, :]
        r = o + input_tensor
        mu = jnp.mean(r, axis=-1, keepdims=True)
        var = jnp.mean(jnp.square(r - mu), axis=-1, keepdims=True)
        y = (r - mu) * jax.lax.rsqrt(var + LN_EPS)
        return y * g_b[:, None, :] + be_b[:, None, :]
    x = _L0_cond_ref(x, condB_safetyscore, L0_cond_U, L0_cond_V, L0_cond_safety_bias, L0_cond_gate_w1, L0_cond_gate_b1, L0_cond_gate_w2, L0_cond_gate_b2, L0_cond_resp_w, L0_cond_resp_b)
    x = _L1_cond_ref(x, condB_theta, condB_phi)
    x = _L2_cond_ref(x, mask_Bx1xSxS_bk0, itok_B_34_63, fside_Bx16xSxS_0, L2_cond_W_ada, L2_cond_b_ada, L2_cond_Wq, L2_cond_bq, L2_cond_Wk, L2_cond_bk, L2_cond_Wv, L2_cond_bv, L2_cond_Wo, L2_cond_bo, L2_cond_W1, L2_cond_b1, L2_cond_W2, L2_cond_b2, L2_cond_g2, L2_cond_beta2)
    x = _L3_cond_ref(x, itok_B_0_7, L3_cond_Wi, L3_cond_bi, L3_cond_Wo, L3_cond_bo, L3_cond_gamma, L3_cond_beta)
    return x

_drawn_inputs = setup_inputs


def setup_inputs(seed=0):
    import zlib

    import numpy as np

    out = dict(_drawn_inputs(seed))
    spreads = {'L0_cond_safety_bias': (0.0, 2.0),
     'L0_cond_gate_b1': (0.0, 2.0),
     'L0_cond_resp_b': (0.0, 2.0),
     'L2_cond_b_ada': (0.0, 0.1),
     'L2_cond_bq': (0.0, 0.8),
     'L2_cond_bk': (0.0, 2.0),
     'L2_cond_bv': (0.0, 0.1),
     'L2_cond_bo': (0.0, 0.1),
     'L2_cond_b1': (0.0, 0.1),
     'L2_cond_b2': (0.0, 0.1),
     'L2_cond_g2': (1.0, 0.2),
     'L2_cond_beta2': (0.0, 0.362),
     'L3_cond_bi': (0.0, 0.1),
     'L3_cond_bo': (0.0, 0.1),
     'L3_cond_gamma': (1.0, 0.2),
     'L3_cond_beta': (0.0, 0.1)}
    factors = {'condB_safetyscore': 64.0,
     'fside_Bx16xSxS_0': 8.0,
     'L0_cond_V': 64.0,
     'L0_cond_gate_w1': 64.0,
     'L0_cond_gate_w2': 64.0,
     'L2_cond_Wq': 8.0,
     'L2_cond_Wk': 8.0,
     'L0_cond_U': 8.0,
     'L0_cond_resp_w': 8.0}
    for name, (base, spread) in spreads.items():
        noise = np.random.default_rng([zlib.crc32(name.encode()), seed]).standard_normal(out[name].shape)
        drawn = base * np.exp(spread * noise) if base else spread * noise
        out[name] = jnp.asarray(drawn.astype(out[name].dtype))
    for name, factor in factors.items():
        out[name] = (out[name] * factor).astype(out[name].dtype)
    return out
```

```python
from contextlib import ExitStack

import concourse.bass as bass
from concourse import mybir

F32 = mybir.dt.float32
F32R = mybir.dt.float32r
BF16 = mybir.dt.bfloat16
U16 = mybir.dt.uint16
U8 = mybir.dt.uint8
I32 = mybir.dt.int32
ACT = mybir.ActivationFunctionType
ALU = mybir.AluOpType
AX = mybir.AxisListType.X
ds = bass.ds

P = 128
B, S, D = 2, 2048, 512
H, DH = 16, 32
R = 32
FF = 2048
E = 8
TOK = B * S
C = D // P
GT = 4
GTOK = GT * P
NG = TOK // GTOK
GB = NG // B
FC = FF // P
QUARTERS = 4
QF = FF // QUARTERS
HG = 4
NHG = H // HG
QB = 256
NQ = S // QB
STEPS = B * NHG * NQ
KT = S // P
PI = 3.141592653589793
TWO_PI_A, TWO_PI_B, TWO_PI_C = 6.28125, 0.0019350051879882812, 3.019916050561733e-07
ROUND = 12582912.0
MASKED = -1.0e30
LOWEST = -3.0e38


class Link:

    def __init__(self, eng, sem, base=0, per=None, at=None):
        self.eng, self.sem, self.n = eng, sem, 0
        self.start = base if at is None else at * per + base

    def __call__(self, ins):
        self.n += 1
        ins.then_inc(self.sem, 1)
        self.eng.wait_ge(self.sem, self.start + self.n)


def planes(ap):
    return ap.bitcast(BF16).rearrange("p (n two) -> p n two", two=2)


class Core:

    def __init__(self, nc):
        self.nc, self.sems = nc, []

    def sem(self, name):
        self.sems.append(self.nc.alloc_semaphore(name=name))
        return self.sems[-1]

    def pass_done(self):
        self.nc.clear_and_free_semaphores(self.sems)
        self.nc.all_engine_barrier()
        self.sems = []

    def sb(self, ctx, name, shape, dt=F32):
        return ctx.enter_context(self.nc.sbuf_tensor(name, shape, dt))

    def ps(self, ctx, name, shape, dt=F32):
        return ctx.enter_context(self.nc.psum_tensor(name, shape, dt))

    def dram(self, name, shape, dt=F32):
        return self.nc.dram_tensor(name, shape, dt, kind="Internal").ap()


def constants(k, i, keep):
    nc = k.nc
    with ExitStack() as ctx:
        sb = lambda *a: k.sb(ctx, *a)
        basis = [keep.basis, sb("basis_odd", [P, C, 2, R])]
        norm2_mask = sb("step_mask", [P, 64])
        resp_w = sb("resp_w", [P, C, R])
        resp_row = sb("resp_row", [33, 512])
        safety_row = sb("safety_row", [33, 512])
        mean_w = sb("mean_w", [P, P])
        ones = sb("ones", [P, P])
        gate_w1 = sb("gate_w1", [P, D])
        gate_b1 = sb("gate_b1", [P, 1])
        gate_w2 = sb("gate_w2", [P, 1])
        gate_b2 = sb("gate_b2", [P, 1])
        score = sb("score", [P, B])
        step_i = sb("step_i", [P, B], I32)
        step_f = sb("step_f", [P, B])
        freq = sb("freq", [P, 2])
        w_ada = sb("w_ada", [P, C, 2 * D])
        b_ada_t = sb("b_ada_t", [P, 2 * C])
        b_ada_bc = sb("b_ada_bc", [P, 2 * D])
        x_in = sb("x_mean", [P, 2, GT, D])
        angle = sb("angle", [P, 16])
        turns = sb("turns", [P, 16])
        shift_t = sb("shift_t", [P, 16])
        shift_a = sb("shift_a", [P, 16])
        sincos = sb("sincos", [P, 16])
        sig = sb("sig", [P, 2 * C])
        z = sb("z", [P, C, B])
        rot_c = sb("rot_c", [P, B, 2, 4])
        nrm = sb("nrm", [P, 2, 2])
        rr = sb("rr", [P, 2])
        r2 = sb("r2", [P, 2])
        coef = sb("coef", [P, 2, R - 1])
        coef2 = sb("coef2", [P, 2, R - 1])
        outer_p = sb("outer_p", [P, C, 2, R - 1])
        vtv = sb("vtv", [R, R])
        resp_t = sb("resp_t", [R, D])
        a1 = sb("a1", [R, D])
        g33 = sb("g33", [R + 1, D])
        g33s = sb("g33s", [R + 1, D])
        gtmp = sb("gtmp", [R + 1, D])
        eye_s = sb("eye_s", [P, P])
        eye_c = sb("eye_c", [P, P])
        prod = sb("prod", [P, D])
        h1 = sb("h1", [P, B])
        h1r = sb("h1r", [P, B])
        base_act = sb("base_act", [P, B])
        mod = sb("mod", [P, B])
        strength = sb("strength", [P, B])
        wraw = sb("wraw", [P, C, D])
        pool_mean = [k.ps(ctx, f"mean_ps{b}", [P, D]) for b in range(B)]
        coef_ps = [k.ps(ctx, f"coef_ps{n}", [P, 2, R]) for n in range(2)]
        small_ps = k.ps(ctx, "small_ps", [P, 512])
        ada_ps = k.ps(ctx, "ada_ps", [P, 2 * C, B])
        row_ps = [k.ps(ctx, f"row_ps{n}", [P, 512]) for n in range(2)]

        small_loaded, x_loaded = k.sem("small_loaded"), [k.sem(f"x_loaded{n}") for n in range(2)]
        eye_ready, eye_wiped = k.sem("eye_ready"), k.sem("eye_wiped")
        consts_set, mean_tiles = k.sem("consts_set"), k.sem("mean_tiles")
        basis_ready, coef_ready, nrm_ready = k.sem("basis_ready"), k.sem("coef_ready"), k.sem("nrm_ready")
        own = k.sem("dve_chain")
        angles_ready, sincos_ready, z_ready = (k.sem(n) for n in ("angles_ready", "sincos_ready", "z_ready"))
        h1_ready, gate_ps_ready, gate_ready = k.sem("h1_ready"), k.sem("gate_ps_ready"), k.sem("gate_ready")
        ada_ps_ready, row_ready, row_taken = k.sem("ada_ps_ready"), k.sem("row_ready"), k.sem("row_taken")
        vtv_ready, vtv_taken, respt_ready, respt_taken = (k.sem(n) for n in ("vtv_ready", "vtv_taken", "respt_ready", "respt_taken"))
        a1_ready, a1_taken, g_ready = k.sem("a1_ready"), k.sem("a1_taken"), k.sem("g_ready")
        w_loaded, w_split, w_low = k.sem("w_loaded"), k.sem("w_split"), k.sem("w_low")

        x_g = i.x.rearrange("b (g t p) d -> (b g) p t d", t=GT, p=P)
        row = lambda ap: ap.rearrange("(a n) -> a n", a=1)
        bc = lambda ap, n: row(ap).to_broadcast([P, n])
        loads = [
            (basis[0][:, :, 0, :], i.U.rearrange("(c p) r -> p c r", p=P)),
            (basis[0][:, :, 1, :], i.V.rearrange("(c p) r -> p c r", p=P)),
            (resp_w[:], i.resp_w.rearrange("(c p) r -> p c r", p=P)),
            (resp_row[R:R + 1, :], row(i.resp_b)),
            (safety_row[R:R + 1, :], row(i.safety_bias)),
            (gate_w1[:], i.gate_w1),
            (gate_b1[:], i.gate_b1.rearrange("(n a) -> n a", a=1)),
            (gate_w2[:], i.gate_w2.rearrange("a n -> n a")),
            (gate_b2[:], bc(i.gate_b2, 1)),
            (score[:], bc(i.score, B)),
            (step_i[:], bc(i.step, B)),
            (freq[:], i.freq.rearrange("(c p) -> p c", p=P)),
            (angle[:, 0:2], bc(i.theta, B)),
            (angle[:, 2:4], bc(i.phi, B)),
            (w_ada[:], i.W_ada.rearrange("(c p) n -> p c n", p=P)),
            (b_ada_t[:], i.b_ada.rearrange("(f p) -> p f", p=P)),
            (b_ada_bc[:], bc(i.b_ada, 2 * D)),
            (keep.bq[:], i.bq.rearrange("(m p) -> p m", p=P)),
            (keep.bk[:], i.bk.rearrange("(m p) -> p m", p=P)),
            (keep.bv[:], bc(i.bv, D)),
        ]

        with nc.Block() as block:
            @block.sync
            def _(sp):
                for dst, src in loads:
                    sp.dma_start(dst, src, allow_slow_non_contiguous=True).then_inc(small_loaded, 16)
                with sp.Fori(0, NG // 2) as it:
                    for n in range(2):
                        sp.wait_ge(mean_tiles, it * 2 + n + 1)
                        sp.dma_start(x_in[:, n], x_g[ds(it * 2 + n, 1)].rearrange("a p t d -> p (a t) d")).then_inc(x_loaded[n], 16)

            @block.gpsimd
            def _(pool):
                nc.gpsimd.memset(keep.eye[:], 0.0).then_inc(eye_wiped, 1)
                pool.wait_ge(eye_wiped, 1)
                nc.gpsimd.affine_select(out=keep.eye[:], in_=keep.eye[:], compare_op=ALU.not_equal, fill=1.0,
                                        base=0, pattern=[[-1, P]], channel_multiplier=1).then_inc(eye_ready, 1)
                for n, src in enumerate((i.Wq, i.Wk, i.Wv)):
                    if n:
                        pool.wait_ge(w_low, n)
                    pool.dma_start(wraw[:], src.rearrange("(c p) n -> p c n", p=P)).then_inc(w_loaded, 16)
                    pool.wait_ge(w_loaded, 16 * (n + 1))
                    nc.gpsimd.tensor_copy(keep.w_hi[:, n], wraw[:]).then_inc(w_split, 1)
                    pool.wait_ge(w_split, n + 1)
                    nc.gpsimd.tensor_tensor(keep.w_lo[:, n], wraw[:], keep.w_hi[:, n].bitcast(F32), ALU.subtract).then_inc(w_low, 1)

            @block.vector
            def _(dve):
                link = Link(dve, own)
                nc.vector.memset(turns[:], 0.0).then_inc(mean_tiles, 2)
                nc.vector.memset(coef[:], 0.0).then_inc(basis_ready, 1)
                nc.vector.memset(mean_w[:], 1.0 / S).then_inc(consts_set, 1)
                nc.vector.memset(ones[:], 1.0).then_inc(consts_set, 1)
                nc.vector.memset(norm2_mask[:, 0:32], 1.0).then_inc(consts_set, 1)
                nc.vector.memset(norm2_mask[:, 32:64], 0.0).then_inc(consts_set, 1)
                nc.vector.memset(keep.eps5[:], 1e-5).then_inc(consts_set, 1)
                nc.vector.memset(keep.y33[R:R + 1, :], 1.0).then_inc(consts_set, 1)
                link(nc.vector.memset(shift_t[:, 0:8], 0.0))
                link(nc.vector.memset(shift_t[:, 8:16], 0.25))
                link(nc.vector.memset(shift_a[:, 0:8], 0.0))
                link(nc.vector.memset(shift_a[:, 8:16], PI / 2))
                dve.wait_ge(consts_set, 6)
                dve.wait_ge(small_loaded, 16 * len(loads))

                with dve.Fori(0, R // 2) as it:
                    for n in range(2):
                        src, dst = basis[n], basis[1 - n]
                        chain = Link(dve, own, base=4 + 7 * n, per=14, at=it)
                        dve.wait_ge(nrm_ready, it * 2 + n + 1)
                        chain(nc.vector.tensor_tensor(
                            coef[:], coef_ps[n][:, :, 1:R],
                            norm2_mask[:, ds(it * 2 + n + 1, R - 1)].unsqueeze(1).to_broadcast([P, 2, R - 1]), ALU.mult))
                        chain(nc.vector.tensor_scalar(rr[:], nrm[:, n], 1e-8, None, ALU.add))
                        chain(nc.vector.reciprocal(rr[:], rr[:]))
                        chain(nc.vector.tensor_tensor(r2[:], rr[:], rr[:], ALU.mult))
                        chain(nc.vector.tensor_tensor(coef2[:], coef[:], r2[:].unsqueeze(2).to_broadcast([P, 2, R - 1]), ALU.mult))
                        chain(nc.vector.tensor_tensor(
                            outer_p[:], src[:, :, :, 0:1].to_broadcast([P, C, 2, R - 1]),
                            coef2[:].unsqueeze(1).to_broadcast([P, C, 2, R - 1]), ALU.mult))
                        chain(nc.vector.tensor_tensor(dst[:, :, :, 0:R - 1], src[:, :, :, 1:R], outer_p[:], ALU.subtract))
                        nc.vector.tensor_tensor(dst[:, :, :, R - 1:R], src[:, :, :, 0:1],
                                                rr[:].unsqueeze(1).unsqueeze(3).to_broadcast([P, C, 2, 1]), ALU.mult).then_inc(basis_ready, 1)
                        dve.wait_ge(basis_ready, it * 2 + n + 2)
                link = Link(dve, own, base=4 + 7 * R)

                link(nc.vector.tensor_copy(step_f[:], step_i[:]))
                link(nc.vector.tensor_scalar(step_f[:], step_f[:], 40.0, None, ALU.mult))
                for c in range(2):
                    link(nc.vector.tensor_scalar(angle[:, 4 + 2 * c:6 + 2 * c], step_f[:], freq[:, c:c + 1], None, ALU.mult))
                link(nc.vector.tensor_copy(angle[:, 8:16], angle[:, 0:8]))
                link(nc.vector.tensor_scalar(turns[:], angle[:], 1.0 / (2 * PI), None, ALU.mult))
                link(nc.vector.tensor_tensor(turns[:], turns[:], shift_t[:], ALU.add))
                link(nc.vector.tensor_scalar(turns[:], turns[:], ROUND, None, ALU.add))
                link(nc.vector.tensor_scalar(turns[:], turns[:], -ROUND, None, ALU.add))
                for part in (TWO_PI_A, TWO_PI_B, TWO_PI_C):
                    link(nc.vector.scalar_tensor_tensor(angle[:], turns[:], -part, angle[:], ALU.mult, ALU.add))
                link(nc.vector.tensor_tensor(angle[:], angle[:], shift_a[:], ALU.add))
                nc.vector.tensor_scalar(angle[:], angle[:], 3.1415925, -3.1415925, ALU.min, ALU.max).then_inc(angles_ready, 1)
                dve.wait_ge(sincos_ready, 3)
                nc.vector.tensor_tensor(z[:, 0:2].rearrange("p c b -> p (c b)"), sincos[:, 4:8], sig[:, 0:4], ALU.mult).then_inc(z_ready, 1)
                nc.vector.tensor_tensor(z[:, 2:4].rearrange("p c b -> p (c b)"), sincos[:, 12:16], sig[:, 4:8], ALU.mult).then_inc(z_ready, 1)

                for col, src, sign in ((0, 0, 1.0), (1, 0, -1.0), (2, 2, 1.0), (3, 2, -1.0)):
                    link(nc.vector.tensor_copy(rot_c[:, :, 0, col], sincos[:, 8 + src:10 + src]))
                    link(nc.vector.tensor_scalar(rot_c[:, :, 1, col], sincos[:, src:src + 2], sign, None, ALU.mult))

                dve.wait_ge(mean_tiles, 2 + NG)
                for b in range(B):
                    link(nc.vector.tensor_tensor_reduce(out=prod[:], in0=pool_mean[b][:], in1=gate_w1[:], scale=1.0, scalar=0.0,
                                                        op0=ALU.mult, op1=ALU.add, accum_out=h1[:, b:b + 1]))
                link(nc.vector.tensor_scalar(h1r[:], h1[:], gate_b1[:], 0.0, ALU.add, ALU.max))
                nc.vector.tensor_scalar(h1[:], h1r[:], gate_w2[:], None, ALU.mult).then_inc(h1_ready, 1)
                dve.wait_ge(gate_ready, 2)
                link(nc.vector.tensor_tensor(strength[:], base_act[:], mod[:], ALU.mult))

                dve.wait_ge(ada_ps_ready, 1)
                link(nc.vector.tensor_tensor(keep.ada[:], ada_ps[:], b_ada_t[:].unsqueeze(2).to_broadcast([P, 2 * C, B]), ALU.add))
                link(nc.vector.tensor_scalar(keep.ada[:, 0:C], keep.ada[:, 0:C], 1.0, None, ALU.add))
                for b in range(B):
                    for half in range(2):
                        n = 2 * b + half
                        dve.wait_ge(row_ready, n + 1)
                        nc.vector.scalar_tensor_tensor(keep.ada_row[:, b, half], row_ps[n % 2][:], 1.0 - half,
                                                       b_ada_bc[:, half * D:(half + 1) * D], ALU.add, ALU.add).then_inc(row_taken, 1)
                dve.wait_ge(vtv_ready, 1)
                nc.vector.tensor_copy(vtv[:], small_ps[0:R, 0:R]).then_inc(vtv_taken, 1)
                dve.wait_ge(respt_ready, C)
                nc.vector.tensor_copy(resp_t[:], row_ps[0][0:R, :]).then_inc(respt_taken, 1)
                dve.wait_ge(a1_ready, 1)
                nc.vector.tensor_copy(a1[:], row_ps[1][0:R, :]).then_inc(a1_taken, 1)
                dve.wait_ge(g_ready, 1)
                link(nc.vector.tensor_copy(g33[0:R, :], row_ps[0][0:R, :]))
                link(nc.vector.tensor_tensor(g33[R:R + 1, :], resp_row[R:R + 1, :], safety_row[R:R + 1, :], ALU.add))

                dve.wait_ge(eye_ready, 1)
                pair = lambda ap: ap.rearrange("p (n two) -> p n two", two=2)
                link(nc.vector.tensor_copy(keep.eye_bf[:], keep.eye[:]))
                for src, dst in ((g33, g33s), (keep.eye, eye_s)):
                    link(nc.vector.tensor_copy(pair(dst[:])[:, :, 0], pair(src[:])[:, :, 1]))
                    link(nc.vector.tensor_copy(pair(dst[:])[:, :, 1], pair(src[:])[:, :, 0]))
                quad = lambda ap: ap.rearrange("p (n four) -> p n four", four=4)
                for b in range(B):
                    for src, swapped, tmp, dst, n in ((g33, g33s, gtmp, keep.g33[:, b], R + 1), (keep.eye, eye_s, eye_c, keep.rot[:, b], P)):
                        m = src.shape[1] // 4
                        c_of = lambda w: rot_c[0:n, b, w].unsqueeze(1).to_broadcast([n, m, 4])
                        link(nc.vector.tensor_tensor(quad(tmp[:]), quad(swapped[:]), c_of(1), ALU.mult))
                        link(nc.vector.tensor_tensor(quad(dst), quad(src[:]), c_of(0), ALU.mult))
                        link(nc.vector.tensor_tensor(dst, dst, tmp[:], ALU.add))
                    link(nc.vector.tensor_scalar(keep.g33[:, b], keep.g33[:, b], strength[0:R + 1, b:b + 1], None, ALU.mult))
                link(nc.vector.tensor_scalar(keep.bq[:], keep.bq[:], DH ** -0.5, None, ALU.mult))

            @block.scalar
            def _(act):
                with act.Fori(0, R // 2) as it:
                    for n in range(2):
                        act.wait_ge(coef_ready, it * 2 + n + 1)
                        nc.scalar.activation(nrm[:, n], coef_ps[n][:, :, 0], ACT.Sqrt).then_inc(nrm_ready, 1)
                act.wait_ge(angles_ready, 1)
                nc.scalar.activation(sincos[:], angle[:], ACT.Sin).then_inc(sincos_ready, 1)
                act.wait_ge(sincos_ready, 1)
                nc.scalar.activation(sig[:, 0:4], sincos[:, 4:8], ACT.Sigmoid).then_inc(sincos_ready, 1)
                nc.scalar.activation(sig[:, 4:8], sincos[:, 12:16], ACT.Sigmoid).then_inc(sincos_ready, 1)
                act.wait_ge(sincos_ready, 3)
                nc.scalar.activation(mod[:], score[:], ACT.Sigmoid).then_inc(gate_ready, 1)
                act.wait_ge(gate_ps_ready, 1)
                nc.scalar.activation(base_act[:], coef_ps[0][:, 0, 0:B], ACT.Sigmoid, bias=gate_b2[:]).then_inc(gate_ready, 1)

            @block.tensor
            def _(pe):
                mm = nc.tensor.matmul
                pe.wait_ge(consts_set, 6)
                for b in range(B):
                    for g in range(GB):
                        n = b * GB + g
                        pe.wait_ge(x_loaded[n % 2], 16 * (n // 2 + 1))
                        for t in range(GT):
                            last = mm(pool_mean[b][:], mean_w[:], x_in[:, n % 2, t, :], start=(g == 0 and t == 0),
                                      stop=(g == GB - 1 and t == GT - 1))
                        last.then_inc(mean_tiles, 1)
                pe.wait_ge(small_loaded, 16 * len(loads))
                with pe.Fori(0, R // 2) as it:
                    for n in range(2):
                        pe.wait_ge(basis_ready, it * 2 + n + 1)
                        for w in range(2):
                            for c in range(C):
                                last = mm(coef_ps[n][:, w, :], basis[n][:, c, w, 0:1].to_broadcast([P, P]), basis[n][:, c, w, :],
                                          start=(c == 0), stop=(c == C - 1))
                        last.then_inc(coef_ready, 1)
                pe.wait_ge(z_ready, 2)
                for f in range(2 * C):
                    for c in range(C):
                        last = mm(ada_ps[:, f, :], w_ada[:, c, f * P:(f + 1) * P], z[:, c, :], start=(c == 0), stop=(c == C - 1))
                last.then_inc(ada_ps_ready, 1)
                pe.wait_ge(h1_ready, 1)
                mm(coef_ps[0][:, 0, 0:B], ones[:], h1[:], start=True, stop=True).then_inc(gate_ps_ready, 1)
                for b in range(B):
                    for half in range(2):
                        n = 2 * b + half
                        if n >= 2:
                            pe.wait_ge(row_taken, n - 1)
                        for c in range(C):
                            last = mm(row_ps[n % 2][:], z[:, c, b:b + 1].to_broadcast([P, P]), w_ada[:, c, half * D:(half + 1) * D],
                                      start=(c == 0), stop=(c == C - 1))
                        last.then_inc(row_ready, 1)
                q0 = basis[0]
                for c in range(C):
                    last = mm(small_ps[0:R, 0:R], q0[:, c, 1, :], q0[:, c, 1, :], start=(c == 0), stop=(c == C - 1))
                last.then_inc(vtv_ready, 1)
                pe.wait_ge(row_taken, 4)
                pe.wait_ge(eye_ready, 1)
                for c in range(C):
                    nc.tensor.transpose(row_ps[0][0:R, c * P:(c + 1) * P], resp_w[:, c, :], keep.eye[:]).then_inc(respt_ready, 1)
                pe.wait_ge(respt_taken, 1)
                mm(row_ps[1][0:R, :], q0[0:R, 0, 0, :], resp_t[:], start=True, stop=True).then_inc(a1_ready, 1)
                pe.wait_ge(vtv_taken, 1)
                pe.wait_ge(a1_taken, 1)
                mm(row_ps[0][0:R, :], vtv[:], a1[:], start=True, stop=True).then_inc(g_ready, 1)


def each_row(eng):
    for b in range(B):
        yield b, eng.Fori(b * GB, (b + 1) * GB)


def embed(k, i, keep, scr):
    nc = k.nc
    with ExitStack() as ctx:
        sb = lambda *a: k.sb(ctx, *a)
        x_in = sb("x_in", [P, GT, D])
        xt = sb("xt", [P, C, GTOK])
        stats, mv = sb("stats1", [P, 6]), sb("mv1", [P, GT, 2])
        std, rstd = sb("std1", [P, GT]), sb("rstd1", [P, GT])
        xn = sb("xn1", [P, GT, D])
        x2 = sb("x2_out", [P, GT, D])
        t32 = sb("t32_1", [P, 2, GTOK])
        th, tl = sb("th1", [P, C, GTOK], F32R), sb("tl1", [P, C, GTOK], F32R)
        tp = [k.ps(ctx, f"tp{n}", [P, 512]) for n in range(2)]
        yp = k.ps(ctx, "yp", [P, 512])
        x1p = [k.ps(ctx, f"x1p{n}", [P, D]) for n in range(2)]

        x_loaded, x_read, xt_turned, xt_taken = (k.sem("em_" + n) for n in ("x_loaded", "x_read", "xt_turned", "xt_taken"))
        y_ready, y_taken, x1_ready, x1_taken = (k.sem("em_" + n) for n in ("y_ready", "y_taken", "x1_ready", "x1_taken"))
        own_idle = k.sem("em_idle")
        var_ready, std_ready, own, xn_ready = (k.sem("em_" + n) for n in ("var_ready", "std_ready", "dve_chain", "xn_ready"))
        xnt_turned, t32_ready, t32_split = (k.sem("em_" + n) for n in ("xnt_turned", "t32_ready", "t32_split"))
        x2_ready, pool_own, x2_stored, t_stored = (k.sem("em_" + n) for n in ("x2_ready", "pool_chain", "x2_stored", "t_stored"))
        x_g = i.x.rearrange("b (g t p) d -> (b g) p t d", t=GT, p=P)
        x2_g = scr.x2.rearrange("(g t p) d -> g p t d", t=GT, p=P)
        tile_of = lambda ap, it: ap[ds(it, 1)].rearrange("a p t d -> p (a t) d")

        def store(sp, it):
            sp.wait_ge(x2_ready, it * GT + GT + 1)
            sp.dma_start(tile_of(x2_g, it), x2[:]).then_inc(x2_stored, 16)
            sp.wait_ge(t32_split, it * C + C + 2)
            for w, src in enumerate((th, tl)):
                sp.dma_start(scr.x2t[w].rearrange("(c p) n -> p c n", p=P)[:, :, ds(it * GTOK, GTOK)],
                             src[:].bitcast(F32)).then_inc(t_stored, 16)

        with nc.Block() as block:
            @block.sync
            def _(sp):
                sp.dma_start(x_in[:], tile_of(x_g, 0)).then_inc(x_loaded, 16)
                with sp.Fori(0, NG - 1) as it:
                    sp.wait_ge(xt_turned, it * GT + GT)
                    sp.dma_start(x_in[:], tile_of(x_g, it + 1)).then_inc(x_loaded, 16)
                    store(sp, it)
                store(sp, NG - 1)
                sp.wait_ge(x2_stored, 16 + 16 * NG)
                sp.wait_ge(t_stored, 32 + 32 * NG)

            @block.gpsimd
            def _(pool):
                pool.sem_inc(x2_stored, 16)
                pool.sem_inc(x2_ready, 1)
                for b, turn in each_row(pool):
                  with turn as it:
                    for t in range(GT):
                        pool.wait_ge(xn_ready, it * GT + t + 1)
                        if t == 0:
                            pool.wait_ge(x2_stored, it * 16 + 16)
                        nc.gpsimd.tensor_tensor(x2[:, t], xn[:, t], keep.ada_row[:, b, 0], ALU.mult).then_inc(pool_own, 1)
                        pool.wait_ge(pool_own, it * GT + t + 1)
                        nc.gpsimd.tensor_tensor(x2[:, t], x2[:, t], keep.ada_row[:, b, 1], ALU.add).then_inc(x2_ready, 1)

            @block.tensor
            def _(pe):
                mm = nc.tensor.matmul
                for b, turn in each_row(pe):
                  with turn as it:
                    pe.wait_ge(x_loaded, it * 16 + 16)
                    for t in range(GT):
                        pe.wait_ge(t32_ready, it * C + t + 3) if t < 2 else pe.wait_ge(xt_taken, it * GT + t - 1)
                        for c in range(C):
                            last = nc.tensor.transpose(tp[t % 2][:, c * P:(c + 1) * P], x_in[:, t, c * P:(c + 1) * P], keep.eye[:])
                        last.then_inc(xt_turned, 1)
                    pe.wait_ge(xt_taken, it * GT + GT)
                    for c in range(C):
                        last = mm(yp[0:R, :], keep.basis[:, c, 0, :], xt[:, c, :], start=(c == 0), stop=(c == C - 1))
                    last.then_inc(y_ready, 1)
                    pe.wait_ge(y_taken, it + 1)
                    for t in range(GT):
                        pe.wait_ge(x1_taken, it * GT + t + 1)
                        tok = slice(t * P, (t + 1) * P)
                        mm(x1p[t % 2][:], keep.y33[:, tok], keep.g33[:, b], start=True, stop=False, skip_group_check=True)
                        for c in range(C):
                            last = mm(x1p[t % 2][:, c * P:(c + 1) * P], xt[:, c, tok], keep.rot[:, b],
                                      start=False, stop=(c == C - 1), skip_group_check=True)
                        last.then_inc(x1_ready, 1)
                    pe.wait_ge(xn_ready, it * GT + GT)
                    for c in range(C):
                        pe.wait_ge(xt_taken, it * GT + c + 3) if c < 2 else pe.wait_ge(t32_ready, it * C + C + c - 1)
                        for t in range(GT):
                            last = nc.tensor.transpose(tp[c % 2][:, t * P:(t + 1) * P], xn[:, t, c * P:(c + 1) * P], keep.eye[:])
                        last.then_inc(xnt_turned, 1)

            @block.scalar
            def _(act):
                act.sem_inc(t32_ready, C)
                act.sem_inc(t32_split, 2)
                act.sem_inc(xnt_turned, 1)
                for b, turn in each_row(act):
                  with turn as it:
                    for t in range(GT):
                        act.wait_ge(xt_turned, it * GT + t + 1)
                        if t == 0:
                            act.wait_ge(x1_taken, it * GT + 2)
                        nc.scalar.copy(xt[:, :, t * P:(t + 1) * P], tp[t % 2][:].rearrange("p (c n) -> p c n", c=C)).then_inc(xt_taken, 1)
                    act.wait_ge(y_ready, it + 1)
                    nc.scalar.copy(keep.y33[0:R, :], yp[0:R, :]).then_inc(y_taken, 1)
                    for t in range(GT):
                        act.wait_ge(var_ready, it * GT + t + 1)
                        nc.scalar.activation(std[:, t:t + 1], mv[:, t, 1:2], ACT.Sqrt, bias=keep.eps5[:]).then_inc(std_ready, 1)
                    for c in range(C):
                        act.wait_ge(xnt_turned, it * C + c + 2)
                        act.wait_ge(t32_split, it * C + c + 1)
                        nc.scalar.activation(t32[:, c % 2], tp[c % 2][:], ACT.Identity,
                                             scale=keep.ada[:, c, b:b + 1], bias=keep.ada[:, C + c, b:b + 1]).then_inc(t32_ready, 1)

            @block.vector
            def _(dve):
                dve.sem_inc(x1_taken, 2)
                dve.sem_inc(t_stored, 32)
                for b, turn in each_row(dve):
                  with turn as it:
                    link = Link(dve, own, per=GT * 2 + C, at=it)
                    dve.wait_ge(xnt_turned, it * C + 1)
                    dve.wait_ge(x2_ready, it * GT + 1)
                    for t in range(GT):
                        dve.wait_ge(x1_ready, it * GT + t + 1)
                        link(nc.vector.bn_stats(stats[:], x1p[t % 2][:]))
                        dve.sem_inc(own_idle, 1)
                        nc.vector.bn_aggr(mv[:, t], stats[:]).then_inc(var_ready, 1)
                        dve.wait_ge(std_ready, it * GT + t + 1)
                        link(nc.vector.reciprocal(rstd[:, t:t + 1], std[:, t:t + 1]))
                        nc.vector.tensor_scalar(xn[:, t], x1p[t % 2][:], mv[:, t, 0:1], rstd[:, t:t + 1], ALU.subtract, ALU.mult).then_inc(xn_ready, 1)
                        dve.wait_ge(xn_ready, it * GT + t + 1)
                        dve.sem_inc(x1_taken, 1)
                    dve.wait_ge(t_stored, it * 32 + 32)
                    for c in range(C):
                        dve.wait_ge(t32_ready, it * C + C + c + 1)
                        link(nc.vector.tensor_copy(th[:, c], t32[:, c % 2]))
                        nc.vector.tensor_tensor(tl[:, c], t32[:, c % 2], th[:, c].bitcast(F32), ALU.subtract).then_inc(t32_split, 1)


def project(k, i, keep, scr):
    nc = k.nc
    with ExitStack() as ctx:
        sb = lambda *a: k.sb(ctx, *a)
        xt = [[sb(f"x2t_{n}_{w}", [P, C, GTOK], F32R) for w in range(2)] for n in range(2)]
        q32 = sb("q32", [P, 2, GTOK])
        parts = [sb(f"qk_parts{n}", [P, 2, GTOK], F32R) for n in range(2)]
        v_out = [sb(f"v_out{n}", [P, D]) for n in range(2)]
        mask_in = [sb(f"mask_in{n}", [P, S // 4], I32) for n in range(2)]
        mask_bf = [sb(f"mask_bf{n}", [P, S], BF16) for n in range(2)]
        bank = [k.ps(ctx, f"pj{n}", [P, 512]) for n in range(8)]
        x_loaded = [k.sem(f"pj_x_loaded{n}") for n in range(2)]
        x_used, job_ready, qk_taken, v_taken = (k.sem("pj_" + n) for n in ("x_used", "job_ready", "qk_taken", "v_taken"))
        hi_done, lo_done = k.sem("pj_hi_done"), k.sem("pj_lo_done")
        qk_stored = [k.sem(f"pj_qk_stored{n}") for n in range(2)]
        v_stored = [k.sem(f"pj_v_stored{n}") for n in range(2)]
        m_loaded, m_stored, m_credit = ([k.sem(f"pj_{n}{j}") for j in range(2)] for n in ("m_loaded", "m_stored", "m_credit"))
        m_cast = k.sem("pj_m_cast")
        NJ = 3 * C

        def load(sp, g, n):
            for w in range(2):
                sp.dma_start(xt[n][w][:].bitcast(F32),
                             scr.x2t[w].rearrange("(c p) n -> p c n", p=P)[:, :, ds(g * GTOK, GTOK)]).then_inc(x_loaded[n], 16)

        def pair(sp, it, more):
            for n in range(2):
                g = it * 2 + n
                for m in range(2 * C):
                    sp.wait_ge(lo_done, g * 2 * C + m + 1)
                    dst = (scr.q if m < C else scr.k)[:, (m % C) * P:(m % C + 1) * P, ds(g * GTOK, GTOK)]
                    sp.dma_start(dst.rearrange("w f s -> f w s"), parts[m % 2][:].bitcast(F32)).then_inc(qk_stored[m % 2], 16)
                for t in range(GT):
                    sp.wait_ge(v_taken, g * GT + t + 1 + GT)
                    sp.dma_start(scr.v[ds(g * GTOK + t * P, P), :], v_out[t % 2][:]).then_inc(v_stored[t % 2], 16)
                if more:
                    sp.wait_ge(x_used, g + 1)
                    load(sp, g + 2, n)

        with nc.Block() as block:
            @block.sync
            def _(sp):
                for n in range(2):
                    load(sp, n, n)
                with sp.Fori(0, NG // 2 - 1) as it:
                    pair(sp, it, True)
                pair(sp, NG // 2 - 1, False)
                for n in range(2):
                    sp.wait_ge(qk_stored[n], 16 + 16 * NG * C)
                    sp.wait_ge(v_stored[n], 16 + 16 * NG * GT // 2)

            @block.gpsimd
            def _(pool):
                mask_rows = i.mask.rearrange("b a q s -> (b a q) s")
                pool.sem_inc(m_cast, 2)
                for n in range(2):
                    pool.sem_inc(m_credit[n], 16)
                with pool.Fori(0, TOK // P // 2) as it:
                    for n in range(2):
                        pool.wait_ge(m_cast, it * 2 + n + 1)
                        pool.dma_start(mask_in[n][:], mask_rows[ds(it * 2 * P + n * P, P), :]).then_inc(m_loaded[n], 16)
                    for n in range(2):
                        pool.wait_ge(m_cast, it * 2 + n + 3)
                        pool.dma_start(scr.mask[ds(it * 2 * P + n * P, P), :], mask_bf[n][:]).then_inc(m_stored[n], 16)
                        pool.wait_ge(m_stored[n], it * 16 + 16)
                        pool.sem_inc(m_credit[n], 16)

            @block.tensor
            def _(pe):
                mm = nc.tensor.matmul
                with pe.Fori(0, NG // 2) as it:
                    for n in range(2):
                        g = it * 2 + n
                        pe.wait_ge(x_loaded[n], it * 32 + 32)
                        hi, lo = xt[n]
                        for j in range(NJ):
                            at = bank[(n * NJ + j) % 8]
                            if j < C:
                                pe.wait_ge(qk_taken, g * 2 * C + j + C + 1)
                            elif j < 2 * C:
                                pe.wait_ge(v_taken, g * GT + j - C + 1)
                            else:
                                pe.wait_ge(qk_taken, g * 2 * C + j + 1)
                            first, last = True, None
                            for c in range(C):
                                for a, w in ((hi, keep.w_hi), (lo, keep.w_hi), (hi, keep.w_lo)):
                                    end = c == C - 1 and w is keep.w_lo
                                    if j < 2 * C:
                                        m = j % C
                                        last = mm(at[:], w[:, j // C, c, m * P:(m + 1) * P], a[:, c, :], start=first, stop=end)
                                    else:
                                        t = j - 2 * C
                                        last = mm(at[:], a[:, c, t * P:(t + 1) * P], w[:, 2, c, :], start=first, stop=end)
                                    first = False
                            last.then_inc(job_ready, 1)
                            if j == NJ - 1:
                                pe.wait_ge(job_ready, g * NJ + NJ)
                                pe.sem_inc(x_used, 1)

            @block.scalar
            def _(act):
                act.sem_inc(qk_taken, 2 * C)
                with act.Fori(0, NG // 2) as it:
                    for n in range(2):
                        g = it * 2 + n
                        for j in range(2 * C):
                            act.wait_ge(job_ready, g * NJ + j + 1)
                            if j < 2:
                                act.wait_ge(v_taken, g * GT + GT)
                            else:
                                act.wait_ge(lo_done, g * 2 * C + j - 1)
                            bias, scale = (keep.bq, DH ** -0.5) if j < C else (keep.bk, 1.0)
                            nc.scalar.activation(q32[:, j % 2], bank[(n * NJ + j) % 8][:], ACT.Identity,
                                                 scale=scale, bias=bias[:, j % C:j % C + 1]).then_inc(qk_taken, 1)

            @block.vector
            def _(dve):
                dve.sem_inc(v_taken, GT)
                for n in range(2):
                    dve.sem_inc(qk_stored[n], 16)
                    dve.sem_inc(v_stored[n], 16)
                with dve.Fori(0, NG // 2) as it:
                    for n in range(2):
                        g = it * 2 + n
                        for j in range(2 * C):
                            dve.wait_ge(qk_taken, g * 2 * C + 2 * C + j + 1)
                            dve.wait_ge(qk_stored[j % 2], (g * C + j // 2) * 16 + 16)
                            nc.vector.tensor_copy(parts[j % 2][:, 0], q32[:, j % 2]).then_inc(hi_done, 1)
                            dve.wait_ge(hi_done, g * 2 * C + j + 1)
                            nc.vector.tensor_tensor(parts[j % 2][:, 1], q32[:, j % 2], parts[j % 2][:, 0].bitcast(F32), ALU.subtract).then_inc(lo_done, 1)
                        for t in range(GT):
                            dve.wait_ge(job_ready, g * NJ + 2 * C + t + 1)
                            dve.wait_ge(v_stored[t % 2], (g * 2 + t // 2) * 16 + 16)
                            nc.vector.tensor_tensor(v_out[t % 2][:], bank[(n * NJ + 2 * C + t) % 8][:], keep.bv[:], ALU.add).then_inc(v_taken, 1)
                            dve.wait_ge(m_loaded[t % 2], (g * 2 + t // 2) * 16 + 16)
                            dve.wait_ge(m_credit[t % 2], (g * 2 + t // 2) * 16 + 16)
                            nc.vector.tensor_copy(mask_bf[t % 2][:], mask_in[t % 2][:].bitcast(U8)).then_inc(m_cast, 1)


def attend(k, i, keep, scr):
    nc = k.nc
    UNITS = 2 * HG
    RING = 7
    SHARED = ((0, 0), (2, 0), (3, 0), (5, 0))
    LEAD = 2
    LAG = 2
    PV_CHUNKS = 20
    PV_SKIP = 4
    NCH = S // 512
    KH = KT // 2
    with ExitStack() as ctx:
        sb = lambda *a: k.sb(ctx, *a)
        kst = [sb(f"k_stack{h}", [P, S], F32R) for h in range(HG)]
        qst = [sb(f"q_stack{t}", [P, HG, P], F32R) for t in range(2)]
        vt = sb("v_tile", [P, KT, P])
        mask = [sb(f"mask{t}", [P, S], BF16) for t in range(2)]
        unit = [sb(f"unit{u}", [P, S]) for u in range(UNITS)]
        probs_t = [sb(f"probs_t{c}", [P, HG, KH, QB]) for c in range(2)]
        part_max, neg_max = sb("part_max", [P, UNITS, NCH]), sb("neg_max", [P, UNITS])
        total, inv_total = sb("total", [P, UNITS]), sb("inv_total", [P, UNITS])
        masked = sb("masked", [P, P], BF16)
        ctx_t = sb("ctx_t", [P, QB])
        ctx_out = sb("ctx_out", [P, 2, P])
        w32 = sb("w32", [P, D])
        whr, wlr = sb("whr", [P, D], F32R), sb("wlr", [P, D], F32R)
        expert = sb("expert", [1, B], I32)
        ring = [k.ps(ctx, f"ring{n}", [P, 512]) for n in range(RING)]
        out_ps = k.ps(ctx, "out_ps", [P, 2 * QB])
        ctx_ps, back_ps = out_ps[:, 0:QB], out_ps[:, QB:2 * QB].rearrange("p (t f) -> p t f", t=2)

        bias_loaded = [k.sem(f"at_bias_loaded{u}") for u in range(UNITS)]
        qm_loaded = [k.sem(f"at_qm_loaded{t}") for t in range(2)]
        k_loaded = [k.sem(f"at_k_loaded{h}") for h in range(HG)]
        v_loaded, masked_set = k.sem("at_v_loaded"), k.sem("at_masked_set")
        sc_ready = k.sem("at_sc_ready")
        bank_free = [k.sem(f"at_bank_free{n}") for n in range(RING)]
        max_ready, max_parts, max_read = k.sem("at_max_ready"), k.sem("at_max_parts"), k.sem("at_max_read")
        exp_done, inv_ready = k.sem("at_exp_done"), k.sem("at_inv_ready")
        turned = [k.sem(f"at_turned_{n}") for n in ("low", "high")]
        pv_half, ctx_taken, back_ready, normed = (k.sem("at_" + n) for n in ("pv_half", "ctx_taken", "back_ready", "normed"))
        ctx_stored, idle, pool_idle = k.sem("at_ctx_stored"), k.sem("at_idle"), k.sem("at_pool_idle")
        w_loaded, w_high, w_low, w_stored, e_loaded = (k.sem("at_" + n) for n in ("w_loaded", "w_high", "w_low", "w_stored", "e_loaded"))

        scored = lambda u: [("scores", u, c) for c in range(NCH)]
        halves = lambda u, c: [(which, u, c) for which in (1, 0)]
        SECOND = [(6, 0), (0, 1), (1, 1), (7, 0)] + [(u, 1) for u in range(2, UNITS)]
        order = []
        for u in range(LEAD, UNITS):
            order += scored(u) + (halves(u - LAG, 0) if u >= LAG else [])
        for u, c in SECOND:
            order += halves(u, c) + (scored(u - UNITS + LEAD) if c and u >= UNITS - LEAD else [])
        SHORT = (-len(order)) % RING * (RING - 1)
        banks = [n % (RING - 1) if n < SHORT else (n - SHORT) % RING for n in range(len(order))]
        fills = [banks.count(n) for n in range(RING)]
        led = [banks[n] for n, what in enumerate(order) if what[0] == "scores" and what[1] < LEAD]
        turns = lambda which: [what for what in order if what[0] == which]

        def place(*what):
            n = order.index(what)
            return banks[n], banks[:n].count(banks[n])

        bias_rows = i.bias.rearrange("b h q s -> (b h q) s")
        PER_ROW = NHG * NQ

        def where(s):
            b = s // PER_ROW
            return b * S + (s % NQ) * QB, b * S, ((s // NQ) % NHG) * P

        def load_qm(sp, s, t):
            row, _, feat = where(s)
            for a in range(4):
                src = scr.q[a // 2, ds(feat, P), ds(row + t * P, P)]
                sp.dma_start(qst[t][a * DH:(a + 1) * DH].bitcast(F32), src.rearrange("(h d) s -> d h s", d=DH)).then_inc(qm_loaded[t], 16)
            sp.dma_start(mask[t][:], scr.mask[ds(row + t * P, P), :]).then_inc(qm_loaded[t], 16)

        def load_bias(sp, s, u):
            t, h = u // HG, u % HG
            row = ((s // NQ) * HG + h) * S + (s % NQ) * QB + t * P
            sp.dma_start(unit[u][:], bias_rows[ds(row, P), :]).then_inc(bias_loaded[u], 16)

        def store_ctx(sp, s):
            row, _, feat = where(s)
            sp.wait_ge(normed, s + 2)
            sp.dma_start(scr.ctx[ds(row, QB), ds(feat, P)].rearrange("(t p) f -> p t f", p=P), ctx_out[:]).then_inc(ctx_stored, 16)

        with nc.Block() as block:
            @block.sync
            def _(sp):
                for t in range(2):
                    load_qm(sp, 0, t)
                    for u in range(t * HG, (t + 1) * HG):
                        load_bias(sp, 0, u)
                def next_step(s, before):
                    for t in range(2):
                        sp.wait_ge(sc_ready, (s * UNITS + (t + 1) * HG) * NCH)
                        load_qm(sp, s + 1, t)
                        for u in range(t * HG, (t + 1) * HG):
                            for which in range(2):
                                sp.wait_ge(turned[which], s * 2 * UNITS + turns(which).index((which, u, 1)) + 1)
                            load_bias(sp, s + 1, u)
                            if u == HG and before is not None:
                                store_ctx(sp, before)

                next_step(0, None)
                with sp.Fori(1, STEPS - 1) as s:
                    next_step(s, s - 1)
                store_ctx(sp, STEPS - 2)
                store_ctx(sp, STEPS - 1)
                sp.wait_ge(ctx_stored, 16 * STEPS + 16)

            def load_kv(pool, g):
                b, feat = g // NHG, (g % NHG) * P
                for h in range(HG):
                    if not isinstance(g, int) or g:
                        pool.wait_ge(sc_ready, (g * NQ * UNITS - HG + h + 1) * NCH)
                        pool.sem_inc(pool_idle, 1)
                    for a in range(4):
                        pool.dma_start(kst[h][a * DH:(a + 1) * DH, :].bitcast(F32),
                                       scr.k[a % 2, ds(feat + h * DH, DH), ds(b * S, S)]).then_inc(k_loaded[h], 16)
                if not isinstance(g, int) or g:
                    pool.wait_ge(pv_half, g * NQ * 2 + 2)
                    pool.sem_inc(pool_idle, 1)
                pool.dma_start(vt[:], scr.v[ds(b * S, S), ds(feat, P)].rearrange("(t p) f -> p t f", p=P)).then_inc(v_loaded, 16)

            @block.gpsimd
            def _(pool):
                load_kv(pool, 0)
                pool.dma_start(expert[:], i.expert.rearrange("(a n) -> a n", a=1)).then_inc(e_loaded, 16)
                pool.wait_ge(e_loaded, 16)
                chosen = [pool.value_load(expert[0:1, b:b + 1], min_val=0, max_val=E - 1) for b in range(B)]
                wide = lambda ap: ap.rearrange("r (n c) -> (r n) c", c=D)
                experts_in, experts_out = i.Wi.rearrange("e r (n c) -> (e r n) c", c=D), i.We.rearrange("e r c -> (e r) c")
                ROWS = D * FF // D
                sources = [(wide(i.W1), None, scr.w1, 0), (i.W2, None, scr.w2, 0)]
                for b in range(B):
                    sources += [(experts_in, chosen[b], scr.wi, b), (experts_out, chosen[b], scr.we, b)]

                def eighth(g):
                    n = 0
                    PER = 2 * len(sources) + 1
                    jobs = [(src, pick, dst, b, part) for src, pick, dst, b in sources for part in range(2)]
                    jobs.append((i.Wo, None, scr.wo, 0, None))
                    for src, pick, dst, b, part in jobs:
                        rows = P if part is not None else D // NHG // B
                        at = g * 2 * P + part * P if part is not None else g * rows
                        frm = at if pick is None else pick * ROWS + at
                        done = g * PER + n
                        pool.dma_start(w32[0:rows], src[ds(frm, rows), :]).then_inc(w_loaded, 16)
                        pool.wait_ge(w_loaded, done * 16 + 16)
                        pool.sem_inc(pool_idle, 1)
                        nc.gpsimd.tensor_copy(whr[0:rows], w32[0:rows]).then_inc(w_high, 1)
                        pool.wait_ge(w_high, done + 1)
                        nc.gpsimd.tensor_tensor(wlr[0:rows], w32[0:rows], whr[0:rows].bitcast(F32), ALU.subtract).then_inc(w_low, 1)
                        pool.wait_ge(w_low, done + 1)
                        pool.sem_inc(pool_idle, 1)
                        to = b * ROWS + at if part is not None else at
                        for w, tile in enumerate((whr, wlr)):
                            pool.dma_start(dst[w][ds(to, rows), :], tile[0:rows].bitcast(F32)).then_inc(w_stored, 16)
                        pool.wait_ge(w_stored, done * 32 + 32)
                        pool.sem_inc(pool_idle, 1)
                        n += 1

                with pool.Fori(0, B * NHG - 1) as g:
                    eighth(g)
                    load_kv(pool, g + 1)
                eighth(B * NHG - 1)

            def reads(s, *what):
                n, before = place(*what)
                ahead = what[0] == "scores" and what[1] < LEAD
                return ring[n], bank_free[n], (s if ahead else s + 1) * fills[n] + before + 1

            def wait_bank(s, what):
                bank, free, count = reads(s, *what)
                nc.tensor.wait_ge(free, count)
                return bank

            def scores(s, u, c):
                t, h = u // HG, u % HG
                pe = nc.tensor
                if c == 0:
                    pe.wait_ge(qm_loaded[t], s * 80 + 80)
                    pe.wait_ge(k_loaded[h], (s // NQ) * 64 + 64)
                at = wait_bank(s, ("scores", u, c))
                cols = slice(c * 512, (c + 1) * 512)
                nc.tensor.matmul(at[:], qst[t][:, h, :], kst[h][:, cols], start=True, stop=False)
                nc.tensor.matmul(at[:], masked[:], mask[t][:, cols], start=False, stop=True).then_inc(sc_ready, 1)

            def turn(s, u, c):
                if c == 0:
                    nc.tensor.wait_ge(exp_done, s * UNITS + u + 1)
                src = planes(unit[u][:])
                for which in (1, 0):
                    at = wait_bank(s, (which, u, c))[:].bitcast(BF16)
                    for j in range(KH):
                        keys = slice((c * KH + j) * P, (c * KH + j + 1) * P)
                        last = nc.tensor.transpose(at[:, j * P:(j + 1) * P], src[:, keys, which], keep.eye_bf[:])
                    last.then_inc(turned[which], 1)

            def take(eng, copy, s, u, c, which):
                t, h = u // HG, u % HG
                eng.wait_ge(turned[which], s * 2 * UNITS + turns(which).index((which, u, c)) + 1)
                if u == 0:
                    eng.wait_ge(pv_half, s * 2 + c + 1)
                dst = probs_t[c][:, h, :, t * P:(t + 1) * P].bitcast(U16).rearrange("p k (q two) -> p k q two", two=2)[:, :, :, which]
                n, _ = place(which, u, c)
                copy(dst, ring[n][:].bitcast(U16).rearrange("p (k q) -> p k q", q=P)).then_inc(bank_free[n], 1)

            def take_high(s, u, c):
                take(nc.scalar, nc.scalar.copy, s, u, c, 1)
                if (u, c) in SHARED:
                    take(nc.scalar, nc.scalar.copy, s, u, c, 0)

            def take_low(s, u, c):
                if (u, c) not in SHARED:
                    take(nc.vector, nc.vector.tensor_copy, s, u, c, 0)

            def weigh(s, kt):
                pe = nc.tensor
                if kt == 0:
                    pe.wait_ge(v_loaded, (s // NQ) * 16 + 16)
                    pe.wait_ge(normed, s + 1)
                c = kt // KH
                if kt % KH == 0:
                    for n in range(RING):
                        what = [w for w, bank in zip(order, banks) if bank == n and w[0] != "scores" and w[2] == c]
                        if what:
                            _, free, count = reads(s, *what[-1])
                            pe.wait_ge(free, count + 1)
                for h in range(HG):
                    last = nc.tensor.matmul(ctx_ps[h * DH:(h + 1) * DH, :], vt[:, kt, h * DH:(h + 1) * DH], probs_t[c][:, h, kt % KH, :],
                                            start=(kt == 0), stop=(kt == KT - 1))
                if kt % KH == KH - 1:
                    last.then_inc(pv_half, 1)

            def turn_back(s):
                pe = nc.tensor
                pe.wait_ge(ctx_taken, s + 1)
                for t in range(2):
                    last = nc.tensor.transpose(back_ps[:, t, :], ctx_t[:, t * P:(t + 1) * P], keep.eye[:])
                last.then_inc(back_ready, 1)

            def chunk_max(s, u, c):
                dve = nc.vector
                if c == 0:
                    dve.wait_ge(bias_loaded[u], s * 16 + 16)
                dve.wait_ge(sc_ready, (s * UNITS + u) * NCH + c + 1)
                dve.sem_inc(idle, 1)
                cols = slice(c * 512, (c + 1) * 512)
                n, _ = place("scores", u, c)
                nc.vector.tensor_tensor_reduce(out=unit[u][:, cols], in0=ring[n][:], in1=unit[u][:, cols], scale=1.0, scalar=LOWEST,
                                               op0=ALU.add, op1=ALU.max, accum_out=part_max[:, u, c:c + 1]).then_inc(bank_free[n], 1)

            def unit_max(s, u):
                dve = nc.vector
                for c in range(NCH):
                    _, free, count = reads(s, "scores", u, c)
                    dve.wait_ge(free, count + 1)
                nc.vector.tensor_reduce(neg_max[:, u:u + 1], part_max[:, u, :], AX, ALU.max, negate=True).then_inc(max_ready, 1)

            def exponents(s, u):
                act = nc.scalar
                act.wait_ge(max_ready, s * UNITS + u + 1)
                if u == 0:
                    act.wait_ge(inv_ready, s + 1)
                nc.scalar.activation(unit[u][:], unit[u][:], ACT.Exp, bias=neg_max[:, u:u + 1], accum_out=total[:, u:u + 1]).then_inc(exp_done, 1)

            @block.tensor
            def _(pe):
                pe.wait_ge(masked_set, 1)

                def all_scores(s, u):
                    for c in range(NCH):
                        scores(s, u, c)

                def round_of(s, before, more):
                    kt = KH
                    for u in range(LEAD, UNITS):
                        for c in range(NCH):
                            scores(s, u, c)
                            while before is not None and kt < min(KT, KH + KH * ((u - LEAD) * NCH + c + 1) // PV_CHUNKS):
                                weigh(before, kt)
                                kt += 1
                        if u >= LAG:
                            turn(s, u - LAG, 0)
                    kt = 0
                    for n, (u, c) in enumerate(SECOND):
                        turn(s, u, c)
                        if n == 1 and before is not None:
                            turn_back(before)
                        while kt < KH * (n + 1 - PV_SKIP) // (len(SECOND) - PV_SKIP):
                            weigh(s, kt)
                            kt += 1
                        if c and u >= UNITS - LEAD:
                            if more:
                                all_scores(s + 1, u - UNITS + LEAD)
                            else:
                                for part in range(NCH):
                                    what = ("scores", u - UNITS + LEAD, part)
                                    wait_bank(s + 1, what)
                                    pe.sem_inc(bank_free[place(*what)[0]], 1)

                for u in range(LEAD):
                    all_scores(0, u)
                round_of(0, None, True)
                with pe.Fori(0, STEPS - 2) as s:
                    round_of(s + 1, s, True)
                round_of(STEPS - 1, STEPS - 2, False)
                for kt in range(KH, KT):
                    weigh(STEPS - 1, kt)
                turn_back(STEPS - 1)

            @block.scalar
            def _(act):
                for n in range(RING):
                    act.sem_inc(bank_free[n], fills[n] + 1 - led.count(n))
                act.sem_inc(pv_half, 2)

                def context(s):
                    act.wait_ge(pv_half, s * 2 + 4)
                    act.wait_ge(back_ready, s + 1)
                    nc.scalar.copy(ctx_t[:], ctx_ps).then_inc(ctx_taken, 1)

                def round_of(s, before, more):
                    for u in range(LEAD, UNITS):
                        if u == UNITS - 1 and before is not None:
                            context(before)
                        exponents(s, u - 1)
                        if u >= LAG:
                            take_high(s, u - LAG, 0)
                    exponents(s, UNITS - 1)
                    for u, c in SECOND:
                        take_high(s, u, c)
                        if c and u > UNITS - LEAD and more:
                            exponents(s + 1, u - UNITS + LEAD - 1)

                for u in range(LEAD - 1):
                    exponents(0, u)
                round_of(0, None, True)
                with act.Fori(0, STEPS - 2) as s:
                    round_of(s + 1, s, True)
                round_of(STEPS - 1, STEPS - 2, False)
                context(STEPS - 1)

            @block.vector
            def _(dve):
                nc.vector.tensor_scalar(masked[:], keep.eye[:], MASKED, None, ALU.mult).then_inc(masked_set, 1)
                dve.sem_inc(inv_ready, 1)
                dve.sem_inc(normed, 1)
                dve.sem_inc(back_ready, 1)
                dve.sem_inc(ctx_stored, 16)

                def normalise(s):
                    dve.wait_ge(inv_ready, s + 2)
                    dve.wait_ge(ctx_stored, s * 16 + 16)
                    dve.wait_ge(back_ready, s + 2)
                    nc.vector.tensor_tensor(ctx_out[:].rearrange("p t (h d) -> p (t h) d", d=DH), back_ps.rearrange("p t (h d) -> p (t h) d", d=DH),
                                            inv_total[:].unsqueeze(2).to_broadcast([P, UNITS, DH]), ALU.mult).then_inc(normed, 1)

                def invert(s):
                    dve.wait_ge(exp_done, s * UNITS + UNITS)
                    dve.wait_ge(normed, s + 1)
                    nc.vector.reciprocal(inv_total[:], total[:]).then_inc(inv_ready, 1)

                def maxima(s, u, since):
                    for c in range(NCH):
                        chunk_max(s, u, c)
                        if since is not None and c == 0:
                            unit_max(s, since)

                def round_of(s, before, more):
                    for u in range(LEAD, UNITS):
                        maxima(s, u, u - 1 if u > LEAD else None)
                        if u == UNITS - 1:
                            unit_max(s, u)
                        if u >= LAG:
                            take_low(s, u - LAG, 0)
                    for n, (u, c) in enumerate(SECOND):
                        take_low(s, u, c)
                        if n == 2 and before is not None:
                            normalise(before)
                        if n == 3:
                            invert(s)
                        if c and u >= UNITS - LEAD and more:
                            maxima(s + 1, u - UNITS + LEAD, None)
                            unit_max(s + 1, u - UNITS + LEAD)

                for u in range(LEAD):
                    maxima(0, u, None)
                    unit_max(0, u)
                round_of(0, None, True)
                with dve.Fori(0, STEPS - 2) as s:
                    round_of(s + 1, s, True)
                round_of(STEPS - 1, STEPS - 2, False)
                normalise(STEPS - 1)


def load_big(pool, k, keep, w1, w2, at, freed=None):
    for q in range(QUARTERS):
        if freed:
            freed(q, 0)
        for w in range(2):
            wide = w1[w][at:at + FF].rearrange("(c p n) x -> p c n x", p=P, n=FF // D)
            pool.dma_start(keep.w1[w][:, :, q * QF:(q + 1) * QF].bitcast(F32), wide[:, :, q, :]).then_inc(keep.w1_loaded[q], 16)
        if freed:
            freed(q, 1)
        for w in range(2):
            rows = w2[w][at + q * QF:at + (q + 1) * QF].rearrange("(f p) n -> p f n", p=P)
            pool.dma_start(keep.w2[w][:, q * QF // P:(q + 1) * QF // P, :].bitcast(F32), rows).then_inc(keep.w2_loaded[q], 16)


def mix(k, i, keep, scr):
    nc = k.nc
    with ExitStack() as ctx:
        sb = lambda *a: k.sb(ctx, *a)
        wo = [sb(f"wo{w}", [P, C, D], F32R) for w in range(2)]
        bo, g2, beta2 = sb("bo", [P, D]), sb("g2", [P, C]), sb("beta2", [P, C])
        ctx_in = sb("ctx_in", [P, GT, D])
        x2 = [sb(f"x2_in{t}", [P, D]) for t in range(GT)]
        ct = [sb(f"ctx_t{w}", [P, C, GTOK], F32R) for w in range(2)]
        x3, xn = sb("x3_mix", [P, GT, D]), sb("xn2", [P, GT, D])
        stats, mv = sb("stats2", [P, 6]), sb("mv2", [P, GT, 2])
        std, rstd = sb("std2", [P, GT]), sb("rstd2", [P, GT])
        t32 = [sb(f"t32_2{n}", [P, GTOK]) for n in range(2)]
        parts = [sb(f"h_parts{n}", [P, 2, GTOK], F32R) for n in range(2)]
        tp = [k.ps(ctx, f"mix_tp{n}", [P, 512]) for n in range(2)]
        hp = [k.ps(ctx, f"mix_hp{n}", [P, 512]) for n in range(2)]
        op = [k.ps(ctx, f"mix_op{n}", [P, D]) for n in range(GT)]
        consts_loaded, ctx_loaded = k.sem("mx_consts_loaded"), k.sem("mx_ctx_loaded")
        x2_loaded = [k.sem(f"mx_x2_loaded{t}") for t in range(GT)]
        ct_turned, ct_high, ct_low, wo_ready, x2_ready, x3_ready = (
            k.sem("mx_" + n) for n in ("ct_turned", "ct_high", "ct_low", "wo_ready", "x2_ready", "x3_ready"))
        own, var_ready, std_ready, xn_ready, xn_turned, t32_ready, h_high, h_low, idle = (
            k.sem("mx_" + n) for n in ("dve_chain", "var_ready", "std_ready", "xn_ready", "xn_turned", "t32_ready", "h_high", "h_low", "idle"))
        x3_stored, h_stored = k.sem("mx_x3_stored"), [k.sem(f"mx_h_stored{n}") for n in range(2)]
        row = lambda ap: ap.rearrange("(a n) -> a n", a=1)
        loads = [(wo[w][:].bitcast(F32), scr.wo[w].rearrange("(c p) n -> p c n", p=P)) for w in range(2)]
        loads += [(bo[:], row(i.bo).to_broadcast([P, D]))]
        loads += [(t[:], v.rearrange("(c p) -> p c", p=P)) for t, v in ((g2, i.g2), (beta2, i.beta2))]
        grouped = lambda ap: ap.rearrange("(g t p) d -> g p t d", t=GT, p=P)
        tile_of = lambda ap, g: grouped(ap)[ds(g, 1)].rearrange("a p t d -> p (a t) d")

        def load_x2(sp, g, t):
            sp.dma_start(x2[t][:], scr.x2[ds(g * GTOK + t * P, P), :]).then_inc(x2_loaded[t], 16)

        def store_x3(sp, g):
            sp.wait_ge(x3_ready, g * GT + GT)
            sp.dma_start(tile_of(scr.x3, g), x3[:]).then_inc(x3_stored, 16)

        def store_h(sp, g):
            for c in range(C):
                sp.wait_ge(h_low, g * C + c + 3)
                sp.dma_start(scr.ht[:, c * P:(c + 1) * P, ds(g * GTOK, GTOK)].rearrange("w f s -> f w s"),
                             parts[c % 2][:].bitcast(F32)).then_inc(h_stored[c % 2], 16)

        with nc.Block() as block:
            @block.sync
            def _(sp):
                sp.dma_start(ctx_in[:], tile_of(scr.ctx, 0)).then_inc(ctx_loaded, 16)
                for dst, src in loads:
                    sp.dma_start(dst, src, allow_slow_non_contiguous=True).then_inc(consts_loaded, 16)
                for t in range(GT):
                    load_x2(sp, 0, t)

                def after(sp, g, more):
                    if more:
                        sp.wait_ge(ct_turned, g * C + C)
                        sp.dma_start(ctx_in[:], tile_of(scr.ctx, g + 1)).then_inc(ctx_loaded, 16)
                        for t in range(GT):
                            sp.wait_ge(x3_ready, g * GT + t + 1)
                            load_x2(sp, g + 1, t)
                    store_x3(sp, g)
                after(sp, 0, True)
                with sp.Fori(1, NG - 1) as g:
                    store_h(sp, g - 1)
                    after(sp, g, True)
                store_h(sp, NG - 2)
                after(sp, NG - 1, False)
                store_h(sp, NG - 1)
                sp.wait_ge(x3_stored, 16 * NG + 16)
                for n in range(2):
                    sp.wait_ge(h_stored[n], 16 * NG * C // 2 + 16)

            @block.gpsimd
            def _(pool):
                load_big(pool, k, keep, scr.w1, scr.w2, 0)
                pool.wait_ge(consts_loaded, 16 * len(loads))
                with pool.Fori(0, NG) as g:
                    for t in range(GT):
                        pool.wait_ge(x2_loaded[t], g * 16 + 16)
                        nc.gpsimd.tensor_tensor(x2[t][:], x2[t][:], bo[:], ALU.add).then_inc(x2_ready, 1)

            @block.tensor
            def _(pe):
                mm = nc.tensor.matmul

                def turn_ctx(g):
                    pe.wait_ge(ctx_loaded, g * 16 + 16)
                    for c in range(C):
                        pe.wait_ge(ct_low, g * C + c + 1)
                        for t in range(GT):
                            last = nc.tensor.transpose(tp[c % 2][:, t * P:(t + 1) * P], ctx_in[:, t, c * P:(c + 1) * P], keep.eye[:])
                        last.then_inc(ct_turned, 1)

                def turn_h(g):
                    pe.wait_ge(xn_ready, g * GT + GT + 1)
                    for c in range(C):
                        pe.wait_ge(t32_ready, g * C + c + 1)
                        for t in range(GT):
                            last = nc.tensor.transpose(hp[c % 2][:, t * P:(t + 1) * P], xn[:, t, c * P:(c + 1) * P], keep.eye[:])
                        last.then_inc(xn_turned, 1)

                def product(g):
                    pe.wait_ge(ct_low, g * C + C + 2)
                    for t in range(GT):
                        pe.wait_ge(x3_ready, g * GT + t + 1 - GT) if not isinstance(g, int) or g else None
                        tok = slice(t * P, (t + 1) * P)
                        n = 0
                        for c in range(C):
                            for a, w in ((0, 0), (1, 0), (0, 1)):
                                n += 1
                                last = mm(op[t][:], ct[a][:, c, tok], wo[w][:, c, :], start=(n == 1), stop=(n == 3 * C))
                        last.then_inc(wo_ready, 1)

                pe.wait_ge(consts_loaded, 16 * len(loads))
                turn_ctx(0)
                product(0)
                with pe.Fori(1, NG) as g:
                    turn_ctx(g)
                    turn_h(g - 1)
                    product(g)
                turn_h(NG - 1)

            @block.scalar
            def _(act):
                act.sem_inc(t32_ready, 2)
                act.wait_ge(consts_loaded, 16 * len(loads))

                def high(g):
                    act.wait_ge(wo_ready, g * GT) if not isinstance(g, int) or g else None
                    for c in range(C):
                        act.wait_ge(ct_turned, g * C + c + 1)
                        nc.scalar.copy(ct[0][:, c, :], tp[c % 2][:]).then_inc(ct_high, 1)

                def affine(g):
                    for c in range(C):
                        act.wait_ge(xn_turned, g * C + c + 1)
                        act.wait_ge(h_low, g * C + c + 1)
                        nc.scalar.activation(t32[c % 2][:], hp[c % 2][:], ACT.Identity, scale=g2[:, c:c + 1], bias=beta2[:, c:c + 1]).then_inc(t32_ready, 1)

                def deviations(g):
                    for t in range(GT):
                        act.wait_ge(var_ready, g * GT + t + 1)
                        nc.scalar.activation(std[:, t:t + 1], mv[:, t, 1:2], ACT.Sqrt, bias=keep.eps5[:]).then_inc(std_ready, 1)

                high(0)
                deviations(0)
                with act.Fori(1, NG) as g:
                    high(g)
                    affine(g - 1)
                    deviations(g)
                affine(NG - 1)

            @block.vector
            def _(dve):
                dve.sem_inc(ct_low, 2)
                dve.sem_inc(h_low, 2)
                dve.sem_inc(xn_ready, 1)
                dve.sem_inc(x3_stored, 16)
                for n in range(2):
                    dve.sem_inc(h_stored[n], 16)

                def low(g):
                    for c in range(C):
                        dve.wait_ge(ct_high, g * C + c + 1)
                        nc.vector.tensor_tensor(ct[1][:, c, :], tp[c % 2][:], ct[0][:, c, :].bitcast(F32), ALU.subtract).then_inc(ct_low, 1)

                def split(g):
                    for c in range(C):
                        dve.wait_ge(t32_ready, g * C + c + 3)
                        dve.wait_ge(h_stored[c % 2], (g * C // 2 + c // 2) * 16 + 16)
                        nc.vector.tensor_copy(parts[c % 2][:, 0], t32[c % 2][:]).then_inc(h_high, 1)
                        dve.wait_ge(h_high, g * C + c + 1)
                        nc.vector.tensor_tensor(parts[c % 2][:, 1], t32[c % 2][:], parts[c % 2][:, 0].bitcast(F32), ALU.subtract).then_inc(h_low, 1)

                def normalise(g):
                    link = Link(dve, own, per=3 * GT, at=g)
                    dve.wait_ge(x3_stored, g * 16 + 16)
                    if not isinstance(g, int) or g:
                        dve.wait_ge(xn_turned, g * C)
                    for t in range(GT):
                        dve.wait_ge(wo_ready, g * GT + t + 1)
                        dve.wait_ge(x2_ready, g * GT + t + 1)
                        nc.vector.tensor_tensor(x3[:, t], op[t][:], x2[t][:], ALU.add).then_inc(x3_ready, 1)
                        dve.wait_ge(x3_ready, g * GT + t + 1)
                        link(nc.vector.bn_stats(stats[:], x3[:, t]))
                        dve.sem_inc(idle, 1)
                        nc.vector.bn_aggr(mv[:, t], stats[:]).then_inc(var_ready, 1)
                        dve.wait_ge(std_ready, g * GT + t + 1)
                        link(nc.vector.reciprocal(rstd[:, t:t + 1], std[:, t:t + 1]))
                        link(nc.vector.tensor_scalar(xn[:, t], x3[:, t], mv[:, t, 0:1], rstd[:, t:t + 1], ALU.subtract, ALU.mult))
                        dve.sem_inc(xn_ready, 1)

                low(0)
                normalise(0)
                with dve.Fori(1, NG) as g:
                    low(g)
                    split(g - 1)
                    normalise(g)
                split(NG - 1)


def turn(k, i, keep, scr):
    nc = k.nc
    with ExitStack() as ctx:
        x4 = [k.sb(ctx, f"x4_turn{n}", [P, GT, D]) for n in range(2)]
        parts = [k.sb(ctx, f"x4t_parts{n}", [P, 2, GTOK], F32R) for n in range(4)]
        tp = [k.ps(ctx, f"turn_tp{n}", [P, 512]) for n in range(4)]
        x_loaded, stored = ([k.sem(f"tu_{n}{j}") for j in range(m)] for n, m in (("x_loaded", 2), ("stored", 4)))
        turned, high, low = (k.sem("tu_" + n) for n in ("turned", "high", "low"))
        tile_of = lambda ap, g: ap.rearrange("(g t p) d -> g p t d", t=GT, p=P)[ds(g, 1)].rearrange("a p t d -> p (a t) d")

        with nc.Block() as block:
            @block.sync
            def _(sp):
                for n in range(2):
                    sp.dma_start(x4[n][:], tile_of(scr.x4, n)).then_inc(x_loaded[n], 16)

                def both(it, more):
                    for n in range(2):
                        g = it * 2 + n
                        for c in range(C):
                            sp.wait_ge(low, g * C + c + 1 + C)
                            if c == C - 1 and more:
                                sp.dma_start(x4[n][:], tile_of(scr.x4, g + 2)).then_inc(x_loaded[n], 16)
                            sp.dma_start(scr.ht[:, c * P:(c + 1) * P, ds(g * GTOK, GTOK)].rearrange("w f s -> f w s"),
                                         parts[c][:].bitcast(F32)).then_inc(stored[c], 16)
                with sp.Fori(0, NG // 2 - 1) as it:
                    both(it, True)
                both(NG // 2 - 1, False)
                for n in range(4):
                    sp.wait_ge(stored[n], 16 * NG + 16)

            @block.tensor
            def _(pe):
                with pe.Fori(0, NG // 2) as it:
                    for n in range(2):
                        g = it * 2 + n
                        pe.wait_ge(x_loaded[n], it * 16 + 16)
                        for c in range(C):
                            pe.wait_ge(low, g * C + c + 1)
                            for t in range(GT):
                                last = nc.tensor.transpose(tp[c][:, t * P:(t + 1) * P], x4[n][:, t, c * P:(c + 1) * P], keep.eye[:])
                            last.then_inc(turned, 1)

            @block.scalar
            def _(act):
                for c in range(C):
                    act.sem_inc(stored[c], 16)
                with act.Fori(0, NG) as g:
                    for c in range(C):
                        act.wait_ge(turned, g * C + c + 1)
                        act.wait_ge(stored[c], g * 16 + 16)
                        nc.scalar.copy(parts[c][:, 0], tp[c][:]).then_inc(high, 1)

            @block.vector
            def _(dve):
                dve.sem_inc(low, C)
                with dve.Fori(0, NG) as g:
                    for c in range(C):
                        dve.wait_ge(high, g * C + c + 1)
                        nc.vector.tensor_tensor(parts[c][:, 1], tp[c][:], parts[c][:, 0].bitcast(F32), ALU.subtract).then_inc(low, 1)


def feed(k, i, keep, scr, out, experts):
    nc = k.nc
    tag = "ex_" if experts else "fd_"
    with ExitStack() as ctx:
        sb = lambda n, *a: k.sb(ctx, tag + n, *a)
        sem = lambda n: k.sem(tag + n)
        NV = B if experts else 1
        ht = [[sb(f"ht{n}{w}", [P, C, GTOK], F32R) for w in range(2)] for n in range(2)]
        b_in, b_out = sb("b_in", [P, NV, FC]), sb("b_out", [P, NV, D])
        gate_b = sb("gate_b", [P, FC])
        sig = [sb(f"sig{n}", [P, GTOK]) for n in range(2)]
        hid32 = sig if experts else [sb(f"hid32{n}", [P, GTOK]) for n in range(2)]
        hid = [[sb(f"hid{n}{w}", [P, GTOK], F32R) for w in range(2)] for n in range(2)]
        res, o_t = sb("res", [P, GT, D]), sb("o_t", [P, GT, D])
        if experts:
            gamma, beta = sb("gamma", [P, NV, D]), sb("beta", [P, NV, D])
            chosen_t = sb("chosen", [1, B], I32)
            stats, mv = sb("stats", [P, 6]), sb("mv", [P, GT, 2])
            std, rstd, eps12 = sb("std", [P, GT]), sb("rstd", [P, GT]), sb("eps12", [P, 1])
        fp = [k.ps(ctx, f"{tag}fp{n}", [P, GTOK]) for n in range(2)]
        acc = [k.ps(ctx, f"{tag}acc{n}", [P, D]) for n in range(GT)]

        vec_loaded, e_loaded, h_loaded = sem("vec_loaded"), sem("e_loaded"), [sem(f"h_loaded{n}") for n in range(2)]
        res_loaded, res_ready, hid_ready, gate_ready, fp_taken, h32_ready, hid_high, hid_low, second_done = (
            sem(n) for n in ("res_loaded", "res_ready", "hid_ready", "gate_ready", "fp_taken", "h32_ready", "hid_high", "hid_low", "second_done"))
        acc_ready, acc_taken, out_ready, out_stored, own, pool_own, var_ready, std_ready, y_ready, idle, set_up = (
            sem(n) for n in ("acc_ready", "acc_taken", "out_ready", "out_stored", "dve_chain", "pool_chain", "var_ready", "std_ready", "y_ready", "idle", "set_up"))
        act_idle, idle_v, r_ready = sem("act_idle"), sem("dve_idle"), sem("r_ready")
        tile_of = lambda ap, g: ap.rearrange("(g t p) d -> g p t d", t=GT, p=P)[ds(g, 1)].rearrange("a p t d -> p (a t) d")
        row = lambda ap: ap.rearrange("(a n) -> a n", a=1)
        source, dest = (scr.x4, out.rearrange("b s d -> (b s) d")) if experts else (scr.x3, scr.x4)
        N_VEC = 4 * B if experts else 2

        def load_h(sp, g, n):
            for w in range(2):
                sp.dma_start(ht[n][w][:].bitcast(F32), scr.ht[w].rearrange("(c p) n -> p c n", p=P)[:, :, ds(g * GTOK, GTOK)]).then_inc(h_loaded[n], 16)

        def over_pairs(eng, body):
            with eng.Fori(0, NG // 2 - 1) as it:
                for n in range(2):
                    body(it * 2 + n, n, True)
            for n in range(2):
                body(NG - 2 + n, n, n == 0)

        with nc.Block() as block:
            @block.sync
            def _(sp):
                if experts:
                    sp.dma_start(chosen_t[:], row(i.expert)).then_inc(e_loaded, 16)
                    sp.wait_ge(e_loaded, 16)
                    for b in range(B):
                        e = sp.value_load(chosen_t[0:1, b:b + 1], min_val=0, max_val=E - 1)
                        sp.dma_start(b_in[:, b], i.bi[ds(e, 1)].rearrange("a (f p) -> p (a f)", p=P), allow_slow_non_contiguous=True).then_inc(vec_loaded, 16)
                        for t, v in ((b_out, i.be), (gamma, i.gamma), (beta, i.beta)):
                            sp.dma_start(t[:, b], v[ds(e, 1)].to_broadcast([P, D])).then_inc(vec_loaded, 16)
                else:
                    sp.dma_start(b_in[:, 0], i.b1.rearrange("(f p) -> p f", p=P), allow_slow_non_contiguous=True).then_inc(vec_loaded, 16)
                    sp.dma_start(b_out[:, 0], row(i.b2).to_broadcast([P, D])).then_inc(vec_loaded, 16)
                load_h(sp, 0, 0)
                sp.dma_start(res[:], tile_of(source, 0)).then_inc(res_loaded, 16)

                def body(g, n, more):
                    if more:
                        sp.wait_ge(hid_ready, g * FC + 1)
                        load_h(sp, g + 1, 1 - n)
                    sp.wait_ge(acc_taken, g * GT + 2 * GT)
                    if more:
                        sp.dma_start(res[:], tile_of(source, g + 1)).then_inc(res_loaded, 16)
                    sp.wait_ge(out_ready, g * GT + GT)
                    sp.dma_start(tile_of(dest, g), o_t[:]).then_inc(out_stored, 16)
                over_pairs(sp, body)
                sp.wait_ge(out_stored, 16 * NG + 16)

            @block.gpsimd
            def _(pool):
                pool.wait_ge(vec_loaded, 16 * N_VEC)

                def residual(g):
                    pool.wait_ge(res_loaded, g * 16 + 16)
                    pool.sem_inc(idle, 1)
                    bias = b_out[:, ds(g // GB, 1), :] if experts else b_out[:]
                    nc.gpsimd.tensor_tensor(res[:], res[:], bias.to_broadcast([P, GT, D]), ALU.add).then_inc(res_ready, 1)

                def finish(g):
                    for t in range(GT):
                        pool.wait_ge(y_ready, g * GT + t + 1)
                        pool.sem_inc(idle, 1)
                        nc.gpsimd.tensor_tensor(o_t[:, t:t + 1], o_t[:, t:t + 1], gamma[:, ds(g // GB, 1), :], ALU.mult).then_inc(pool_own, 1)
                        pool.wait_ge(pool_own, g * GT + t + 1)
                        pool.sem_inc(idle, 1)
                        nc.gpsimd.tensor_tensor(o_t[:, t:t + 1], o_t[:, t:t + 1], beta[:, ds(g // GB, 1), :], ALU.add).then_inc(out_ready, 1)

                def freed(done):
                    def wait(q, which):
                        if which == 0:
                            pool.wait_ge(hid_ready, (done - 1) * FC + (q + 1) * FC // QUARTERS)
                        else:
                            pool.wait_ge(second_done, (done - 1) * FC + (q + 1) * FC // QUARTERS + 2)
                    return wait
                residual(0)
                if experts:
                    with pool.Fori(0, GB - 1) as g:
                        finish(g)
                        residual(g + 1)
                    load_big(pool, k, keep, scr.wi, scr.we, FF, freed(GB))
                    with pool.Fori(GB - 1, NG - 1) as g:
                        finish(g)
                        residual(g + 1)
                    finish(NG - 1)
                else:
                    with pool.Fori(1, NG) as g:
                        residual(g)
                    load_big(pool, k, keep, scr.wi, scr.we, 0, freed(NG))

            @block.tensor
            def _(pe):
                mm = nc.tensor.matmul
                loaded = lambda g: (g // GB * 32 + 64) if experts else 32

                def first(g, n, fc):
                    q = fc * P // QF
                    if fc == 0:
                        pe.wait_ge(h_loaded[n], (g // 2) * 32 + 32)
                    if fc % (QF // P) == 0:
                        pe.wait_ge(keep.w1_loaded[q], loaded(g))
                    pe.wait_ge(fp_taken, g * FC + fc + 1)
                    m = 0
                    for c in range(C):
                        for a, w in ((0, 0), (1, 0), (0, 1)):
                            m += 1
                            last = mm(fp[fc % 2][:], keep.w1[w][:, c, fc * P:(fc + 1) * P], ht[n][a][:, c, :], start=(m == 1), stop=(m == 3 * C))
                    last.then_inc(hid_ready, 1)

                def second(g, fc):
                    if fc % (QF // P) == 0:
                        pe.wait_ge(keep.w2_loaded[fc * P // QF], loaded(g))
                    pe.wait_ge(hid_low, g * FC + fc + 3)
                    for t in range(GT):
                        if fc == 0:
                            pe.wait_ge(acc_taken, g * GT + t + 1)
                        tok = slice(t * P, (t + 1) * P)
                        for m, (a, w) in enumerate(((0, 0), (1, 0), (0, 1))):
                            last = mm(acc[t][:], hid[fc % 2][a][:, tok], keep.w2[w][:, fc, :],
                                      start=(fc == 0 and m == 0), stop=(fc == FC - 1 and m == 2))
                        if fc == FC - 1:
                            last.then_inc(acc_ready, 1)
                        elif t == GT - 1:
                            last.then_inc(second_done, 1)
                    if fc == FC - 1:
                        pe.wait_ge(acc_ready, g * GT + GT)
                        pe.sem_inc(second_done, 1)

                def body(g, n, more):
                    for fc in range(FC):
                        if fc < FC - 1:
                            first(g, n, fc + 1)
                        elif more:
                            first(g + 1, 1 - n, 0)
                        second(g, fc)
                first(0, 0, 0)
                over_pairs(pe, body)

            @block.scalar
            def _(act):
                act.wait_ge(vec_loaded, 16 * N_VEC)
                if not experts:
                    act.wait_ge(set_up, 1)

                def activate(g, n, fc):
                    act.wait_ge(hid_ready, g * FC + fc + 1)
                    if experts:
                        act.wait_ge(hid_low, g * FC + fc + 1)
                        act.sem_inc(act_idle, 1)
                        nc.scalar.activation(sig[fc % 2][:], fp[fc % 2][:], ACT.Gelu,
                                             bias=b_in[:].rearrange("p v f -> p (v f)")[:, ds(g // GB * FC + fc, 1)]).then_inc(fp_taken, 1)
                    else:
                        act.wait_ge(fp_taken, g * FC + fc + 1)
                        nc.scalar.activation(sig[fc % 2][:], fp[fc % 2][:], ACT.Sigmoid, scale=1.702, bias=gate_b[:, fc:fc + 1]).then_inc(gate_ready, 1)

                def body(g, n, more):
                    for fc in range(FC):
                        if fc < FC - 1:
                            activate(g, n, fc + 1)
                        elif more:
                            activate(g + 1, 1 - n, 0)
                    if experts:
                        act.wait_ge(var_ready, g + 1)
                        nc.scalar.activation(std[:], mv[:, :, 1], ACT.Sqrt, bias=eps12[:]).then_inc(std_ready, 1)
                activate(0, 0, 0)
                over_pairs(act, body)

            @block.vector
            def _(dve):
                dve.sem_inc(fp_taken, 2)
                dve.sem_inc(hid_low, 2)
                dve.sem_inc(second_done, 2)
                dve.sem_inc(acc_taken, GT)
                dve.sem_inc(out_stored, 16)
                if experts:
                    nc.vector.memset(eps12[:], 1e-12).then_inc(set_up, 1)
                else:
                    dve.wait_ge(vec_loaded, 16 * N_VEC)
                    nc.vector.tensor_scalar(gate_b[:], b_in[:, 0], 1.702, None, ALU.mult).then_inc(set_up, 1)

                def split(g, n, fc):
                    chunk = g * FC + fc
                    if experts:
                        dve.wait_ge(fp_taken, chunk + 3)
                    else:
                        dve.wait_ge(hid_low, chunk + 1)
                        dve.wait_ge(gate_ready, chunk + 1)
                        nc.vector.scalar_tensor_tensor(hid32[fc % 2][:], fp[fc % 2][:], b_in[:, 0, fc:fc + 1], sig[fc % 2][:], ALU.add, ALU.mult).then_inc(fp_taken, 1)
                        dve.wait_ge(fp_taken, chunk + 3)
                    dve.wait_ge(second_done, chunk + 1)
                    nc.vector.tensor_copy(hid[fc % 2][0][:], hid32[fc % 2][:]).then_inc(hid_high, 1)
                    dve.wait_ge(hid_high, chunk + 1)
                    nc.vector.tensor_tensor(hid[fc % 2][1][:], hid32[fc % 2][:], hid[fc % 2][0][:].bitcast(F32), ALU.subtract).then_inc(hid_low, 1)

                def epilogue(g):
                    dve.wait_ge(res_ready, g + 1)
                    dve.wait_ge(out_stored, g * 16 + 16)
                    for t in range(GT):
                        dve.wait_ge(acc_ready, g * GT + t + 1)
                        sum_ = nc.vector.tensor_tensor(o_t[:, t], acc[t][:], res[:, t], ALU.add)
                        sum_.then_inc(acc_taken, 1)
                        if not experts:
                            dve.wait_ge(acc_taken, g * GT + GT + t + 1)
                            dve.sem_inc(out_ready, 1)
                    if experts:
                        link = Link(dve, own, per=2 * GT, at=g)
                        for t in range(GT):
                            dve.wait_ge(acc_taken, g * GT + GT + t + 1)
                            link(nc.vector.bn_stats(stats[:], o_t[:, t]))
                            dve.sem_inc(idle_v, 1)
                            link(nc.vector.bn_aggr(mv[:, t], stats[:]))
                        dve.sem_inc(var_ready, 1)
                        dve.wait_ge(std_ready, g + 1)
                        nc.vector.reciprocal(rstd[:], std[:]).then_inc(r_ready, 1)
                        dve.wait_ge(r_ready, g + 1)
                        for t in range(GT):
                            nc.vector.tensor_scalar(o_t[:, t], o_t[:, t], mv[:, t, 0:1], rstd[:, t:t + 1], ALU.subtract, ALU.mult).then_inc(y_ready, 1)

                def body(g, n, more):
                    for fc in range(FC):
                        if fc < FC - 1:
                            split(g, n, fc + 1)
                        elif more:
                            split(g + 1, 1 - n, 0)
                    epilogue(g)
                split(0, 0, 0)
                over_pairs(dve, body)


class Names:
    pass


def program(nc, i, out):
    with ExitStack() as outer:
        k = Core(nc)
        scr = Names()
        scr.x2 = k.dram("x2_dram", [TOK, D])
        scr.x2t = k.dram("x2t_dram", [2, D, TOK])
        scr.q = k.dram("q_dram", [2, D, TOK])
        scr.k = k.dram("k_dram", [2, D, TOK])
        scr.v = k.dram("v_dram", [TOK, D])
        scr.mask = k.dram("mask_dram", [TOK, S], BF16)
        scr.ctx = k.dram("ctx_dram", [TOK, D])
        scr.x3 = k.dram("x3_dram", [TOK, D])
        scr.x4 = k.dram("x4_dram", [TOK, D])
        scr.ht = k.dram("ht_dram", [2, D, TOK])
        scr.wo = k.dram("wo_parts", [2, D, D])
        scr.w1 = k.dram("w1_parts", [2, FF, D])
        scr.w2 = k.dram("w2_parts", [2, FF, D])
        scr.wi = k.dram("wi_parts", [2, B * FF, D])
        scr.we = k.dram("we_parts", [2, B * FF, D])
        keep = Names()
        keep.eye = k.sb(outer, "eye", [P, P])
        keep.eye_bf = k.sb(outer, "eye_bf", [P, P], BF16)
        keep.eps5 = k.sb(outer, "eps5", [P, 1])
        with ExitStack() as front:
            sb = lambda *a: k.sb(front, *a)
            keep.basis = sb("basis", [P, C, 2, R])
            keep.ada = sb("ada", [P, 2 * C, B])
            keep.ada_row = sb("ada_row", [P, B, 2, D])
            keep.g33 = sb("g33_rot", [R + 1, B, D])
            keep.rot = sb("rot", [P, B, P])
            keep.y33 = sb("y33", [R + 1, GTOK])
            keep.bq, keep.bk, keep.bv = sb("bq", [P, C]), sb("bk", [P, C]), sb("bv", [P, D])
            keep.w_hi = sb("w_hi", [P, 3, C, D], F32R)
            keep.w_lo = sb("w_lo", [P, 3, C, D], F32R)
            constants(k, i, keep)
            k.pass_done()
            embed(k, i, keep, scr)
            k.pass_done()
            project(k, i, keep, scr)
            k.pass_done()
        attend(k, i, keep, scr)
        k.pass_done()
        with ExitStack() as back:
            keep.w1 = [k.sb(back, f"w1_{w}", [P, C, FF], F32R) for w in range(2)]
            keep.w2 = [k.sb(back, f"w2_{w}", [P, FC, D], F32R) for w in range(2)]
            keep.w1_loaded = [nc.alloc_semaphore(name=f"w1_loaded{q}") for q in range(QUARTERS)]
            keep.w2_loaded = [nc.alloc_semaphore(name=f"w2_loaded{q}") for q in range(QUARTERS)]
            mix(k, i, keep, scr)
            k.pass_done()
            feed(k, i, keep, scr, out, experts=False)
            k.pass_done()
            turn(k, i, keep, scr)
            k.pass_done()
            feed(k, i, keep, scr, out, experts=True)


INPUTS = {"x": "x", "score": "condB_safetyscore", "theta": "condB_theta", "phi": "condB_phi",
    "step": "itok_B_34_63", "bias": "fside_Bx16xSxS_0", "expert": "itok_B_0_7", "mask": "mask_Bx1xSxS_bk0",
    "U": "L0_cond_U", "V": "L0_cond_V", "safety_bias": "L0_cond_safety_bias", "gate_w1": "L0_cond_gate_w1",
    "gate_b1": "L0_cond_gate_b1", "gate_w2": "L0_cond_gate_w2", "gate_b2": "L0_cond_gate_b2",
    "resp_w": "L0_cond_resp_w", "resp_b": "L0_cond_resp_b", "W_ada": "L2_cond_W_ada", "b_ada": "L2_cond_b_ada",
    "Wq": "L2_cond_Wq", "bq": "L2_cond_bq", "Wk": "L2_cond_Wk", "bk": "L2_cond_bk", "Wv": "L2_cond_Wv",
    "bv": "L2_cond_bv", "Wo": "L2_cond_Wo", "bo": "L2_cond_bo", "W1": "L2_cond_W1", "b1": "L2_cond_b1",
    "W2": "L2_cond_W2", "b2": "L2_cond_b2", "g2": "L2_cond_g2", "beta2": "L2_cond_beta2", "Wi": "L3_cond_Wi",
    "bi": "L3_cond_bi", "We": "L3_cond_Wo", "be": "L3_cond_bo", "gamma": "L3_cond_gamma",
    "beta": "L3_cond_beta"}


def kernel(**inputs):
    import numpy as np
    import concourse.bacc as bacc
    from concourse.bass_utils import run_bass_kernel_spmd

    nc = bacc.Bacc("TRN2", target_bir_lowering=False, num_devices=1)
    arrays = {short: np.ascontiguousarray(inputs[name]) for short, name in INPUTS.items()}
    arrays["mask"] = arrays["mask"].view(np.int32)
    arrays["freq"] = np.exp(np.arange(D // 2, dtype=np.float32) * np.float32(-np.log(10000.0) / (D // 2 - 1)))
    i = Names()
    for short, a in arrays.items():
        i.__dict__[short] = nc.dram_tensor(f"in_{short}", a.shape, mybir.dt.from_np(a.dtype), kind="ExternalInput").ap()
    out = nc.dram_tensor("out", (B, S, D), F32, kind="ExternalOutput").ap()
    program(nc, i, out)
    r = run_bass_kernel_spmd(nc, [{f"in_{short}": a for short, a in arrays.items()}], core_ids=[0])
    return r.results[0]["out"]
```

```python
from contextlib import ExitStack

import concourse.bass as bass
from concourse import mybir

F32 = mybir.dt.float32
F32R = mybir.dt.float32r
BF16 = mybir.dt.bfloat16
U16 = mybir.dt.uint16
U8 = mybir.dt.uint8
I32 = mybir.dt.int32
ACT = mybir.ActivationFunctionType
ALU = mybir.AluOpType
AX = mybir.AxisListType.X
ds = bass.ds

P = 128
B, S, D = 2, 2048, 512
H, DH = 16, 32
R = 32
FF = 2048
E = 8
TOK = B * S
C = D // P
GT = 4
GTOK = GT * P
NG = TOK // GTOK
GB = NG // B
FC = FF // P
QUARTERS = 4
QF = FF // QUARTERS
HG = 4
NHG = H // HG
QB = 256
NQ = S // QB
STEPS = B * NHG * NQ
KT = S // P
PI = 3.141592653589793
TWO_PI_A, TWO_PI_B, TWO_PI_C = 6.28125, 0.0019350051879882812, 3.019916050561733e-07
ROUND = 12582912.0
MASKED = -1.0e30
LOWEST = -3.0e38


class Link:

    def __init__(self, eng, sem, base=0, per=None, at=None):
        self.eng, self.sem, self.n = eng, sem, 0
        self.start = base if at is None else at * per + base

    def __call__(self, ins):
        self.n += 1
        ins.then_inc(self.sem, 1)
        self.eng.wait_ge(self.sem, self.start + self.n)


def planes(ap):
    return ap.bitcast(BF16).rearrange("p (n two) -> p n two", two=2)


class Core:

    def __init__(self, nc):
        self.nc, self.sems = nc, []

    def sem(self, name):
        self.sems.append(self.nc.alloc_semaphore(name=name))
        return self.sems[-1]

    def pass_done(self):
        self.nc.clear_and_free_semaphores(self.sems)
        self.nc.all_engine_barrier()
        self.sems = []

    def sb(self, ctx, name, shape, dt=F32):
        return ctx.enter_context(self.nc.sbuf_tensor(name, shape, dt))

    def ps(self, ctx, name, shape, dt=F32):
        return ctx.enter_context(self.nc.psum_tensor(name, shape, dt))

    def dram(self, name, shape, dt=F32):
        return self.nc.dram_tensor(name, shape, dt, kind="Internal").ap()


def constants(k, i, keep, scr):
    nc = k.nc
    with ExitStack() as ctx:
        sb = lambda *a: k.sb(ctx, *a)
        basis = [keep.basis, sb("basis_odd", [P, C, 2, R])]
        norm2_mask = sb("step_mask", [P, 64])
        resp_w = sb("resp_w", [P, C, R])
        resp_row = sb("resp_row", [33, 512])
        safety_row = sb("safety_row", [33, 512])
        mean_w = sb("mean_w", [P, P])
        ones = sb("ones", [P, P])
        gate_w1 = sb("gate_w1", [P, D])
        gate_b1 = sb("gate_b1", [P, 1])
        gate_w2 = sb("gate_w2", [P, 1])
        gate_b2 = sb("gate_b2", [P, 1])
        score = sb("score", [P, B])
        step_i = sb("step_i", [P, B], I32)
        step_f = sb("step_f", [P, B])
        freq = sb("freq", [P, 2])
        w_ada = sb("w_ada", [P, C, 2 * D])
        b_ada_t = sb("b_ada_t", [P, 2 * C])
        b_ada_bc = sb("b_ada_bc", [P, 2 * D])
        x_in = sb("x_mean", [P, 2, D])
        zeros = sb("zeros", [P, D])
        angle = sb("angle", [P, 16])
        turns = sb("turns", [P, 16])
        shift_t = sb("shift_t", [P, 16])
        shift_a = sb("shift_a", [P, 16])
        sincos = sb("sincos", [P, 16])
        sig = sb("sig", [P, 2 * C])
        z = sb("z", [P, C, B])
        rot_c = sb("rot_c", [P, B, 2, 4])
        nrm = sb("nrm", [P, 2, 2])
        rr = sb("rr", [P, 2])
        prods = sb("prods", [P, C, 2, R])
        dots = sb("dots", [P, 2, R])
        coef = sb("coef", [P, 2, R - 1])
        coef2 = sb("coef2", [P, 2, R - 1])
        outer_p = sb("outer_p", [P, C, 2, R - 1])
        vtv = sb("vtv", [R, R])
        resp_t = sb("resp_t", [R, D])
        a1 = sb("a1", [R, D])
        g33 = sb("g33", [R + 1, D])
        g33s = sb("g33s", [R + 1, D])
        gtmp = sb("gtmp", [R + 1, D])
        eye_s = sb("eye_s", [P, P])
        eye_c = sb("eye_c", [P, P])
        prod = sb("prod", [P, D])
        h1 = sb("h1", [P, B])
        h1r = sb("h1r", [P, B])
        base_act = sb("base_act", [P, B])
        mod = sb("mod", [P, B])
        strength = sb("strength", [P, B])
        wraw = sb("wraw", [P, C, D])
        pool_mean = [k.ps(ctx, f"mean_ps{b}", [P, D]) for b in range(B)]
        coef_ps = [k.ps(ctx, f"coef_ps{n}", [P, 2, R]) for n in range(2)]
        small_ps = k.ps(ctx, "small_ps", [P, 512])
        ada_ps = k.ps(ctx, "ada_ps", [P, 2 * C, B])
        row_ps = [k.ps(ctx, f"row_ps{n}", [P, 512]) for n in range(2)]

        mask_in = [sb(f"mask_in{n}", [P, S // 4], I32) for n in range(2)]
        mask_bf = [sb(f"mask_bf{n}", [P, S], BF16) for n in range(2)]
        m_loaded, m_stored = ([k.sem(f"{n}{j}") for j in range(2)] for n in ("m_loaded", "m_stored"))
        m_cast = k.sem("m_cast")
        small_loaded, x_loaded = k.sem("small_loaded"), [k.sem(f"x_loaded{n}") for n in range(2)]
        eye_ready, eye_wiped = k.sem("eye_ready"), k.sem("eye_wiped")
        consts_set, mean_tiles, means_ready = k.sem("consts_set"), k.sem("mean_tiles"), k.sem("means_ready")
        basis_ready, coef_ready, nrm_ready = k.sem("basis_ready"), k.sem("coef_ready"), k.sem("nrm_ready")
        own = k.sem("dve_chain")
        angles_ready, sincos_ready, z_ready = (k.sem(n) for n in ("angles_ready", "sincos_ready", "z_ready"))
        h1_ready, gate_ps_ready, gate_ready = k.sem("h1_ready"), k.sem("gate_ps_ready"), k.sem("gate_ready")
        ada_ps_ready, row_ready, row_taken = k.sem("ada_ps_ready"), k.sem("row_ready"), k.sem("row_taken")
        vtv_ready, vtv_taken, respt_ready, respt_taken = (k.sem(n) for n in ("vtv_ready", "vtv_taken", "respt_ready", "respt_taken"))
        a1_ready, a1_taken, g_ready = k.sem("a1_ready"), k.sem("a1_taken"), k.sem("g_ready")
        w_loaded, w_split, w_low = k.sem("w_loaded"), k.sem("w_split"), k.sem("w_low")

        row = lambda ap: ap.rearrange("(a n) -> a n", a=1)
        bc = lambda ap, n: row(ap).to_broadcast([P, n])
        loads = [
            (basis[0][:, :, 0, :], i.U.rearrange("(c p) r -> p c r", p=P)),
            (basis[0][:, :, 1, :], i.V.rearrange("(c p) r -> p c r", p=P)),
            (resp_w[:], i.resp_w.rearrange("(c p) r -> p c r", p=P)),
            (resp_row[R:R + 1, :], row(i.resp_b)),
            (safety_row[R:R + 1, :], row(i.safety_bias)),
            (gate_w1[:], i.gate_w1),
            (gate_b1[:], i.gate_b1.rearrange("(n a) -> n a", a=1)),
            (gate_w2[:], i.gate_w2.rearrange("a n -> n a")),
            (gate_b2[:], bc(i.gate_b2, 1)),
            (score[:], bc(i.score, B)),
            (step_i[:], bc(i.step, B)),
            (freq[:], i.freq.rearrange("(c p) -> p c", p=P)),
            (angle[:, 0:2], bc(i.theta, B)),
            (angle[:, 2:4], bc(i.phi, B)),
            (w_ada[:], i.W_ada.rearrange("(c p) n -> p c n", p=P)),
            (b_ada_t[:], i.b_ada.rearrange("(f p) -> p f", p=P)),
            (b_ada_bc[:], bc(i.b_ada, 2 * D)),
            (keep.bq[:], i.bq.rearrange("(m p) -> p m", p=P)),
            (keep.bk[:], i.bk.rearrange("(m p) -> p m", p=P)),
            (keep.bv[:], bc(i.bv, D)),
        ]

        with nc.Block() as block:
            @block.sync
            def _(sp):
                for dst, src in loads:
                    sp.dma_start(dst, src, allow_slow_non_contiguous=True).then_inc(small_loaded, 16)
                x_rows = i.x.rearrange("b s d -> (b s) d")

                def x_load(n, at):
                    sp.dma_start(x_in[:, n], x_rows[ds(at * P, P), :]).then_inc(x_loaded[n], 16)
                mask_rows = i.mask.rearrange("b a q s -> (b a q) s")

                def mask_load(n, at):
                    sp.dma_start(mask_in[n][:], mask_rows[ds(at * P, P), :]).then_inc(m_loaded[n], 16)

                def mask_store(it, n):
                    sp.wait_ge(m_cast, it * 2 + n + 1)
                    sp.dma_start(scr.mask[ds((it * 2 + n) * P, P), :], mask_bf[n][:]).then_inc(m_stored[n], 16)
                for n in range(2):
                    x_load(n, n)
                    mask_load(n, n)
                with sp.Fori(0, R // 2 - 1) as it:
                    for n in range(2):
                        sp.wait_ge(mean_tiles, it * 2 + n + 1)
                        x_load(n, it * 2 + n + 2)
                        mask_store(it, n)
                        mask_load(n, it * 2 + n + 2)
                for n in range(2):
                    mask_store(R // 2 - 1, n)
                for n in range(2):
                    sp.wait_ge(m_stored[n], 16 + 16 * (R // 2))

            @block.gpsimd
            def _(pool):
                nc.gpsimd.memset(keep.eye[:], 0.0).then_inc(eye_wiped, 1)
                pool.wait_ge(eye_wiped, 1)
                nc.gpsimd.affine_select(out=keep.eye[:], in_=keep.eye[:], compare_op=ALU.not_equal, fill=1.0,
                                        base=0, pattern=[[-1, P]], channel_multiplier=1).then_inc(eye_ready, 1)
                for n, src in enumerate((i.Wq, i.Wk, i.Wv)):
                    if n:
                        pool.wait_ge(w_low, n)
                    pool.dma_start(wraw[:], src.rearrange("(c p) n -> p c n", p=P)).then_inc(w_loaded, 16)
                    pool.wait_ge(w_loaded, 16 * (n + 1))
                    nc.gpsimd.tensor_copy(keep.w_hi[:, n], wraw[:]).then_inc(w_split, 1)
                    pool.wait_ge(w_split, n + 1)
                    nc.gpsimd.tensor_tensor(keep.w_lo[:, n], wraw[:], keep.w_hi[:, n].bitcast(F32), ALU.subtract).then_inc(w_low, 1)

            @block.vector
            def _(dve):
                link = Link(dve, own)
                nc.vector.memset(mean_w[:], 1.0 / S).then_inc(consts_set, 1)
                nc.vector.memset(zeros[:], 0.0).then_inc(consts_set, 1)
                nc.vector.memset(ones[:], 1.0).then_inc(consts_set, 1)
                nc.vector.memset(norm2_mask[:, 0:32], 1.0).then_inc(consts_set, 1)
                nc.vector.memset(norm2_mask[:, 32:64], 0.0).then_inc(consts_set, 1)
                nc.vector.memset(keep.eps5[:], 1e-5).then_inc(consts_set, 1)
                nc.vector.memset(keep.y33[R:R + 1, :], 1.0).then_inc(consts_set, 1)
                link(nc.vector.memset(shift_t[:, 0:8], 0.0))
                link(nc.vector.memset(shift_t[:, 8:16], 0.25))
                link(nc.vector.memset(shift_a[:, 0:8], 0.0))
                link(nc.vector.memset(shift_a[:, 8:16], PI / 2))
                dve.wait_ge(consts_set, 7)
                dve.wait_ge(small_loaded, 16 * len(loads))

                with dve.Fori(0, R // 2) as it:
                    for n in range(2):
                        src, dst = basis[n], basis[1 - n]
                        chain = Link(dve, own, base=4 + 9 * n, per=18, at=it)
                        chain(nc.vector.tensor_tensor(prods[:], src[:], src[:, :, :, 0:1].to_broadcast([P, C, 2, R]), ALU.mult))
                        chain(nc.vector.tensor_tensor(prods[:, 0:2], prods[:, 0:2], prods[:, 2:4], ALU.add))
                        nc.vector.tensor_tensor(dots[:], prods[:, 0], prods[:, 1], ALU.add).then_inc(basis_ready, 1)
                        dve.wait_ge(nrm_ready, it * 2 + n + 1)
                        chain(nc.vector.tensor_scalar(rr[:], nrm[:, n], 1e-8, None, ALU.add))
                        chain(nc.vector.reciprocal(rr[:], rr[:]))
                        chain(nc.vector.tensor_tensor(
                            coef[:], coef_ps[n][:, :, 1:R],
                            norm2_mask[:, ds(it * 2 + n + 1, R - 1)].unsqueeze(1).to_broadcast([P, 2, R - 1]), ALU.mult))
                        chain(nc.vector.tensor_tensor(coef2[:], coef[:], rr[:].unsqueeze(2).to_broadcast([P, 2, R - 1]), ALU.mult))
                        chain(nc.vector.tensor_tensor(dst[:, :, :, R - 1:R], src[:, :, :, 0:1],
                                                      rr[:].unsqueeze(1).unsqueeze(3).to_broadcast([P, C, 2, 1]), ALU.mult))
                        chain(nc.vector.tensor_tensor(
                            outer_p[:], dst[:, :, :, R - 1:R].to_broadcast([P, C, 2, R - 1]),
                            coef2[:].unsqueeze(1).to_broadcast([P, C, 2, R - 1]), ALU.mult))
                        chain(nc.vector.tensor_tensor(dst[:, :, :, 0:R - 1], src[:, :, :, 1:R], outer_p[:], ALU.subtract))
                link = Link(dve, own, base=4 + 9 * R)

                link(nc.vector.tensor_copy(step_f[:], step_i[:]))
                link(nc.vector.tensor_scalar(step_f[:], step_f[:], 40.0, None, ALU.mult))
                for c in range(2):
                    link(nc.vector.tensor_scalar(angle[:, 4 + 2 * c:6 + 2 * c], step_f[:], freq[:, c:c + 1], None, ALU.mult))
                link(nc.vector.tensor_copy(angle[:, 8:16], angle[:, 0:8]))
                link(nc.vector.tensor_scalar(turns[:], angle[:], 1.0 / (2 * PI), None, ALU.mult))
                link(nc.vector.tensor_tensor(turns[:], turns[:], shift_t[:], ALU.add))
                link(nc.vector.tensor_scalar(turns[:], turns[:], ROUND, None, ALU.add))
                link(nc.vector.tensor_scalar(turns[:], turns[:], -ROUND, None, ALU.add))
                for part in (TWO_PI_A, TWO_PI_B, TWO_PI_C):
                    link(nc.vector.scalar_tensor_tensor(angle[:], turns[:], -part, angle[:], ALU.mult, ALU.add))
                link(nc.vector.tensor_tensor(angle[:], angle[:], shift_a[:], ALU.add))
                nc.vector.tensor_scalar(angle[:], angle[:], 3.1415925, -3.1415925, ALU.min, ALU.max).then_inc(angles_ready, 1)
                dve.wait_ge(sincos_ready, 3)
                nc.vector.tensor_tensor(z[:, 0:2].rearrange("p c b -> p (c b)"), sincos[:, 4:8], sig[:, 0:4], ALU.mult).then_inc(z_ready, 1)
                nc.vector.tensor_tensor(z[:, 2:4].rearrange("p c b -> p (c b)"), sincos[:, 12:16], sig[:, 4:8], ALU.mult).then_inc(z_ready, 1)

                for col, src, sign in ((0, 0, 1.0), (1, 0, -1.0), (2, 2, 1.0), (3, 2, -1.0)):
                    link(nc.vector.tensor_copy(rot_c[:, :, 0, col], sincos[:, 8 + src:10 + src]))
                    link(nc.vector.tensor_scalar(rot_c[:, :, 1, col], sincos[:, src:src + 2], sign, None, ALU.mult))

                dve.wait_ge(means_ready, B)
                for b in range(B):
                    link(nc.vector.tensor_tensor_reduce(out=prod[:], in0=pool_mean[b][:], in1=gate_w1[:], scale=1.0, scalar=0.0,
                                                        op0=ALU.mult, op1=ALU.add, accum_out=h1[:, b:b + 1]))
                link(nc.vector.tensor_scalar(h1r[:], h1[:], gate_b1[:], 0.0, ALU.add, ALU.max))
                nc.vector.tensor_scalar(h1[:], h1r[:], gate_w2[:], None, ALU.mult).then_inc(h1_ready, 1)
                dve.wait_ge(gate_ready, 2)
                link(nc.vector.tensor_tensor(strength[:], base_act[:], mod[:], ALU.mult))

                dve.wait_ge(ada_ps_ready, 1)
                link(nc.vector.tensor_tensor(keep.ada[:], ada_ps[:], b_ada_t[:].unsqueeze(2).to_broadcast([P, 2 * C, B]), ALU.add))
                link(nc.vector.tensor_scalar(keep.ada[:, 0:C], keep.ada[:, 0:C], 1.0, None, ALU.add))
                for b in range(B):
                    for half in range(2):
                        n = 2 * b + half
                        dve.wait_ge(row_ready, n + 1)
                        nc.vector.scalar_tensor_tensor(keep.ada_row[:, b, half], row_ps[n % 2][:], 1.0 - half,
                                                       b_ada_bc[:, half * D:(half + 1) * D], ALU.add, ALU.add).then_inc(row_taken, 1)
                dve.wait_ge(vtv_ready, 1)
                nc.vector.tensor_copy(vtv[:], small_ps[0:R, 0:R]).then_inc(vtv_taken, 1)
                dve.wait_ge(respt_ready, C)
                nc.vector.tensor_copy(resp_t[:], row_ps[0][0:R, :]).then_inc(respt_taken, 1)
                dve.wait_ge(a1_ready, 1)
                nc.vector.tensor_copy(a1[:], row_ps[1][0:R, :]).then_inc(a1_taken, 1)
                dve.wait_ge(g_ready, 1)
                link(nc.vector.tensor_copy(g33[0:R, :], row_ps[0][0:R, :]))
                link(nc.vector.tensor_tensor(g33[R:R + 1, :], resp_row[R:R + 1, :], safety_row[R:R + 1, :], ALU.add))

                dve.wait_ge(eye_ready, 1)
                pair = lambda ap: ap.rearrange("p (n two) -> p n two", two=2)
                link(nc.vector.tensor_copy(keep.eye_bf[:], keep.eye[:]))
                for src, dst in ((g33, g33s), (keep.eye, eye_s)):
                    link(nc.vector.tensor_copy(pair(dst[:])[:, :, 0], pair(src[:])[:, :, 1]))
                    link(nc.vector.tensor_copy(pair(dst[:])[:, :, 1], pair(src[:])[:, :, 0]))
                quad = lambda ap: ap.rearrange("p (n four) -> p n four", four=4)
                for b in range(B):
                    for src, swapped, tmp, dst, n in ((g33, g33s, gtmp, keep.g33[:, b], R + 1), (keep.eye, eye_s, eye_c, keep.rot[:, b], P)):
                        m = src.shape[1] // 4
                        c_of = lambda w: rot_c[0:n, b, w].unsqueeze(1).to_broadcast([n, m, 4])
                        link(nc.vector.tensor_tensor(quad(tmp[:]), quad(swapped[:]), c_of(1), ALU.mult))
                        link(nc.vector.tensor_tensor(quad(dst), quad(src[:]), c_of(0), ALU.mult))
                        link(nc.vector.tensor_tensor(dst, dst, tmp[:], ALU.add))
                    link(nc.vector.tensor_scalar(keep.g33[:, b], keep.g33[:, b], strength[0:R + 1, b:b + 1], None, ALU.mult))
                link(nc.vector.tensor_scalar(keep.bq[:], keep.bq[:], DH ** -0.5, None, ALU.mult))

            @block.scalar
            def _(act):
                for n in range(2):
                    act.sem_inc(m_stored[n], 16)
                with act.Fori(0, R // 2) as it:
                    for n in range(2):
                        act.wait_ge(coef_ready, it * 2 + n + 1)
                        nc.scalar.activation(nrm[:, n], coef_ps[n][:, :, 0], ACT.Sqrt).then_inc(nrm_ready, 1)
                        act.wait_ge(m_loaded[n], it * 16 + 16)
                        act.wait_ge(m_stored[n], it * 16 + 16)
                        nc.scalar.copy(mask_bf[n][:], mask_in[n][:].bitcast(U8)).then_inc(m_cast, 1)
                act.wait_ge(angles_ready, 1)
                nc.scalar.activation(sincos[:], angle[:], ACT.Sin).then_inc(sincos_ready, 1)
                act.wait_ge(sincos_ready, 1)
                nc.scalar.activation(sig[:, 0:4], sincos[:, 4:8], ACT.Sigmoid).then_inc(sincos_ready, 1)
                nc.scalar.activation(sig[:, 4:8], sincos[:, 12:16], ACT.Sigmoid).then_inc(sincos_ready, 1)
                act.wait_ge(sincos_ready, 3)
                nc.scalar.activation(mod[:], score[:], ACT.Sigmoid).then_inc(gate_ready, 1)
                act.wait_ge(gate_ps_ready, 1)
                nc.scalar.activation(base_act[:], coef_ps[0][:, 0, 0:B], ACT.Sigmoid, bias=gate_b2[:]).then_inc(gate_ready, 1)

            @block.tensor
            def _(pe):
                mm = nc.tensor.matmul
                pe.wait_ge(consts_set, 7)
                pe.wait_ge(small_loaded, 16 * len(loads))
                steps = R // 2 // B
                for b in range(B):
                    mm(pool_mean[b][:], mean_w[:], zeros[:], start=True, stop=False, skip_group_check=True)
                    with pe.Fori(b * steps, (b + 1) * steps) as it:
                        for n in range(2):
                            pe.wait_ge(basis_ready, it * 2 + n + 1)
                            mm(coef_ps[n][:], ones[:], dots[:], start=True, stop=True).then_inc(coef_ready, 1)
                            pe.wait_ge(x_loaded[n], it * 16 + 16)
                            mm(pool_mean[b][:], mean_w[:], x_in[:, n], start=False, stop=False, skip_group_check=True).then_inc(mean_tiles, 1)
                    mm(pool_mean[b][:], mean_w[:], zeros[:], start=False, stop=True, skip_group_check=True).then_inc(means_ready, 1)
                pe.wait_ge(z_ready, 2)
                for f in range(2 * C):
                    for c in range(C):
                        last = mm(ada_ps[:, f, :], w_ada[:, c, f * P:(f + 1) * P], z[:, c, :], start=(c == 0), stop=(c == C - 1))
                last.then_inc(ada_ps_ready, 1)
                pe.wait_ge(h1_ready, 1)
                mm(coef_ps[0][:, 0, 0:B], ones[:], h1[:], start=True, stop=True).then_inc(gate_ps_ready, 1)
                for b in range(B):
                    for half in range(2):
                        n = 2 * b + half
                        if n >= 2:
                            pe.wait_ge(row_taken, n - 1)
                        for c in range(C):
                            last = mm(row_ps[n % 2][:], z[:, c, b:b + 1].to_broadcast([P, P]), w_ada[:, c, half * D:(half + 1) * D],
                                      start=(c == 0), stop=(c == C - 1))
                        last.then_inc(row_ready, 1)
                q0 = basis[0]
                for c in range(C):
                    last = mm(small_ps[0:R, 0:R], q0[:, c, 1, :], q0[:, c, 1, :], start=(c == 0), stop=(c == C - 1))
                last.then_inc(vtv_ready, 1)
                pe.wait_ge(row_taken, 4)
                pe.wait_ge(eye_ready, 1)
                for c in range(C):
                    nc.tensor.transpose(row_ps[0][0:R, c * P:(c + 1) * P], resp_w[:, c, :], keep.eye[:]).then_inc(respt_ready, 1)
                pe.wait_ge(respt_taken, 1)
                mm(row_ps[1][0:R, :], q0[0:R, 0, 0, :], resp_t[:], start=True, stop=True).then_inc(a1_ready, 1)
                pe.wait_ge(vtv_taken, 1)
                pe.wait_ge(a1_taken, 1)
                mm(row_ps[0][0:R, :], vtv[:], a1[:], start=True, stop=True).then_inc(g_ready, 1)


def embed(k, i, keep, scr):
    nc = k.nc
    with ExitStack() as ctx:
        sb = lambda *a: k.sb(ctx, *a)
        x_in = sb("x_in", [P, GT, D])
        xt = sb("xt", [P, C, GTOK])
        stats, mv = sb("stats1", [P, 6]), sb("mv1", [P, GT, 2])
        std, rstd = sb("std1", [P, GT]), sb("rstd1", [P, GT])
        xn = sb("xn1", [P, GT, D])
        x2 = sb("x2_out", [P, GT, D])
        t32 = sb("t32_1", [P, 2, GTOK])
        th, tl = sb("th1", [P, C, GTOK], F32R), sb("tl1", [P, C, GTOK], F32R)
        tp = [k.ps(ctx, f"tp{n}", [P, 512]) for n in range(2)]
        hp = [k.ps(ctx, f"hp{n}", [P, 512]) for n in range(2)]
        yp = k.ps(ctx, "yp", [P, 512])
        x1p = [k.ps(ctx, f"x1p{n}", [P, D]) for n in range(3)]

        x_loaded, xt_turned, xt_taken = (k.sem("em_" + n) for n in ("x_loaded", "xt_turned", "xt_taken"))
        y_ready, y_taken, x1_ready, x1_taken = (k.sem("em_" + n) for n in ("y_ready", "y_taken", "x1_ready", "x1_taken"))
        own_idle = k.sem("em_idle")
        var_ready, std_ready, own, xn_ready = (k.sem("em_" + n) for n in ("var_ready", "std_ready", "dve_chain", "xn_ready"))
        xnt_turned, t32_ready, t32_split, t_high = (k.sem("em_" + n) for n in ("xnt_turned", "t32_ready", "t32_split", "t_high"))
        x2_ready, pool_own, x2_stored, t_stored = (k.sem("em_" + n) for n in ("x2_ready", "pool_chain", "x2_stored", "t_stored"))
        x_g = i.x.rearrange("b (g t p) d -> (b g) p t d", t=GT, p=P)
        x2_g = scr.x2.rearrange("(g t p) d -> g p t d", t=GT, p=P)
        tile_of = lambda ap, it: ap[ds(it, 1)].rearrange("a p t d -> p (a t) d")

        def over_groups(eng, body):
            body(0, 0, None)
            for b in range(B):
                if b:
                    body(b * GB, b, b - 1)
                with eng.Fori(b * GB + 1, (b + 1) * GB) as g:
                    body(g, b, b)

        with nc.Block() as block:
            @block.sync
            def _(sp):
                def load(g):
                    sp.dma_start(x_in[:], tile_of(x_g, g)).then_inc(x_loaded, 16)

                def store_x2(g):
                    sp.wait_ge(x2_ready, g * GT + GT)
                    sp.dma_start(tile_of(x2_g, g), x2[:]).then_inc(x2_stored, 16)

                def store_t(g):
                    sp.wait_ge(t32_split, g * C + C + 2)
                    for w, src in enumerate((th, tl)):
                        sp.dma_start(scr.x2t[w].rearrange("(c p) n -> p c n", p=P)[:, :, ds(g * GTOK, GTOK)],
                                     src[:].bitcast(F32)).then_inc(t_stored, 16)

                load(0)
                sp.wait_ge(xt_turned, GT)
                load(1)
                store_x2(0)
                with sp.Fori(1, NG - 1) as g:
                    sp.wait_ge(xt_turned, g * GT + GT)
                    load(g + 1)
                    store_t(g - 1)
                    store_x2(g)
                store_t(NG - 2)
                store_x2(NG - 1)
                store_t(NG - 1)
                sp.wait_ge(x2_stored, 16 + 16 * NG)
                sp.wait_ge(t_stored, 32 + 32 * NG)

            @block.gpsimd
            def _(pool):
                pool.sem_inc(x2_stored, 16)

                def body(g, b, _):
                    for t in range(GT):
                        pool.wait_ge(xn_ready, g * GT + t + 1)
                        if t == 0:
                            pool.wait_ge(x2_stored, g * 16 + 16)
                        nc.gpsimd.tensor_tensor(x2[:, t], xn[:, t], keep.ada_row[:, b, 0], ALU.mult).then_inc(pool_own, 1)
                        pool.wait_ge(pool_own, g * GT + t + 1)
                        nc.gpsimd.tensor_tensor(x2[:, t], x2[:, t], keep.ada_row[:, b, 1], ALU.add).then_inc(x2_ready, 1)
                over_groups(pool, body)

            @block.tensor
            def _(pe):
                mm = nc.tensor.matmul

                def turn_xn(g):
                    pe.wait_ge(xn_ready, g * GT + GT)
                    for c in range(C):
                        pe.wait_ge(t32_ready, g * C + c + 1)
                        for t in range(GT):
                            last = nc.tensor.transpose(hp[c % 2][:, t * P:(t + 1) * P], xn[:, t, c * P:(c + 1) * P], keep.eye[:])
                        last.then_inc(xnt_turned, 1)

                def body(g, b, before):
                    pe.wait_ge(x_loaded, g * 16 + 16)
                    for t in range(GT):
                        pe.wait_ge(xt_taken, g * GT + t + 1)
                        for c in range(C):
                            last = nc.tensor.transpose(tp[t % 2][:, c * P:(c + 1) * P], x_in[:, t, c * P:(c + 1) * P], keep.eye[:])
                        last.then_inc(xt_turned, 1)
                    if before is not None:
                        turn_xn(g - 1)
                    pe.wait_ge(xt_taken, g * GT + GT + 2)
                    for c in range(C):
                        last = mm(yp[0:R, :], keep.basis[:, c, 0, :], xt[:, c, :], start=(c == 0), stop=(c == C - 1))
                    last.then_inc(y_ready, 1)
                    pe.wait_ge(y_taken, g + 1)
                    for t in range(GT):
                        if t == 0:
                            pe.wait_ge(x1_taken, g * GT + 1)
                        if t == 3:
                            pe.wait_ge(x1_taken, g * GT + 2)
                        tok = slice(t * P, (t + 1) * P)
                        mm(x1p[t % 3][:], keep.y33[:, tok], keep.g33[:, b], start=True, stop=False, skip_group_check=True)
                        for c in range(C):
                            last = mm(x1p[t % 3][:, c * P:(c + 1) * P], xt[:, c, tok], keep.rot[:, b],
                                      start=False, stop=(c == C - 1), skip_group_check=True)
                        last.then_inc(x1_ready, 1)
                over_groups(pe, body)
                turn_xn(NG - 1)

            @block.scalar
            def _(act):
                act.sem_inc(xt_taken, 2)
                act.sem_inc(t32_ready, 2)
                act.sem_inc(t32_split, 2)

                def affine(g, b):
                    for c in range(C):
                        act.wait_ge(xnt_turned, g * C + c + 1)
                        act.wait_ge(t32_split, g * C + c + 1)
                        nc.scalar.activation(t32[:, c % 2], hp[c % 2][:], ACT.Identity,
                                             scale=keep.ada[:, c, b:b + 1], bias=keep.ada[:, C + c, b:b + 1]).then_inc(t32_ready, 1)

                def body(g, b, before):
                    if before is not None:
                        act.wait_ge(x1_ready, g * GT)
                    for t in range(GT):
                        act.wait_ge(xt_turned, g * GT + t + 1)
                        nc.scalar.copy(xt[:, :, t * P:(t + 1) * P], tp[t % 2][:].rearrange("p (c n) -> p c n", c=C)).then_inc(xt_taken, 1)
                    if before is not None:
                        affine(g - 1, before)
                    act.wait_ge(y_ready, g + 1)
                    nc.scalar.copy(keep.y33[0:R, :], yp[0:R, :]).then_inc(y_taken, 1)
                    for t in range(GT):
                        act.wait_ge(var_ready, g * GT + t + 1)
                        nc.scalar.activation(std[:, t:t + 1], mv[:, t, 1:2], ACT.Sqrt, bias=keep.eps5[:]).then_inc(std_ready, 1)
                over_groups(act, body)
                affine(NG - 1, B - 1)

            @block.vector
            def _(dve):
                dve.sem_inc(x1_taken, 1)
                dve.sem_inc(t_stored, 32)

                def split(g):
                    dve.wait_ge(t_stored, g * 32 + 32)
                    for c in range(C):
                        dve.wait_ge(t32_ready, g * C + c + 3)
                        nc.vector.tensor_copy(th[:, c], t32[:, c % 2]).then_inc(t_high, 1)
                        dve.wait_ge(t_high, g * C + c + 1)
                        nc.vector.tensor_tensor(tl[:, c], t32[:, c % 2], th[:, c].bitcast(F32), ALU.subtract).then_inc(t32_split, 1)

                def body(g, b, before):
                    if before is not None:
                        split(g - 1)
                        dve.wait_ge(xnt_turned, g * C)
                        dve.wait_ge(x2_ready, g * GT)
                    link = Link(dve, own, per=GT * 2, at=g)
                    for t in range(GT + 1):
                        if t < GT:
                            dve.wait_ge(x1_ready, g * GT + t + 1)
                            if t:
                                dve.wait_ge(var_ready, g * GT + t)
                            link(nc.vector.bn_stats(stats[:], x1p[t % 3][:]))
                            dve.sem_inc(own_idle, 1)
                            nc.vector.bn_aggr(mv[:, t], stats[:]).then_inc(var_ready, 1)
                        if t:
                            dve.wait_ge(std_ready, g * GT + t)
                            link(nc.vector.reciprocal(rstd[:, t - 1:t], std[:, t - 1:t]))
                            nc.vector.tensor_scalar(xn[:, t - 1], x1p[(t - 1) % 3][:], mv[:, t - 1, 0:1], rstd[:, t - 1:t], ALU.subtract, ALU.mult).then_inc(xn_ready, 1)
                            dve.wait_ge(xn_ready, g * GT + t)
                            dve.sem_inc(x1_taken, 1)
                over_groups(dve, body)
                split(NG - 1)


def project(k, i, keep, scr):
    nc = k.nc
    with ExitStack() as ctx:
        sb = lambda *a: k.sb(ctx, *a)
        xt = [[sb(f"x2t_{n}_{w}", [P, C, GTOK], F32R) for w in range(2)] for n in range(2)]
        q32 = sb("q32", [P, 2, GTOK])
        parts = [sb(f"qk_parts{n}", [P, 2, GTOK], F32R) for n in range(2)]
        v_out = [sb(f"v_out{n}", [P, D]) for n in range(2)]
        bank = [k.ps(ctx, f"pj{n}", [P, 512]) for n in range(8)]
        x_loaded = [k.sem(f"pj_x_loaded{n}") for n in range(2)]
        x_used, job_ready, qk_taken, v_taken = (k.sem("pj_" + n) for n in ("x_used", "job_ready", "qk_taken", "v_taken"))
        hi_done, lo_done = k.sem("pj_hi_done"), k.sem("pj_lo_done")
        qk_stored = [k.sem(f"pj_qk_stored{n}") for n in range(2)]
        v_stored = [k.sem(f"pj_v_stored{n}") for n in range(2)]
        NJ = 3 * C

        def load(sp, g, n):
            for w in range(2):
                sp.dma_start(xt[n][w][:].bitcast(F32),
                             scr.x2t[w].rearrange("(c p) n -> p c n", p=P)[:, :, ds(g * GTOK, GTOK)]).then_inc(x_loaded[n], 16)

        def pair(sp, it, more):
            for n in range(2):
                g = it * 2 + n
                for m in range(2 * C):
                    sp.wait_ge(lo_done, g * 2 * C + m + 1)
                    dst = (scr.q if m < C else scr.k)[:, (m % C) * P:(m % C + 1) * P, ds(g * GTOK, GTOK)]
                    sp.dma_start(dst.rearrange("w f s -> f w s"), parts[m % 2][:].bitcast(F32)).then_inc(qk_stored[m % 2], 16)
                for t in range(GT):
                    sp.wait_ge(v_taken, g * GT + t + 1 + GT)
                    sp.dma_start(scr.v[ds(g * GTOK + t * P, P), :], v_out[t % 2][:]).then_inc(v_stored[t % 2], 16)
                if more:
                    sp.wait_ge(x_used, g + 1)
                    load(sp, g + 2, n)

        with nc.Block() as block:
            @block.sync
            def _(sp):
                for n in range(2):
                    load(sp, n, n)
                with sp.Fori(0, NG // 2 - 1) as it:
                    pair(sp, it, True)
                pair(sp, NG // 2 - 1, False)
                for n in range(2):
                    sp.wait_ge(qk_stored[n], 16 + 16 * NG * C)
                    sp.wait_ge(v_stored[n], 16 + 16 * NG * GT // 2)

            @block.tensor
            def _(pe):
                mm = nc.tensor.matmul
                with pe.Fori(0, NG // 2) as it:
                    for n in range(2):
                        g = it * 2 + n
                        pe.wait_ge(x_loaded[n], it * 32 + 32)
                        hi, lo = xt[n]
                        for j in range(NJ):
                            at = bank[(n * NJ + j) % 8]
                            if j < C:
                                pe.wait_ge(qk_taken, g * 2 * C + j + C + 1)
                            elif j < 2 * C:
                                pe.wait_ge(v_taken, g * GT + j - C + 1)
                            else:
                                pe.wait_ge(qk_taken, g * 2 * C + j + 1)
                            first, last = True, None
                            for c in range(C):
                                for a, w in ((hi, keep.w_hi), (lo, keep.w_hi), (hi, keep.w_lo)):
                                    end = c == C - 1 and w is keep.w_lo
                                    if j < 2 * C:
                                        m = j % C
                                        last = mm(at[:], w[:, j // C, c, m * P:(m + 1) * P], a[:, c, :], start=first, stop=end)
                                    else:
                                        t = j - 2 * C
                                        last = mm(at[:], a[:, c, t * P:(t + 1) * P], w[:, 2, c, :], start=first, stop=end)
                                    first = False
                            last.then_inc(job_ready, 1)
                            if j == NJ - 1:
                                pe.wait_ge(job_ready, g * NJ + NJ)
                                pe.sem_inc(x_used, 1)

            @block.scalar
            def _(act):
                act.sem_inc(qk_taken, 2 * C)
                with act.Fori(0, NG // 2) as it:
                    for n in range(2):
                        g = it * 2 + n
                        for j in range(2 * C):
                            act.wait_ge(job_ready, g * NJ + j + 1)
                            if j < 2:
                                act.wait_ge(v_taken, g * GT + GT)
                            else:
                                act.wait_ge(lo_done, g * 2 * C + j - 1)
                            bias, scale = (keep.bq, DH ** -0.5) if j < C else (keep.bk, 1.0)
                            nc.scalar.activation(q32[:, j % 2], bank[(n * NJ + j) % 8][:], ACT.Identity,
                                                 scale=scale, bias=bias[:, j % C:j % C + 1]).then_inc(qk_taken, 1)

            @block.vector
            def _(dve):
                dve.sem_inc(v_taken, GT)
                for n in range(2):
                    dve.sem_inc(qk_stored[n], 16)
                    dve.sem_inc(v_stored[n], 16)
                with dve.Fori(0, NG // 2) as it:
                    for n in range(2):
                        g = it * 2 + n
                        for j in range(2 * C):
                            dve.wait_ge(qk_taken, g * 2 * C + 2 * C + j + 1)
                            dve.wait_ge(qk_stored[j % 2], (g * C + j // 2) * 16 + 16)
                            nc.vector.tensor_copy(parts[j % 2][:, 0], q32[:, j % 2]).then_inc(hi_done, 1)
                            dve.wait_ge(hi_done, g * 2 * C + j + 1)
                            nc.vector.tensor_tensor(parts[j % 2][:, 1], q32[:, j % 2], parts[j % 2][:, 0].bitcast(F32), ALU.subtract).then_inc(lo_done, 1)
                        for t in range(GT):
                            dve.wait_ge(job_ready, g * NJ + 2 * C + t + 1)
                            dve.wait_ge(v_stored[t % 2], (g * 2 + t // 2) * 16 + 16)
                            nc.vector.tensor_tensor(v_out[t % 2][:], bank[(n * NJ + 2 * C + t) % 8][:], keep.bv[:], ALU.add).then_inc(v_taken, 1)


def attend(k, i, keep, scr):
    nc = k.nc
    UNITS = 2 * HG
    RING = 7
    SHARED = ((0, 0), (2, 0), (4, 1), (6, 1))
    LEAD = 2
    LAG = 2
    PV_CHUNKS = 22
    PV_SKIP = 8
    NCH = S // 512
    KH = KT // 2
    with ExitStack() as ctx:
        sb = lambda *a: k.sb(ctx, *a)
        kst = [sb(f"k_stack{h}", [P, S], F32R) for h in range(HG)]
        qst = [sb(f"q_stack{t}", [P, HG, P], F32R) for t in range(2)]
        vt = sb("v_tile", [P, KT, P])
        mask = [sb(f"mask{t}", [P, S], BF16) for t in range(2)]
        unit = [sb(f"unit{u}", [P, S]) for u in range(UNITS)]
        probs_t = [sb(f"probs_t{c}", [P, HG, KH, QB]) for c in range(2)]
        part_max, neg_max = sb("part_max", [P, UNITS, NCH]), sb("neg_max", [P, UNITS])
        total, inv_total = sb("total", [P, UNITS]), sb("inv_total", [P, UNITS])
        masked = sb("masked", [P, P], BF16)
        ctx_t = sb("ctx_t", [P, QB])
        ctx_out = sb("ctx_out", [P, 2, P])
        w32 = sb("w32", [P, D])
        whr, wlr = sb("whr", [P, D], F32R), sb("wlr", [P, D], F32R)
        expert = sb("expert", [1, B], I32)
        ring = [k.ps(ctx, f"ring{n}", [P, 512]) for n in range(RING)]
        out_ps = k.ps(ctx, "out_ps", [P, 2 * QB])
        ctx_ps, back_ps = out_ps[:, 0:QB], out_ps[:, QB:2 * QB].rearrange("p (t f) -> p t f", t=2)

        bias_loaded = [k.sem(f"at_bias_loaded{u}") for u in range(UNITS)]
        qm_loaded = [k.sem(f"at_qm_loaded{t}") for t in range(2)]
        k_loaded = [k.sem(f"at_k_loaded{h}") for h in range(HG)]
        v_loaded, masked_set = k.sem("at_v_loaded"), k.sem("at_masked_set")
        sc_ready = k.sem("at_sc_ready")
        bank_free = [k.sem(f"at_bank_free{n}") for n in range(RING)]
        max_ready = k.sem("at_max_ready")
        exp_done, inv_ready = k.sem("at_exp_done"), k.sem("at_inv_ready")
        turned = [k.sem(f"at_turned_{n}") for n in ("low", "high")]
        pv_half, ctx_taken, back_ready, normed = (k.sem("at_" + n) for n in ("pv_half", "ctx_taken", "back_ready", "normed"))
        ctx_stored, idle, pool_idle = k.sem("at_ctx_stored"), k.sem("at_idle"), k.sem("at_pool_idle")
        w_loaded, w_high, w_low, w_stored, e_loaded = (k.sem("at_" + n) for n in ("w_loaded", "w_high", "w_low", "w_stored", "e_loaded"))

        scored = lambda u: [("scores", u, c) for c in range(NCH)]
        halves = lambda u, c: [(which, u, c) for which in (1, 0)]
        SECOND = [(UNITS - 2, 0), (0, 1), (1, 1), (UNITS - 1, 0)] + [(u, 1) for u in range(2, UNITS)]
        order = []
        for u in range(LEAD, UNITS):
            order += scored(u) + (halves(u - LAG, 0) if u >= LAG else [])
        for u, c in SECOND:
            order += halves(u, c) + (scored(u - UNITS + LEAD) if c and u >= UNITS - LEAD else [])
        SHORT = (-len(order)) % RING * (RING - 1)
        banks = [n % (RING - 1) if n < SHORT else (n - SHORT) % RING for n in range(len(order))]
        fills = [banks.count(n) for n in range(RING)]
        led = [banks[n] for n, what in enumerate(order) if what[0] == "scores" and what[1] < LEAD]
        turns = lambda which: [what for what in order if what[0] == which]

        def place(*what):
            n = order.index(what)
            return banks[n], banks[:n].count(banks[n])

        bias_rows = i.bias.rearrange("b h q s -> (b h q) s")
        PER_ROW = NHG * NQ

        def where(s):
            b = s // PER_ROW
            return b * S + (s % NQ) * QB, b * S, ((s // NQ) % NHG) * P

        def load_qm(sp, s, t):
            row, _, feat = where(s)
            for a in range(4):
                src = scr.q[a // 2, ds(feat, P), ds(row + t * P, P)]
                sp.dma_start(qst[t][a * DH:(a + 1) * DH].bitcast(F32), src.rearrange("(h d) s -> d h s", d=DH)).then_inc(qm_loaded[t], 16)
            sp.dma_start(mask[t][:], scr.mask[ds(row + t * P, P), :]).then_inc(qm_loaded[t], 16)

        def load_bias(sp, s, u):
            t, h = u // HG, u % HG
            row = ((s // NQ) * HG + h) * S + (s % NQ) * QB + t * P
            sp.dma_start(unit[u][:], bias_rows[ds(row, P), :]).then_inc(bias_loaded[u], 16)

        def store_ctx(sp, s):
            row, _, feat = where(s)
            sp.wait_ge(normed, s + 2)
            sp.dma_start(scr.ctx[ds(row, QB), ds(feat, P)].rearrange("(t p) f -> p t f", p=P), ctx_out[:]).then_inc(ctx_stored, 16)

        with nc.Block() as block:
            @block.sync
            def _(sp):
                for t in range(2):
                    load_qm(sp, 0, t)
                    for u in range(t * HG, (t + 1) * HG):
                        if 0 < u < HG:
                            sp.wait_ge(k_loaded[u], 64)
                        load_bias(sp, 0, u)
                def next_step(s, before):
                    for t in range(2):
                        sp.wait_ge(sc_ready, (s * UNITS + (t + 1) * HG) * NCH)
                        load_qm(sp, s + 1, t)
                        for u in range(t * HG, (t + 1) * HG):
                            for which in range(2):
                                sp.wait_ge(turned[which], s * 2 * UNITS + turns(which).index((which, u, 1)) + 1)
                            load_bias(sp, s + 1, u)
                            if u == HG and before is not None:
                                store_ctx(sp, before)

                next_step(0, None)
                with sp.Fori(1, STEPS - 1) as s:
                    next_step(s, s - 1)
                store_ctx(sp, STEPS - 2)
                store_ctx(sp, STEPS - 1)
                sp.wait_ge(ctx_stored, 16 * STEPS + 16)

            def load_kv(pool, g):
                b, feat = g // NHG, (g % NHG) * P
                for h in range(HG):
                    if not isinstance(g, int) or g:
                        pool.wait_ge(sc_ready, (g * NQ * UNITS - HG + h + 1) * NCH)
                        pool.sem_inc(pool_idle, 1)
                    for a in range(4):
                        pool.dma_start(kst[h][a * DH:(a + 1) * DH, :].bitcast(F32),
                                       scr.k[a % 2, ds(feat + h * DH, DH), ds(b * S, S)]).then_inc(k_loaded[h], 16)
                if not isinstance(g, int) or g:
                    pool.wait_ge(pv_half, g * NQ * 2 + 2)
                    pool.sem_inc(pool_idle, 1)
                pool.dma_start(vt[:], scr.v[ds(b * S, S), ds(feat, P)].rearrange("(t p) f -> p t f", p=P)).then_inc(v_loaded, 16)

            @block.gpsimd
            def _(pool):
                load_kv(pool, 0)
                pool.dma_start(expert[:], i.expert.rearrange("(a n) -> a n", a=1)).then_inc(e_loaded, 16)
                pool.wait_ge(e_loaded, 16)
                chosen = [pool.value_load(expert[0:1, b:b + 1], min_val=0, max_val=E - 1) for b in range(B)]
                wide = lambda ap: ap.rearrange("r (n c) -> (r n) c", c=D)
                experts_in, experts_out = i.Wi.rearrange("e r (n c) -> (e r n) c", c=D), i.We.rearrange("e r c -> (e r) c")
                ROWS = D * FF // D
                sources = [(wide(i.W1), None, scr.w1, 0), (i.W2, None, scr.w2, 0)]
                for b in range(B):
                    sources += [(experts_in, chosen[b], scr.wi, b), (experts_out, chosen[b], scr.we, b)]

                def eighth(g):
                    n = 0
                    PER = 2 * len(sources) + 1
                    jobs = [(src, pick, dst, b, part) for src, pick, dst, b in sources for part in range(2)]
                    jobs.append((i.Wo, None, scr.wo, 0, None))
                    for src, pick, dst, b, part in jobs:
                        rows = P if part is not None else D // NHG // B
                        at = g * 2 * P + part * P if part is not None else g * rows
                        frm = at if pick is None else pick * ROWS + at
                        done = g * PER + n
                        pool.dma_start(w32[0:rows], src[ds(frm, rows), :]).then_inc(w_loaded, 16)
                        pool.wait_ge(w_loaded, done * 16 + 16)
                        pool.sem_inc(pool_idle, 1)
                        nc.gpsimd.tensor_copy(whr[0:rows], w32[0:rows]).then_inc(w_high, 1)
                        pool.wait_ge(w_high, done + 1)
                        nc.gpsimd.tensor_tensor(wlr[0:rows], w32[0:rows], whr[0:rows].bitcast(F32), ALU.subtract).then_inc(w_low, 1)
                        pool.wait_ge(w_low, done + 1)
                        pool.sem_inc(pool_idle, 1)
                        to = b * ROWS + at if part is not None else at
                        for w, tile in enumerate((whr, wlr)):
                            pool.dma_start(dst[w][ds(to, rows), :], tile[0:rows].bitcast(F32)).then_inc(w_stored, 16)
                        pool.wait_ge(w_stored, done * 32 + 32)
                        pool.sem_inc(pool_idle, 1)
                        n += 1

                with pool.Fori(0, B * NHG - 1) as g:
                    eighth(g)
                    load_kv(pool, g + 1)
                eighth(B * NHG - 1)

            def reads(s, *what):
                n, before = place(*what)
                ahead = what[0] == "scores" and what[1] < LEAD
                return ring[n], bank_free[n], (s if ahead else s + 1) * fills[n] + before + 1

            def wait_bank(s, what):
                bank, free, count = reads(s, *what)
                nc.tensor.wait_ge(free, count)
                return bank

            def scores(s, u, c):
                t, h = u // HG, u % HG
                pe = nc.tensor
                if c == 0:
                    pe.wait_ge(qm_loaded[t], s * 80 + 80)
                    pe.wait_ge(k_loaded[h], (s // NQ) * 64 + 64)
                at = wait_bank(s, ("scores", u, c))
                cols = slice(c * 512, (c + 1) * 512)
                nc.tensor.matmul(at[:], qst[t][:, h, :], kst[h][:, cols], start=True, stop=False)
                nc.tensor.matmul(at[:], masked[:], mask[t][:, cols], start=False, stop=True).then_inc(sc_ready, 1)

            def turn(s, u, c):
                if c == 0:
                    nc.tensor.wait_ge(exp_done, s * UNITS + u + 1)
                src = planes(unit[u][:])
                for which in (1, 0):
                    at = wait_bank(s, (which, u, c))[:].bitcast(BF16)
                    for j in range(KH):
                        keys = slice((c * KH + j) * P, (c * KH + j + 1) * P)
                        last = nc.tensor.transpose(at[:, j * P:(j + 1) * P], src[:, keys, which], keep.eye_bf[:])
                    last.then_inc(turned[which], 1)

            def take(eng, copy, s, u, c, which):
                t, h = u // HG, u % HG
                eng.wait_ge(turned[which], s * 2 * UNITS + turns(which).index((which, u, c)) + 1)
                if u == 0:
                    eng.wait_ge(pv_half, s * 2 + c + 1)
                dst = probs_t[c][:, h, :, t * P:(t + 1) * P].bitcast(U16).rearrange("p k (q two) -> p k q two", two=2)[:, :, :, which]
                n, _ = place(which, u, c)
                copy(dst, ring[n][:].bitcast(U16).rearrange("p (k q) -> p k q", q=P)).then_inc(bank_free[n], 1)

            def take_high(s, u, c):
                take(nc.scalar, nc.scalar.copy, s, u, c, 1)
                if (u, c) in SHARED:
                    take(nc.scalar, nc.scalar.copy, s, u, c, 0)

            def take_low(s, u, c):
                if (u, c) not in SHARED:
                    take(nc.vector, nc.vector.tensor_copy, s, u, c, 0)

            def weigh(s, kt):
                pe = nc.tensor
                if kt == 0:
                    pe.wait_ge(v_loaded, (s // NQ) * 16 + 16)
                    pe.wait_ge(normed, s + 1)
                c = kt // KH
                if kt % KH == 0:
                    for n in range(RING):
                        what = [w for w, bank in zip(order, banks) if bank == n and w[0] != "scores" and w[2] == c]
                        if what:
                            _, free, count = reads(s, *what[-1])
                            pe.wait_ge(free, count + 1)
                for h in range(HG):
                    last = nc.tensor.matmul(ctx_ps[h * DH:(h + 1) * DH, :], vt[:, kt, h * DH:(h + 1) * DH], probs_t[c][:, h, kt % KH, :],
                                            start=(kt == 0), stop=(kt == KT - 1))
                if kt % KH == KH - 1:
                    last.then_inc(pv_half, 1)

            def turn_back(s):
                pe = nc.tensor
                pe.wait_ge(ctx_taken, s + 1)
                for t in range(2):
                    last = nc.tensor.transpose(back_ps[:, t, :], ctx_t[:, t * P:(t + 1) * P], keep.eye[:])
                last.then_inc(back_ready, 1)

            def chunk_max(s, u, c):
                dve = nc.vector
                if c == 0:
                    dve.wait_ge(bias_loaded[u], s * 16 + 16)
                dve.wait_ge(sc_ready, (s * UNITS + u) * NCH + c + 1)
                dve.sem_inc(idle, 1)
                cols = slice(c * 512, (c + 1) * 512)
                n, _ = place("scores", u, c)
                nc.vector.tensor_tensor_reduce(out=unit[u][:, cols], in0=ring[n][:], in1=unit[u][:, cols], scale=1.0, scalar=LOWEST,
                                               op0=ALU.add, op1=ALU.max, accum_out=part_max[:, u, c:c + 1]).then_inc(bank_free[n], 1)

            def unit_max(s, u):
                dve = nc.vector
                for c in range(NCH):
                    _, free, count = reads(s, "scores", u, c)
                    dve.wait_ge(free, count + 1)
                nc.vector.tensor_reduce(neg_max[:, u:u + 1], part_max[:, u, :], AX, ALU.max, negate=True).then_inc(max_ready, 1)

            def exponents(s, u):
                act = nc.scalar
                act.wait_ge(max_ready, s * UNITS + u + 1)
                if u == 0:
                    act.wait_ge(inv_ready, s + 1)
                nc.scalar.activation(unit[u][:], unit[u][:], ACT.Exp, bias=neg_max[:, u:u + 1], accum_out=total[:, u:u + 1]).then_inc(exp_done, 1)

            @block.tensor
            def _(pe):
                pe.wait_ge(masked_set, 1)

                def all_scores(s, u):
                    for c in range(NCH):
                        scores(s, u, c)

                def round_of(s, before, more):
                    kt = KH
                    for u in range(LEAD, UNITS):
                        for c in range(NCH):
                            scores(s, u, c)
                            while before is not None and kt < min(KT, KH + KH * ((u - LEAD) * NCH + c + 1) // PV_CHUNKS):
                                weigh(before, kt)
                                kt += 1
                        if u >= LAG:
                            turn(s, u - LAG, 0)
                    kt = 0
                    for n, (u, c) in enumerate(SECOND):
                        turn(s, u, c)
                        if n == 1 and before is not None:
                            turn_back(before)
                        while kt < KH * (n + 1 - PV_SKIP) // (len(SECOND) - PV_SKIP):
                            weigh(s, kt)
                            kt += 1
                        if c and u >= UNITS - LEAD:
                            if more:
                                all_scores(s + 1, u - UNITS + LEAD)
                            else:
                                for part in range(NCH):
                                    what = ("scores", u - UNITS + LEAD, part)
                                    wait_bank(s + 1, what)
                                    pe.sem_inc(bank_free[place(*what)[0]], 1)

                for u in range(LEAD):
                    all_scores(0, u)
                round_of(0, None, True)
                with pe.Fori(0, STEPS - 2) as s:
                    round_of(s + 1, s, True)
                round_of(STEPS - 1, STEPS - 2, False)
                for kt in range(KH, KT):
                    weigh(STEPS - 1, kt)
                turn_back(STEPS - 1)

            @block.scalar
            def _(act):
                for n in range(RING):
                    act.sem_inc(bank_free[n], fills[n] + 1 - led.count(n))
                act.sem_inc(pv_half, 2)

                def context(s):
                    act.wait_ge(pv_half, s * 2 + 4)
                    act.wait_ge(back_ready, s + 1)
                    nc.scalar.copy(ctx_t[:], ctx_ps).then_inc(ctx_taken, 1)

                def round_of(s, before, more):
                    for u in range(LEAD, UNITS):
                        if u == UNITS - 1 and before is not None:
                            context(before)
                        exponents(s, u - 1)
                        if u >= LAG:
                            take_high(s, u - LAG, 0)
                    exponents(s, UNITS - 1)
                    for u, c in SECOND:
                        take_high(s, u, c)
                        if c and u > UNITS - LEAD and more:
                            exponents(s + 1, u - UNITS + LEAD - 1)

                for u in range(LEAD - 1):
                    exponents(0, u)
                round_of(0, None, True)
                with act.Fori(0, STEPS - 2) as s:
                    round_of(s + 1, s, True)
                round_of(STEPS - 1, STEPS - 2, False)
                context(STEPS - 1)

            @block.vector
            def _(dve):
                nc.vector.tensor_scalar(masked[:], keep.eye[:], MASKED, None, ALU.mult).then_inc(masked_set, 1)
                dve.sem_inc(inv_ready, 1)
                dve.sem_inc(normed, 1)
                dve.sem_inc(back_ready, 1)
                dve.sem_inc(ctx_stored, 16)

                def normalise(s):
                    dve.wait_ge(inv_ready, s + 2)
                    dve.wait_ge(ctx_stored, s * 16 + 16)
                    dve.wait_ge(back_ready, s + 2)
                    nc.vector.tensor_tensor(ctx_out[:].rearrange("p t (h d) -> p (t h) d", d=DH), back_ps.rearrange("p t (h d) -> p (t h) d", d=DH),
                                            inv_total[:].unsqueeze(2).to_broadcast([P, UNITS, DH]), ALU.mult).then_inc(normed, 1)

                def invert(s):
                    dve.wait_ge(exp_done, s * UNITS + UNITS)
                    dve.wait_ge(normed, s + 1)
                    nc.vector.reciprocal(inv_total[:], total[:]).then_inc(inv_ready, 1)

                def maxima(s, u, since):
                    for c in range(NCH):
                        chunk_max(s, u, c)
                        if since is not None and c == 0:
                            unit_max(s, since)

                def round_of(s, before, more):
                    for u in range(LEAD, UNITS):
                        maxima(s, u, u - 1 if u > LEAD else None)
                        if u == UNITS - 1:
                            unit_max(s, u)
                        if u >= LAG:
                            take_low(s, u - LAG, 0)
                    for n, (u, c) in enumerate(SECOND):
                        take_low(s, u, c)
                        if n == 2 and before is not None:
                            normalise(before)
                        if n == 3:
                            invert(s)
                        if c and u >= UNITS - LEAD and more:
                            maxima(s + 1, u - UNITS + LEAD, None)
                            unit_max(s + 1, u - UNITS + LEAD)

                for u in range(LEAD):
                    maxima(0, u, None)
                    unit_max(0, u)
                round_of(0, None, True)
                with dve.Fori(0, STEPS - 2) as s:
                    round_of(s + 1, s, True)
                round_of(STEPS - 1, STEPS - 2, False)
                normalise(STEPS - 1)


def load_quarter(pool, keep, w1, w2, at, q, freed=None):
    if freed:
        freed(q, 0)
    for w in range(2):
        wide = w1[w][at:at + FF].rearrange("(c p n) x -> p c n x", p=P, n=FF // D)
        pool.dma_start(keep.w1[w][:, :, q * QF:(q + 1) * QF].bitcast(F32), wide[:, :, q, :]).then_inc(keep.w1_loaded[q], 16)
    if freed:
        freed(q, 1)
    for w in range(2):
        rows = w2[w][at + q * QF:at + (q + 1) * QF].rearrange("(f p) n -> p f n", p=P)
        pool.dma_start(keep.w2[w][:, q * QF // P:(q + 1) * QF // P, :].bitcast(F32), rows).then_inc(keep.w2_loaded[q], 16)


def mix(k, i, keep, scr):
    nc = k.nc
    with ExitStack() as ctx:
        sb = lambda *a: k.sb(ctx, *a)
        wo = [sb(f"wo{w}", [P, C, D], F32R) for w in range(2)]
        bo, g2, beta2 = sb("bo", [P, D]), sb("g2", [P, C]), sb("beta2", [P, C])
        ctx_in = sb("ctx_in", [P, GT, D])
        x2 = [sb(f"x2_in{t}", [P, D]) for t in range(GT)]
        ct = [sb(f"ctx_t{w}", [P, C, GTOK], F32R) for w in range(2)]
        x3, xn = sb("x3_mix", [P, GT, D]), sb("xn2", [P, GT, D])
        stats, mv = sb("stats2", [P, 6]), sb("mv2", [P, GT, 2])
        std, rstd = sb("std2", [P, GT]), sb("rstd2", [P, GT])
        ht = [sb(f"h_out{c}", [P, GTOK]) for c in range(C)]
        tp = [k.ps(ctx, f"mix_tp{n}", [P, 512]) for n in range(2)]
        hp = [k.ps(ctx, f"mix_hp{n}", [P, 512]) for n in range(2)]
        op = [k.ps(ctx, f"mix_op{n}", [P, D]) for n in range(GT)]
        consts_loaded, ctx_loaded = k.sem("mx_consts_loaded"), k.sem("mx_ctx_loaded")
        x2_loaded = [k.sem(f"mx_x2_loaded{t}") for t in range(GT)]
        ct_turned, ct_high, ct_low, wo_ready, x2_ready, x3_ready = (
            k.sem("mx_" + n) for n in ("ct_turned", "ct_high", "ct_low", "wo_ready", "x2_ready", "x3_ready"))
        own, var_ready, std_ready, xn_ready, xn_turned, h_ready, idle = (
            k.sem("mx_" + n) for n in ("dve_chain", "var_ready", "std_ready", "xn_ready", "xn_turned", "h_ready", "idle"))
        x3_stored, h_stored = k.sem("mx_x3_stored"), [k.sem(f"mx_h_stored{c}") for c in range(C)]
        row = lambda ap: ap.rearrange("(a n) -> a n", a=1)
        loads = [(wo[w][:].bitcast(F32), scr.wo[w].rearrange("(c p) n -> p c n", p=P)) for w in range(2)]
        loads += [(bo[:], row(i.bo).to_broadcast([P, D]))]
        loads += [(t[:], v.rearrange("(c p) -> p c", p=P)) for t, v in ((g2, i.g2), (beta2, i.beta2))]
        grouped = lambda ap: ap.rearrange("(g t p) d -> g p t d", t=GT, p=P)
        tile_of = lambda ap, g: grouped(ap)[ds(g, 1)].rearrange("a p t d -> p (a t) d")

        def load_x2(sp, g, t):
            sp.dma_start(x2[t][:], scr.x2[ds(g * GTOK + t * P, P), :]).then_inc(x2_loaded[t], 16)

        def store_x3(sp, g):
            sp.wait_ge(x3_ready, g * GT + GT)
            sp.dma_start(tile_of(scr.x3, g), x3[:]).then_inc(x3_stored, 16)

        def store_h(sp, g):
            for c in range(C):
                sp.wait_ge(h_ready, g * C + c + 3)
                sp.dma_start(scr.ht[c * P:(c + 1) * P, ds(g * GTOK, GTOK)], ht[c][:]).then_inc(h_stored[c], 16)

        with nc.Block() as block:
            @block.sync
            def _(sp):
                sp.dma_start(ctx_in[:], tile_of(scr.ctx, 0)).then_inc(ctx_loaded, 16)
                for t in range(GT):
                    load_x2(sp, 0, t)
                for dst, src in loads:
                    sp.dma_start(dst, src, allow_slow_non_contiguous=True).then_inc(consts_loaded, 16)

                def after(sp, g, more):
                    if more:
                        sp.wait_ge(ct_turned, g * C + C)
                        sp.dma_start(ctx_in[:], tile_of(scr.ctx, g + 1)).then_inc(ctx_loaded, 16)
                        for t in range(GT):
                            sp.wait_ge(x3_ready, g * GT + t + 1)
                            load_x2(sp, g + 1, t)
                    store_x3(sp, g)
                after(sp, 0, True)
                with sp.Fori(1, NG - 1) as g:
                    store_h(sp, g - 1)
                    after(sp, g, True)
                store_h(sp, NG - 2)
                after(sp, NG - 1, False)
                store_h(sp, NG - 1)
                sp.wait_ge(x3_stored, 16 * NG + 16)
                for c in range(C):
                    sp.wait_ge(h_stored[c], 16 * NG + 16)

            @block.gpsimd
            def _(pool):
                def residual(g):
                    for t in range(GT):
                        pool.wait_ge(x2_loaded[t], g * 16 + 16)
                        nc.gpsimd.tensor_tensor(x2[t][:], x2[t][:], bo[:], ALU.add).then_inc(x2_ready, 1)

                pool.wait_ge(consts_loaded, 16 * len(loads))
                for q in range(QUARTERS):
                    residual(q)
                    load_quarter(pool, keep, scr.w1, scr.w2, 0, q)
                with pool.Fori(QUARTERS, NG) as g:
                    residual(g)

            @block.tensor
            def _(pe):
                mm = nc.tensor.matmul

                def turn_ctx(g):
                    pe.wait_ge(ctx_loaded, g * 16 + 16)
                    for c in range(C):
                        pe.wait_ge(ct_low, g * C + c + 1)
                        for t in range(GT):
                            last = nc.tensor.transpose(tp[c % 2][:, t * P:(t + 1) * P], ctx_in[:, t, c * P:(c + 1) * P], keep.eye[:])
                        last.then_inc(ct_turned, 1)

                def turn_h(g):
                    pe.wait_ge(xn_ready, g * GT + GT + 1)
                    for c in range(C):
                        pe.wait_ge(h_ready, g * C + c + 1)
                        for t in range(GT):
                            last = nc.tensor.transpose(hp[c % 2][:, t * P:(t + 1) * P], xn[:, t, c * P:(c + 1) * P], keep.eye[:])
                        last.then_inc(xn_turned, 1)

                def product(g):
                    pe.wait_ge(ct_low, g * C + C + 2)
                    for t in range(GT):
                        if not isinstance(g, int) or g:
                            pe.wait_ge(x3_ready, (g - 1) * GT + t + 1)
                        tok = slice(t * P, (t + 1) * P)
                        n = 0
                        for c in range(C):
                            for a, w in ((0, 0), (1, 0), (0, 1)):
                                n += 1
                                last = mm(op[t][:], ct[a][:, c, tok], wo[w][:, c, :], start=(n == 1), stop=(n == 3 * C))
                        last.then_inc(wo_ready, 1)

                turn_ctx(0)
                pe.wait_ge(consts_loaded, 16 * len(loads))
                product(0)
                with pe.Fori(1, NG) as g:
                    turn_ctx(g)
                    turn_h(g - 1)
                    product(g)
                turn_h(NG - 1)

            @block.scalar
            def _(act):
                act.sem_inc(h_ready, 2)
                for c in range(C):
                    act.sem_inc(h_stored[c], 16)

                def high(g):
                    if not isinstance(g, int) or g:
                        act.wait_ge(wo_ready, g * GT)
                    for c in range(C):
                        act.wait_ge(ct_turned, g * C + c + 1)
                        nc.scalar.copy(ct[0][:, c, :], tp[c % 2][:]).then_inc(ct_high, 1)

                def affine(g):
                    for c in range(C):
                        act.wait_ge(xn_turned, g * C + c + 1)
                        act.wait_ge(h_stored[c], g * 16 + 16)
                        nc.scalar.activation(ht[c][:], hp[c % 2][:], ACT.Identity, scale=g2[:, c:c + 1], bias=beta2[:, c:c + 1]).then_inc(h_ready, 1)

                def deviations(g):
                    for t in range(GT):
                        act.wait_ge(var_ready, g * GT + t + 1)
                        nc.scalar.activation(std[:, t:t + 1], mv[:, t, 1:2], ACT.Sqrt, bias=keep.eps5[:]).then_inc(std_ready, 1)

                high(0)
                act.wait_ge(consts_loaded, 16 * len(loads))
                deviations(0)
                with act.Fori(1, NG) as g:
                    high(g)
                    affine(g - 1)
                    deviations(g)
                affine(NG - 1)

            @block.vector
            def _(dve):
                dve.sem_inc(ct_low, 2)
                dve.sem_inc(xn_ready, 1)
                dve.sem_inc(x3_stored, 16)

                def low(g):
                    for c in range(C):
                        dve.wait_ge(ct_high, g * C + c + 1)
                        nc.vector.tensor_tensor(ct[1][:, c, :], tp[c % 2][:], ct[0][:, c, :].bitcast(F32), ALU.subtract).then_inc(ct_low, 1)

                def normalise(g):
                    link = Link(dve, own, per=2 * GT, at=g)
                    dve.wait_ge(x3_stored, g * 16 + 16)
                    if not isinstance(g, int) or g:
                        dve.wait_ge(xn_turned, g * C)
                    for t in range(GT + 1):
                        if t < GT:
                            dve.wait_ge(wo_ready, g * GT + t + 1)
                            dve.wait_ge(x2_ready, g * GT + t + 1)
                            nc.vector.tensor_tensor(x3[:, t], op[t][:], x2[t][:], ALU.add).then_inc(x3_ready, 1)
                            dve.wait_ge(x3_ready, g * GT + t + 1)
                            link(nc.vector.bn_stats(stats[:], x3[:, t]))
                            dve.sem_inc(idle, 1)
                            nc.vector.bn_aggr(mv[:, t], stats[:]).then_inc(var_ready, 1)
                        if t:
                            dve.wait_ge(std_ready, g * GT + t)
                            link(nc.vector.reciprocal(rstd[:, t - 1:t], std[:, t - 1:t]))
                            nc.vector.tensor_scalar(xn[:, t - 1], x3[:, t - 1], mv[:, t - 1, 0:1], rstd[:, t - 1:t], ALU.subtract, ALU.mult).then_inc(xn_ready, 1)

                low(0)
                normalise(0)
                with dve.Fori(1, NG) as g:
                    low(g)
                    normalise(g)


def feed(k, i, keep, scr, out, experts):
    nc = k.nc
    tag = "ex_" if experts else "fd_"
    with ExitStack() as ctx:
        sb = lambda n, *a: k.sb(ctx, tag + n, *a)
        sem = lambda n: k.sem(tag + n)
        NV = B if experts else 1
        ht = [[sb(f"ht{n}{w}", [P, C, GTOK], F32R) for w in range(2)] for n in range(2)]
        b_in, b_out = sb("b_in", [P, NV, FC]), sb("b_out", [P, NV, D])
        gate_b = sb("gate_b", [P, FC])
        sig = [sb(f"sig{n}", [P, GTOK]) for n in range(2)]
        hid32 = sig if experts else [sb(f"hid32{n}", [P, GTOK]) for n in range(2)]
        hid = [[sb(f"hid{n}{w}", [P, GTOK], F32R) for w in range(2)] for n in range(2)]
        res, o_t = sb("res", [P, GT, D]), sb("o_t", [P, GT, D])
        if experts:
            xs = [sb(f"xs{n}", [P, D]) for n in range(2)]
            tp = [k.ps(ctx, f"{tag}tp{n}", [P, 512]) for n in range(2)]
            xs_loaded, xs_turned = [sem(f"xs_loaded{n}") for n in range(2)], sem("xs_turned")
            gamma, beta = sb("gamma", [P, NV, D]), sb("beta", [P, NV, D])
            chosen_t = sb("chosen", [1, B], I32)
            stats, mv = sb("stats", [P, 6]), sb("mv", [P, GT, 2])
            std, rstd, eps12 = sb("std", [P, GT]), sb("rstd", [P, GT]), sb("eps12", [P, 1])
        else:
            h32 = sb("h32", [P, C, GTOK])
        fp = [k.ps(ctx, f"{tag}fp{n}", [P, GTOK]) for n in range(2)]
        acc = [k.ps(ctx, f"{tag}acc{n}", [P, D]) for n in range(GT)]

        vec_loaded, e_loaded, h_loaded, x_high, x_low = (sem(n) for n in ("vec_loaded", "e_loaded", "h_loaded", "x_high", "x_low"))
        res_loaded, res_ready, hid_ready, gate_ready, fp_taken, hid_high, hid_low, second_done = (
            sem(n) for n in ("res_loaded", "res_ready", "hid_ready", "gate_ready", "fp_taken", "hid_high", "hid_low", "second_done"))
        acc_ready, acc_taken, out_ready, out_stored, own, pool_own, var_ready, std_ready, y_ready, idle, set_up = (
            sem(n) for n in ("acc_ready", "acc_taken", "out_ready", "out_stored", "dve_chain", "pool_chain", "var_ready", "std_ready", "y_ready", "idle", "set_up"))
        act_idle, idle_v, r_ready = sem("act_idle"), sem("dve_idle"), sem("r_ready")
        tile_of = lambda ap, g: ap.rearrange("(g t p) d -> g p t d", t=GT, p=P)[ds(g, 1)].rearrange("a p t d -> p (a t) d")
        row = lambda ap: ap.rearrange("(a n) -> a n", a=1)
        source, dest = (scr.x4, out.rearrange("b s d -> (b s) d")) if experts else (scr.x3, scr.x4)
        N_VEC = 4 * B if experts else 2
        NT = GT if experts else C
        TURN_AT = range(4, 4 + NT)

        def load_h(sp, g, n):
            if experts:
                for t in range(GT):
                    sp.wait_ge(xs_turned, g * GT + t + 1)
                    sp.dma_start(xs[t % 2][:], scr.x4[ds(g * GTOK + t * P, P), :]).then_inc(xs_loaded[t % 2], 16)
                return
            sp.wait_ge(x_low, g * C + 2)
            sp.dma_start(h32[:], scr.ht.rearrange("(c p) n -> p c n", p=P)[:, :, ds(g * GTOK, GTOK)]).then_inc(h_loaded, 16)

        def over_pairs(eng, body):
            with eng.Fori(0, NG // 2 - 1) as it:
                for n in range(2):
                    body(it * 2 + n, n, True)
            for n in range(2):
                body(NG - 2 + n, n, n == 0)

        with nc.Block() as block:
            @block.sync
            def _(sp):
                load_h(sp, 0, 0)
                sp.dma_start(res[:], tile_of(source, 0)).then_inc(res_loaded, 16)
                if experts:
                    sp.dma_start(chosen_t[:], row(i.expert)).then_inc(e_loaded, 16)
                    sp.wait_ge(e_loaded, 16)
                    for b in range(B):
                        e = sp.value_load(chosen_t[0:1, b:b + 1], min_val=0, max_val=E - 1)
                        sp.dma_start(b_in[:, b], i.bi[ds(e, 1)].rearrange("a (f p) -> p (a f)", p=P), allow_slow_non_contiguous=True).then_inc(vec_loaded, 16)
                        for t, v in ((b_out, i.be), (gamma, i.gamma), (beta, i.beta)):
                            sp.dma_start(t[:, b], v[ds(e, 1)].to_broadcast([P, D])).then_inc(vec_loaded, 16)
                else:
                    sp.dma_start(b_in[:, 0], i.b1.rearrange("(f p) -> p f", p=P), allow_slow_non_contiguous=True).then_inc(vec_loaded, 16)
                    sp.dma_start(b_out[:, 0], row(i.b2).to_broadcast([P, D])).then_inc(vec_loaded, 16)

                def body(g, n, more):
                    if more:
                        sp.wait_ge(hid_ready, g * FC + 1)
                        load_h(sp, g + 1, 1 - n)
                    sp.wait_ge(acc_taken, g * GT + 2 * GT)
                    if more:
                        sp.dma_start(res[:], tile_of(source, g + 1)).then_inc(res_loaded, 16)
                    sp.wait_ge(out_ready, g * GT + GT)
                    sp.dma_start(tile_of(dest, g), o_t[:]).then_inc(out_stored, 16)
                over_pairs(sp, body)
                sp.wait_ge(out_stored, 16 * NG + 16)

            @block.gpsimd
            def _(pool):
                pool.wait_ge(vec_loaded, 16 * N_VEC)

                def residual(g):
                    pool.wait_ge(res_loaded, g * 16 + 16)
                    pool.sem_inc(idle, 1)
                    bias = b_out[:, ds(g // GB, 1), :] if experts else b_out[:]
                    nc.gpsimd.tensor_tensor(res[:], res[:], bias.to_broadcast([P, GT, D]), ALU.add).then_inc(res_ready, 1)

                def finish(g):
                    for t in range(GT):
                        pool.wait_ge(y_ready, g * GT + t + 1)
                        pool.sem_inc(idle, 1)
                        nc.gpsimd.tensor_tensor(o_t[:, t:t + 1], o_t[:, t:t + 1], gamma[:, ds(g // GB, 1), :], ALU.mult).then_inc(pool_own, 1)
                        pool.wait_ge(pool_own, g * GT + t + 1)
                        pool.sem_inc(idle, 1)
                        nc.gpsimd.tensor_tensor(o_t[:, t:t + 1], o_t[:, t:t + 1], beta[:, ds(g // GB, 1), :], ALU.add).then_inc(out_ready, 1)

                def freed(done):
                    def wait(q, which):
                        if which == 0:
                            pool.wait_ge(hid_ready, (done - 1) * FC + (q + 1) * FC // QUARTERS)
                        else:
                            pool.wait_ge(second_done, (done - 1) * FC + (q + 1) * FC // QUARTERS + 2)
                    return wait
                residual(0)
                if experts:
                    with pool.Fori(0, GB - 1) as g:
                        finish(g)
                        residual(g + 1)
                    for q in range(QUARTERS):
                        load_quarter(pool, keep, scr.wi, scr.we, FF, q, freed(GB))
                    with pool.Fori(GB - 1, NG - 1) as g:
                        finish(g)
                        residual(g + 1)
                    finish(NG - 1)
                else:
                    with pool.Fori(1, NG) as g:
                        residual(g)
                    for q in range(QUARTERS):
                        load_quarter(pool, keep, scr.wi, scr.we, 0, q, freed(NG))

            @block.tensor
            def _(pe):
                mm = nc.tensor.matmul
                loaded = lambda g: (g // GB * 32 + 64) if experts else 32

                def turn(g, t):
                    pe.wait_ge(xs_loaded[t % 2], g * 32 + (t // 2) * 16 + 16)
                    pe.wait_ge(x_low, g * GT + t + 1)
                    for c in range(C):
                        last = nc.tensor.transpose(tp[t % 2][:, c * P:(c + 1) * P], xs[t % 2][:, c * P:(c + 1) * P], keep.eye[:])
                    last.then_inc(xs_turned, 1)

                def first(g, n, fc):
                    q = fc * P // QF
                    if fc == 0:
                        pe.wait_ge(x_low, g * NT + NT + 2)
                    if fc % (QF // P) == 0:
                        pe.wait_ge(keep.w1_loaded[q], loaded(g))
                    pe.wait_ge(fp_taken, g * FC + fc + 1)
                    m = 0
                    for c in range(C):
                        for a, w in ((0, 0), (1, 0), (0, 1)):
                            m += 1
                            last = mm(fp[fc % 2][:], keep.w1[w][:, c, fc * P:(fc + 1) * P], ht[n][a][:, c, :], start=(m == 1), stop=(m == 3 * C))
                    last.then_inc(hid_ready, 1)

                def second(g, fc):
                    if fc % (QF // P) == 0:
                        pe.wait_ge(keep.w2_loaded[fc * P // QF], loaded(g))
                    pe.wait_ge(hid_low, g * FC + fc + 3)
                    for t in range(GT):
                        if fc == 0:
                            pe.wait_ge(acc_taken, g * GT + t + 1)
                        tok = slice(t * P, (t + 1) * P)
                        for m, (a, w) in enumerate(((0, 0), (1, 0), (0, 1))):
                            last = mm(acc[t][:], hid[fc % 2][a][:, tok], keep.w2[w][:, fc, :],
                                      start=(fc == 0 and m == 0), stop=(fc == FC - 1 and m == 2))
                        if fc == FC - 1:
                            last.then_inc(acc_ready, 1)
                        elif t == GT - 1:
                            last.then_inc(second_done, 1)
                    if fc == FC - 1:
                        pe.wait_ge(acc_ready, g * GT + GT)
                        pe.sem_inc(second_done, 1)

                def body(g, n, more):
                    for fc in range(FC):
                        if fc < FC - 1:
                            first(g, n, fc + 1)
                        elif more:
                            first(g + 1, 1 - n, 0)
                        second(g, fc)
                        if experts and more and fc in TURN_AT:
                            turn(g + 1, fc - TURN_AT[0])
                if experts:
                    for t in range(GT):
                        turn(0, t)
                first(0, 0, 0)
                over_pairs(pe, body)

            @block.scalar
            def _(act):

                def high(g, n, t):
                    if not experts:
                        act.wait_ge(h_loaded, g * 16 + 16)
                        nc.scalar.copy(ht[n][0][:, t, :], h32[:, t, :]).then_inc(x_high, 1)
                        return
                    act.wait_ge(xs_turned, g * GT + t + 3)
                    nc.scalar.copy(ht[n][0][:, :, t * P:(t + 1) * P], tp[t % 2][:].rearrange("p (c n) -> p c n", c=C)).then_inc(x_high, 1)

                def activate(g, n, fc):
                    act.wait_ge(hid_ready, g * FC + fc + 1)
                    if experts:
                        act.wait_ge(hid_low, g * FC + fc + 1)
                        act.sem_inc(act_idle, 1)
                        nc.scalar.activation(sig[fc % 2][:], fp[fc % 2][:], ACT.Gelu,
                                             bias=b_in[:].rearrange("p v f -> p (v f)")[:, ds(g // GB * FC + fc, 1)]).then_inc(fp_taken, 1)
                    else:
                        act.wait_ge(fp_taken, g * FC + fc + 1)
                        nc.scalar.activation(sig[fc % 2][:], fp[fc % 2][:], ACT.Sigmoid, scale=1.702, bias=gate_b[:, fc:fc + 1]).then_inc(gate_ready, 1)

                def body(g, n, more):
                    for fc in range(FC):
                        if fc < FC - 1:
                            activate(g, n, fc + 1)
                        elif more:
                            activate(g + 1, 1 - n, 0)
                        if more and fc in TURN_AT:
                            high(g + 1, 1 - n, fc - TURN_AT[0])
                    if experts:
                        act.wait_ge(var_ready, g + 1)
                        nc.scalar.activation(std[:], mv[:, :, 1], ACT.Sqrt, bias=eps12[:]).then_inc(std_ready, 1)
                for t in range(NT):
                    high(0, 0, t)
                act.wait_ge(vec_loaded, 16 * N_VEC)
                if not experts:
                    act.wait_ge(set_up, 1)
                activate(0, 0, 0)
                over_pairs(act, body)

            @block.vector
            def _(dve):
                dve.sem_inc(fp_taken, 2)
                dve.sem_inc(hid_low, 2)
                dve.sem_inc(x_low, 2)
                dve.sem_inc(second_done, 2)
                dve.sem_inc(acc_taken, GT)
                dve.sem_inc(out_stored, 16)
                if experts:
                    dve.sem_inc(xs_turned, 2)
                    nc.vector.memset(eps12[:], 1e-12).then_inc(set_up, 1)

                def low(g, n, t):
                    dve.wait_ge(x_high, g * NT + t + 1)
                    if not experts:
                        nc.vector.tensor_tensor(ht[n][1][:, t, :], h32[:, t, :], ht[n][0][:, t, :].bitcast(F32), ALU.subtract).then_inc(x_low, 1)
                        return
                    tok = slice(t * P, (t + 1) * P)
                    nc.vector.tensor_tensor(ht[n][1][:, :, tok], tp[t % 2][:].rearrange("p (c n) -> p c n", c=C),
                                            ht[n][0][:, :, tok].bitcast(F32), ALU.subtract).then_inc(x_low, 1)

                def split(g, n, fc):
                    chunk = g * FC + fc
                    if experts:
                        dve.wait_ge(fp_taken, chunk + 3)
                    else:
                        dve.wait_ge(hid_low, chunk + 1)
                        dve.wait_ge(gate_ready, chunk + 1)
                        nc.vector.scalar_tensor_tensor(hid32[fc % 2][:], fp[fc % 2][:], b_in[:, 0, fc:fc + 1], sig[fc % 2][:], ALU.add, ALU.mult).then_inc(fp_taken, 1)
                        dve.wait_ge(fp_taken, chunk + 3)
                    dve.wait_ge(second_done, chunk + 1)
                    nc.vector.tensor_copy(hid[fc % 2][0][:], hid32[fc % 2][:]).then_inc(hid_high, 1)
                    dve.wait_ge(hid_high, chunk + 1)
                    nc.vector.tensor_tensor(hid[fc % 2][1][:], hid32[fc % 2][:], hid[fc % 2][0][:].bitcast(F32), ALU.subtract).then_inc(hid_low, 1)

                def epilogue(g):
                    dve.wait_ge(res_ready, g + 1)
                    dve.wait_ge(out_stored, g * 16 + 16)
                    for t in range(GT):
                        dve.wait_ge(acc_ready, g * GT + t + 1)
                        sum_ = nc.vector.tensor_tensor(o_t[:, t], acc[t][:], res[:, t], ALU.add)
                        sum_.then_inc(acc_taken, 1)
                        if not experts:
                            dve.wait_ge(acc_taken, g * GT + GT + t + 1)
                            dve.sem_inc(out_ready, 1)
                    if experts:
                        link = Link(dve, own, per=2 * GT, at=g)
                        for t in range(GT):
                            dve.wait_ge(acc_taken, g * GT + GT + t + 1)
                            link(nc.vector.bn_stats(stats[:], o_t[:, t]))
                            dve.sem_inc(idle_v, 1)
                            link(nc.vector.bn_aggr(mv[:, t], stats[:]))
                        dve.sem_inc(var_ready, 1)
                        dve.wait_ge(std_ready, g + 1)
                        nc.vector.reciprocal(rstd[:], std[:]).then_inc(r_ready, 1)
                        dve.wait_ge(r_ready, g + 1)
                        for t in range(GT):
                            nc.vector.tensor_scalar(o_t[:, t], o_t[:, t], mv[:, t, 0:1], rstd[:, t:t + 1], ALU.subtract, ALU.mult).then_inc(y_ready, 1)

                def body(g, n, more):
                    for fc in range(FC):
                        if fc < FC - 1:
                            split(g, n, fc + 1)
                        elif more:
                            split(g + 1, 1 - n, 0)
                        if more and fc in TURN_AT:
                            low(g + 1, 1 - n, fc - TURN_AT[0])
                    epilogue(g)
                for t in range(NT):
                    low(0, 0, t)
                if not experts:
                    dve.wait_ge(vec_loaded, 16 * N_VEC)
                    nc.vector.tensor_scalar(gate_b[:], b_in[:, 0], 1.702, None, ALU.mult).then_inc(set_up, 1)
                split(0, 0, 0)
                over_pairs(dve, body)


class Names:
    pass


def program(nc, i, out):
    with ExitStack() as outer:
        k = Core(nc)
        scr = Names()
        scr.x2 = k.dram("x2_dram", [TOK, D])
        scr.x2t = k.dram("x2t_dram", [2, D, TOK])
        scr.q = k.dram("q_dram", [2, D, TOK])
        scr.k = k.dram("k_dram", [2, D, TOK])
        scr.v = k.dram("v_dram", [TOK, D])
        scr.mask = k.dram("mask_dram", [TOK, S], BF16)
        scr.ctx = k.dram("ctx_dram", [TOK, D])
        scr.x3 = k.dram("x3_dram", [TOK, D])
        scr.x4 = k.dram("x4_dram", [TOK, D])
        scr.ht = k.dram("ht_dram", [D, TOK])
        scr.wo = k.dram("wo_parts", [2, D, D])
        scr.w1 = k.dram("w1_parts", [2, FF, D])
        scr.w2 = k.dram("w2_parts", [2, FF, D])
        scr.wi = k.dram("wi_parts", [2, B * FF, D])
        scr.we = k.dram("we_parts", [2, B * FF, D])
        keep = Names()
        keep.eye = k.sb(outer, "eye", [P, P])
        keep.eye_bf = k.sb(outer, "eye_bf", [P, P], BF16)
        keep.eps5 = k.sb(outer, "eps5", [P, 1])
        with ExitStack() as front:
            sb = lambda *a: k.sb(front, *a)
            keep.basis = sb("basis", [P, C, 2, R])
            keep.ada = sb("ada", [P, 2 * C, B])
            keep.ada_row = sb("ada_row", [P, B, 2, D])
            keep.g33 = sb("g33_rot", [R + 1, B, D])
            keep.rot = sb("rot", [P, B, P])
            keep.y33 = sb("y33", [R + 1, GTOK])
            keep.bq, keep.bk, keep.bv = sb("bq", [P, C]), sb("bk", [P, C]), sb("bv", [P, D])
            keep.w_hi = sb("w_hi", [P, 3, C, D], F32R)
            keep.w_lo = sb("w_lo", [P, 3, C, D], F32R)
            constants(k, i, keep, scr)
            k.pass_done()
            embed(k, i, keep, scr)
            k.pass_done()
            project(k, i, keep, scr)
            k.pass_done()
        attend(k, i, keep, scr)
        k.pass_done()
        with ExitStack() as back:
            keep.w1 = [k.sb(back, f"w1_{w}", [P, C, FF], F32R) for w in range(2)]
            keep.w2 = [k.sb(back, f"w2_{w}", [P, FC, D], F32R) for w in range(2)]
            keep.w1_loaded = [nc.alloc_semaphore(name=f"w1_loaded{q}") for q in range(QUARTERS)]
            keep.w2_loaded = [nc.alloc_semaphore(name=f"w2_loaded{q}") for q in range(QUARTERS)]
            mix(k, i, keep, scr)
            k.pass_done()
            feed(k, i, keep, scr, out, experts=False)
            k.pass_done()
            feed(k, i, keep, scr, out, experts=True)


INPUTS = {"x": "x", "score": "condB_safetyscore", "theta": "condB_theta", "phi": "condB_phi",
    "step": "itok_B_34_63", "bias": "fside_Bx16xSxS_0", "expert": "itok_B_0_7", "mask": "mask_Bx1xSxS_bk0",
    "U": "L0_cond_U", "V": "L0_cond_V", "safety_bias": "L0_cond_safety_bias", "gate_w1": "L0_cond_gate_w1",
    "gate_b1": "L0_cond_gate_b1", "gate_w2": "L0_cond_gate_w2", "gate_b2": "L0_cond_gate_b2",
    "resp_w": "L0_cond_resp_w", "resp_b": "L0_cond_resp_b", "W_ada": "L2_cond_W_ada", "b_ada": "L2_cond_b_ada",
    "Wq": "L2_cond_Wq", "bq": "L2_cond_bq", "Wk": "L2_cond_Wk", "bk": "L2_cond_bk", "Wv": "L2_cond_Wv",
    "bv": "L2_cond_bv", "Wo": "L2_cond_Wo", "bo": "L2_cond_bo", "W1": "L2_cond_W1", "b1": "L2_cond_b1",
    "W2": "L2_cond_W2", "b2": "L2_cond_b2", "g2": "L2_cond_g2", "beta2": "L2_cond_beta2", "Wi": "L3_cond_Wi",
    "bi": "L3_cond_bi", "We": "L3_cond_Wo", "be": "L3_cond_bo", "gamma": "L3_cond_gamma",
    "beta": "L3_cond_beta"}


def kernel(**inputs):
    import numpy as np
    import concourse.bacc as bacc
    from concourse.bass_utils import run_bass_kernel_spmd

    nc = bacc.Bacc("TRN2", target_bir_lowering=False, num_devices=1)
    arrays = {short: np.ascontiguousarray(inputs[name]) for short, name in INPUTS.items()}
    arrays["mask"] = arrays["mask"].view(np.int32)
    arrays["freq"] = np.exp(np.arange(D // 2, dtype=np.float32) * np.float32(-np.log(10000.0) / (D // 2 - 1)))
    i = Names()
    for short, a in arrays.items():
        i.__dict__[short] = nc.dram_tensor(f"in_{short}", a.shape, mybir.dt.from_np(a.dtype), kind="ExternalInput").ap()
    out = nc.dram_tensor("out", (B, S, D), F32, kind="ExternalOutput").ap()
    program(nc, i, out)
    r = run_bass_kernel_spmd(nc, [{f"in_{short}": a for short, a in arrays.items()}], core_ids=[0])
    return r.results[0]["out"]
```
